# Optimizing a Trainium2 kernel written in Bass

```python
import numpy as np
import jax
import jax.numpy as jnp

def _softmax(x, axis=-1):
    return jax.nn.softmax(x, axis=axis)

def _gelu(x):
    return jax.nn.gelu(x, approximate=True)

def _silu(x):
    return jax.nn.silu(x)

def _sigmoid(x):
    return jax.nn.sigmoid(x)

def _layernorm(x, axis=-1, eps=1e-05):
    m = jnp.mean(x, axis=axis, keepdims=True)
    v = jnp.var(x, axis=axis, keepdims=True)
    return (x - m) / jnp.sqrt(v + eps)

def _scatter_add(tgt, idx, src, axis=0):
    return tgt.at[idx].add(src)

def _segment_sum(src, seg, n):
    return jax.ops.segment_sum(src, seg, n)
kernel_name = 'mk_gnn_preln_d4_gnn_r32_46567b'

def setup_inputs(seed: int=0):
    np.random.seed(seed)
    _w = jnp.asarray

    def _rec_inputs():
        import jax
        import jax.numpy as jnp
        _gk = jax.random.key(seed)
        x = -0.0001079 + 1 * jax.random.normal(jax.random.fold_in(_gk, 1), (3125, 32), jnp.float32)
        src = jax.random.randint(jax.random.fold_in(_gk, 2), (50000,), 0, 3125, jnp.int32)
        dst = jnp.minimum((3125 * jax.random.uniform(jax.random.fold_in(_gk, 3), (50000,)) ** 2.0).astype(jnp.int32), 99999)
        _o = jnp.argsort(dst, stable=True)
        src = src[_o]
        dst = dst[_o]
        edge_attr_3 = jax.random.uniform(jax.random.fold_in(_gk, 12), (50000, 3), jnp.float32, 0.0, 0.999998)
        edge_weight = jax.random.uniform(jax.random.fold_in(_gk, 14), (50000,), jnp.float32, 0.0, 0.999999)
        node_vec = jax.random.uniform(jax.random.fold_in(_gk, 15), (3125,), jnp.float32, 0.0, 0.999994)
        return (x, src, dst, edge_attr_3, edge_weight, node_vec)
    x, src, dst, edge_attr_3, edge_weight, node_vec = _rec_inputs()

    def _L0_gnn_setup():
        import jax, jax.numpy as jnp
        import numpy as np
        NUM_NODES = 3125
        EMB_DIM = 32
        NUM_EDGES = 50000
        key = jax.random.key(seed)
        k1, k2 = jax.random.split(key)
        edge_index = jax.random.randint(k1, (2, NUM_EDGES), 0, NUM_NODES, dtype=jnp.int64)
        embedding_weight = jax.random.normal(k2, (NUM_NODES, EMB_DIM), dtype=jnp.float32)
        return {'edge_index': edge_index, 'embedding_weight': embedding_weight}
    _L0_gnn_all = _L0_gnn_setup()
    _L0_gnn_in = {k: v for k, v in _L0_gnn_all.items() if k in ()}
    del _L0_gnn_all

    def _L1_gnn_setup():
        import jax, jax.numpy as jnp
        import numpy as np
        N = 3125
        E = 50000
        D = 32
        ITERS = 4
        key = jax.random.key(seed)
        ks = jax.random.split(key, 9)
        return {'x': jax.random.normal(ks[0], (N, D), dtype=jnp.float32), 'labels': jax.random.uniform(ks[1], (N,), dtype=jnp.float32), 'edge_weight': jax.random.uniform(ks[2], (E,), dtype=jnp.float32), 'alpha1': jax.random.normal(ks[3], (1,), dtype=jnp.float32), 'alpha2': jax.random.normal(ks[4], (1,), dtype=jnp.float32), 'alpha3': jax.random.normal(ks[5], (1,), dtype=jnp.float32), 'alpha4': jax.random.normal(ks[6], (1,), dtype=jnp.float32), 'edge_src': jax.random.randint(ks[7], (E,), 0, N), 'edge_dst': jax.random.randint(ks[8], (E,), 0, N)}
    _L1_gnn_all = _L1_gnn_setup()
    _L1_gnn_in = {k: v for k, v in _L1_gnn_all.items() if k in ('alpha1', 'alpha2', 'alpha3', 'alpha4')}
    del _L1_gnn_all

    def _L2_gnn_setup():
        import jax, jax.numpy as jnp
        import numpy as np
        N = 3125
        E = 50000
        D = 32
        L = 3

        def _gcn_norm(edge_index, edge_weight, n):
            loop = jnp.arange(n)
            src = jnp.concatenate([edge_index[0], loop])
            dst = jnp.concatenate([edge_index[1], loop])
            w = jnp.concatenate([edge_weight, jnp.ones((n,), edge_weight.dtype)])
            deg = jax.ops.segment_sum(w, dst, num_segments=n)
            dinv = jnp.where(deg > 0, jax.lax.rsqrt(deg), jnp.zeros_like(deg))
            return (src, dst, dinv[src] * w * dinv[dst])
        key = jax.random.key(seed)
        ks = jax.random.split(key, 6)
        X = jax.random.normal(ks[0], (N, D), jnp.float32)
        edge_index = jax.random.randint(ks[1], (2, E), 0, N)
        edge_weight = jax.random.uniform(ks[2], (E,), jnp.float32)
        conv_w = jax.random.normal(ks[3], (L, 8, D, D), jnp.float32) * np.float32(1.0 / np.sqrt(D))
        conv_b = jnp.zeros((L, 8, D), jnp.float32)
        wc = jax.random.normal(ks[4], (L, 3, D), jnp.float32) * np.float32(0.1)
        bg = jnp.zeros((L, 4, D), jnp.float32)
        return dict(X=X, edge_index=edge_index, edge_weight=edge_weight, conv_w=conv_w, conv_b=conv_b, wc=wc, bg=bg)
    _L2_gnn_all = _L2_gnn_setup()
    _L2_gnn_in = {k: v for k, v in _L2_gnn_all.items() if k in ('conv_w', 'conv_b', 'wc', 'bg')}
    del _L2_gnn_all

    def _L3_gnn_setup():
        import jax, jax.numpy as jnp
        import numpy as np
        D = 3
        KS = 5
        K = KS ** D
        S = 2 ** D
        _COMBOS = np.array([[s >> d & 1 for d in range(D)] for s in range(S)], dtype=np.int32)
        _STRIDES = np.array([KS ** (D - 1 - d) for d in range(D)], dtype=np.int32)

        def spline_basis(pseudo):
            pos = pseudo * (KS - 1)
            i0 = jnp.clip(jnp.floor(pos), 0, KS - 2).astype(jnp.int32)
            frac = pos - i0
            combos = jnp.asarray(_COMBOS)
            basis = jnp.prod(jnp.where(combos[None] == 1, frac[:, None, :], 1.0 - frac[:, None, :]), axis=-1)
            idx = jnp.sum((i0[:, None, :] + combos[None]) * jnp.asarray(_STRIDES)[None, None, :], axis=-1)
            return (basis, idx)

        def spline_conv(x, row, col, basis, idx, W, b):
            N = x.shape[0]
            Fout = W.shape[2]
            z = jnp.einsum('ni,kio->nko', x, W).reshape(N * K, Fout)
            gathered = z[col[:, None] * K + idx]
            msg = jnp.einsum('es,eso->eo', basis, gathered)
            out = jax.ops.segment_sum(msg, row, num_segments=N)
            deg = jax.ops.segment_sum(jnp.ones_like(msg[:, 0]), row, num_segments=N)
            return out / jnp.maximum(deg, 1.0)[:, None] + b
        key = jax.random.key(seed)
        ks = jax.random.split(key, 13)
        N, E, Fin, Fout = (625, 10000, 32, 32)

        def u(k, shape, size):
            bound = 1.0 / np.sqrt(size)
            return jax.random.uniform(k, shape, jnp.float32, -bound, bound)
        return dict(x=jax.random.normal(ks[0], (N, Fin), jnp.float32), edge_index=jax.random.randint(ks[1], (2, E), 0, N, dtype=jnp.int32), pseudo=jax.random.uniform(ks[2], (E, D), jnp.float32), stn1_w=u(ks[3], (K, 1, 64), 1 * S), stn1_b=u(ks[4], (64,), 1 * S), stn2_w=u(ks[5], (K, 64, 64), 64 * S), stn2_b=u(ks[6], (64,), 64 * S), stn3_w=u(ks[7], (64, 64), 64), stn3_b=u(ks[8], (64,), 64), stn4_w=u(ks[9], (64, 3), 64), stn4_b=u(ks[10], (3,), 64), conv_w=u(ks[11], (K, Fin, Fout), Fin * S), conv_b=u(ks[12], (Fout,), Fin * S))
    _L3_gnn_all = _L3_gnn_setup()
    _L3_gnn_in = {k: v for k, v in _L3_gnn_all.items() if k in ('stn1_w', 'stn1_b', 'stn2_w', 'stn2_b', 'stn3_w', 'stn3_b', 'stn4_w', 'stn4_b', 'conv_w', 'conv_b')}
    del _L3_gnn_all
    return {'x': x, 'src': src, 'dst': dst, 'edge_attr_3': edge_attr_3, 'edge_weight': edge_weight, 'node_vec': node_vec, 'L1_gnn_alpha1': _L1_gnn_in['alpha1'], 'L1_gnn_alpha2': _L1_gnn_in['alpha2'], 'L1_gnn_alpha3': _L1_gnn_in['alpha3'], 'L1_gnn_alpha4': _L1_gnn_in['alpha4'], 'L2_gnn_conv_w': _L2_gnn_in['conv_w'], 'L2_gnn_conv_b': _L2_gnn_in['conv_b'], 'L2_gnn_wc': _L2_gnn_in['wc'], 'L2_gnn_bg': _L2_gnn_in['bg'], 'L3_gnn_stn1_w': _L3_gnn_in['stn1_w'], 'L3_gnn_stn1_b': _L3_gnn_in['stn1_b'], 'L3_gnn_stn2_w': _L3_gnn_in['stn2_w'], 'L3_gnn_stn2_b': _L3_gnn_in['stn2_b'], 'L3_gnn_stn3_w': _L3_gnn_in['stn3_w'], 'L3_gnn_stn3_b': _L3_gnn_in['stn3_b'], 'L3_gnn_stn4_w': _L3_gnn_in['stn4_w'], 'L3_gnn_stn4_b': _L3_gnn_in['stn4_b'], 'L3_gnn_conv_w': _L3_gnn_in['conv_w'], 'L3_gnn_conv_b': _L3_gnn_in['conv_b']}

def reference(x, src, dst, edge_attr_3, edge_weight, node_vec, L1_gnn_alpha1, L1_gnn_alpha2, L1_gnn_alpha3, L1_gnn_alpha4, L2_gnn_conv_w, L2_gnn_conv_b, L2_gnn_wc, L2_gnn_bg, L3_gnn_stn1_w, L3_gnn_stn1_b, L3_gnn_stn2_w, L3_gnn_stn2_b, L3_gnn_stn3_w, L3_gnn_stn3_b, L3_gnn_stn4_w, L3_gnn_stn4_b, L3_gnn_conv_w, L3_gnn_conv_b):
    import jax
    import jax.numpy as jnp

    def _L0_gnn_ref(edge_index, embedding_weight):
        import jax, jax.numpy as jnp
        import numpy as np
        NUM_NODES = 3125
        EMB_DIM = 32
        NUM_EDGES = 50000
        row, col = (edge_index[0], edge_index[1])
        n = embedding_weight.shape[0]
        ones = jnp.ones(row.shape[0], dtype=embedding_weight.dtype)
        deg = jax.ops.segment_sum(ones, col, num_segments=n)
        deg_inv_sqrt = jnp.where(deg > 0, jax.lax.rsqrt(jnp.maximum(deg, 1.0)), 0.0)
        norm = deg_inv_sqrt[row] * deg_inv_sqrt[col]
        msgs = embedding_weight[row] * norm[:, None]
        out = jax.ops.segment_sum(msgs, col, num_segments=n)
        return out

    def _L1_gnn_ref(x, labels, edge_weight, alpha1, alpha2, alpha3, alpha4, edge_src, edge_dst):
        import jax, jax.numpy as jnp
        import numpy as np
        N = 3125
        E = 50000
        D = 32
        ITERS = 4
        num_nodes = x.shape[0]
        edge_sum = jax.ops.segment_sum(jax.nn.relu(alpha3 * edge_weight), edge_dst, num_segments=num_nodes)
        bias = alpha2 * edge_sum[:, None] + alpha4 * labels[:, None]
        for _ in range(ITERS):
            nbr = jax.ops.segment_sum(x[edge_src], edge_dst, num_segments=num_nodes)
            x = jax.nn.relu(alpha1 * nbr + bias)
        return x

    def _L2_gnn_ref(X, edge_index, edge_weight, conv_w, conv_b, wc, bg):
        import jax, jax.numpy as jnp
        import numpy as np
        N = 3125
        E = 50000
        D = 32
        L = 3

        def _gcn_norm(edge_index, edge_weight, n):
            loop = jnp.arange(n)
            src = jnp.concatenate([edge_index[0], loop])
            dst = jnp.concatenate([edge_index[1], loop])
            w = jnp.concatenate([edge_weight, jnp.ones((n,), edge_weight.dtype)])
            deg = jax.ops.segment_sum(w, dst, num_segments=n)
            dinv = jnp.where(deg > 0, jax.lax.rsqrt(deg), jnp.zeros_like(deg))
            return (src, dst, dinv[src] * w * dinv[dst])
        n = X.shape[0]
        src, dst, nw = _gcn_norm(edge_index, edge_weight, n)

        def gcn(x, W, b):
            xw = x @ W
            agg = jax.ops.segment_sum(nw[:, None] * xw[src], dst, num_segments=n)
            return agg + b
        out = X
        for l in range(conv_w.shape[0]):
            x = out
            H = jnp.zeros((n, conv_w.shape[-1]), x.dtype)
            C = jnp.zeros_like(H)
            Wl, bl = (conv_w[l], conv_b[l])
            I = jax.nn.sigmoid(gcn(x, Wl[0], bl[0]) + gcn(H, Wl[1], bl[1]) + wc[l, 0] * C + bg[l, 0])
            F = jax.nn.sigmoid(gcn(x, Wl[2], bl[2]) + gcn(H, Wl[3], bl[3]) + wc[l, 1] * C + bg[l, 1])
            T = jnp.tanh(gcn(x, Wl[4], bl[4]) + gcn(H, Wl[5], bl[5]) + bg[l, 2])
            C = F * C + I * T
            O = jax.nn.sigmoid(gcn(x, Wl[6], bl[6]) + gcn(H, Wl[7], bl[7]) + wc[l, 2] * C + bg[l, 3])
            out = O * jnp.tanh(C)
        return out

    def _L3_gnn_ref(x, edge_index, pseudo, stn1_w, stn1_b, stn2_w, stn2_b, stn3_w, stn3_b, stn4_w, stn4_b, conv_w, conv_b):
        import jax, jax.numpy as jnp
        import numpy as np
        D = 3
        KS = 5
        K = KS ** D
        S = 2 ** D
        _COMBOS = np.array([[s >> d & 1 for d in range(D)] for s in range(S)], dtype=np.int32)
        _STRIDES = np.array([KS ** (D - 1 - d) for d in range(D)], dtype=np.int32)

        def spline_basis(pseudo):
            pos = pseudo * (KS - 1)
            i0 = jnp.clip(jnp.floor(pos), 0, KS - 2).astype(jnp.int32)
            frac = pos - i0
            combos = jnp.asarray(_COMBOS)
            basis = jnp.prod(jnp.where(combos[None] == 1, frac[:, None, :], 1.0 - frac[:, None, :]), axis=-1)
            idx = jnp.sum((i0[:, None, :] + combos[None]) * jnp.asarray(_STRIDES)[None, None, :], axis=-1)
            return (basis, idx)

        def spline_conv(x, row, col, basis, idx, W, b):
            N = x.shape[0]
            Fout = W.shape[2]
            z = jnp.einsum('ni,kio->nko', x, W).reshape(N * K, Fout)
            gathered = z[col[:, None] * K + idx]
            msg = jnp.einsum('es,eso->eo', basis, gathered)
            out = jax.ops.segment_sum(msg, row, num_segments=N)
            deg = jax.ops.segment_sum(jnp.ones_like(msg[:, 0]), row, num_segments=N)
            return out / jnp.maximum(deg, 1.0)[:, None] + b
        N = x.shape[0]
        row, col = (edge_index[0], edge_index[1])
        basis, idx = spline_basis(pseudo)
        h = jnp.ones((N, 1), x.dtype)
        h = jax.nn.elu(spline_conv(h, row, col, basis, idx, stn1_w, stn1_b))
        h = jax.nn.elu(spline_conv(h, row, col, basis, idx, stn2_w, stn2_b))
        h = jax.nn.elu(h @ stn3_w + stn3_b)
        t = h @ stn4_w + stn4_b
        new_pseudo = jnp.clip(pseudo + t[col] - t[row], 0.0, 1.0)
        basis2, idx2 = spline_basis(new_pseudo)
        return spline_conv(x, row, col, basis2, idx2, conv_w, conv_b)
    edge_index = jnp.stack([src, dst])
    h = jnp.maximum(_layernorm(x, axis=-1), 0.0)
    x = x + _L0_gnn_ref(edge_index, h)
    h = jnp.maximum(_layernorm(x, axis=-1), 0.0)
    x = x + _L1_gnn_ref(h, node_vec, edge_weight, L1_gnn_alpha1, L1_gnn_alpha2, L1_gnn_alpha3, L1_gnn_alpha4, src, dst)
    h = jnp.maximum(_layernorm(x, axis=-1), 0.0)
    x = x + _L2_gnn_ref(h, edge_index, edge_weight, L2_gnn_conv_w, L2_gnn_conv_b, L2_gnn_wc, L2_gnn_bg)
    h = jnp.maximum(_layernorm(x, axis=-1), 0.0)
    x = x + _L3_gnn_ref(h, edge_index, edge_attr_3, L3_gnn_stn1_w, L3_gnn_stn1_b, L3_gnn_stn2_w, L3_gnn_stn2_b, L3_gnn_stn3_w, L3_gnn_stn3_b, L3_gnn_stn4_w, L3_gnn_stn4_b, L3_gnn_conv_w, L3_gnn_conv_b)
    return x

_drawn_inputs = setup_inputs


def setup_inputs(seed=0):
    import zlib

    import numpy as np

    out = dict(_drawn_inputs(seed))
    spreads = {'L2_gnn_conv_b': (0.0, 0.1), 'L2_gnn_bg': (0.0, 0.451)}
    factors = {'edge_attr_3': 3.165,
     'edge_weight': 4.191,
     'node_vec': 4.482,
     'L2_gnn_conv_w': 5.451,
     'L2_gnn_wc': 8.0,
     'L3_gnn_stn1_w': 8.0,
     'L3_gnn_stn1_b': 34.751,
     'L3_gnn_stn2_w': 8.0,
     'L3_gnn_stn2_b': 64.0,
     'L3_gnn_stn3_w': 8.0,
     'L3_gnn_stn3_b': 64.0,
     'L3_gnn_stn4_w': 8.0,
     'L3_gnn_stn4_b': 8.0,
     'L3_gnn_conv_w': 2.947}
    for name, (base, spread) in spreads.items():
        noise = np.random.default_rng([zlib.crc32(name.encode()), seed]).standard_normal(out[name].shape)
        drawn = base * np.exp(spread * noise) if base else spread * noise
        out[name] = jnp.asarray(drawn.astype(out[name].dtype))
    for name, factor in factors.items():
        out[name] = (out[name] * factor).astype(out[name].dtype)
    return out
```

```python
from contextlib import ExitStack

import numpy as np

import concourse.bass as bass
from concourse import mybir

ALU = mybir.AluOpType
ACT = mybir.ActivationFunctionType
AX = mybir.AxisListType
F32 = mybir.dt.float32
F16 = mybir.dt.float16
BF16 = mybir.dt.bfloat16
I32 = mybir.dt.int32

P = 128
D = 32
SPLITS = 3
EPS = 1e-5
ITERS = 4
KS = 5
CELLS = KS - 1
ROW = 4 * D
NODE_ROWS = CELLS * CELLS * KS


def gnn_kernel(nc, x, src, dst, edge_attr, edge_weight, node_vec, alpha1, alpha2, alpha3, alpha4,
               conv_w, conv_b, wc, bg, stn1_w, stn1_b, stn2_w, stn2_b, stn3_w, stn3_b, stn4_w,
               stn4_b, sconv_w, sconv_b, out):
    N = x.shape[0]
    E = src.shape[0]
    LAYERS = conv_w.shape[0]
    H = stn2_w.shape[1]
    NP = 125
    NJ = N // NP
    assert NP * NJ == N and H == 2 * D
    U = 8
    B = U // 2
    TURNS = -(-E // (P * U))
    T = TURNS * U
    TAIL = E - (P - 1) * T
    MID = N // 2
    BANK = 512
    CHUNKS = [(c, min(BANK, N - c)) for c in range(0, N, BANK)]
    M = SPLITS * D + 1
    NOH = 4
    HALF = 2 * CELLS * KS * ROW

    L0, L1, L2 = 0, 1, 1 + ITERS
    C1 = L2 + LAYERS
    C2, C3 = C1 + 2, C1 + 4
    PASSES = C3 + 1

    ctx = ExitStack()
    with ctx:
        def sb(name, shape, dt=F32):
            return ctx.enter_context(nc.sbuf_tensor(name, shape, dt))

        def sem(name):
            return ctx.enter_context(nc.semaphore(name))

        tab_parts = nc.dram_tensor("tab_parts", (N, SPLITS * D), BF16).ap()
        tab_feat = nc.dram_tensor("tab_feat", (N, D), F32).ap()
        tab_t = nc.dram_tensor("tab_t", (N, 4), F32).ap()
        tab_w1 = [nc.dram_tensor(f"tab_w1_{h}", (NODE_ROWS, ROW), F32).ap() for h in range(2)]
        tab_z = [nc.dram_tensor(f"tab_z_{h}", (N * NODE_ROWS, ROW), F32).ap() for h in range(3)]

        PS = ctx.enter_context(nc.psum_tensor("PS", [P, 8 * BANK], F32))

        src_i, dst_i = sb("src_i", [P, T], I32), sb("dst_i", [P, T], I32)
        src_c, dst_c = sb("src_c", [P, T]), sb("dst_c", [P, T])
        weight = sb("weight", [P, T])
        attr = sb("attr", [P, T, 3])
        val = sb("val", [P, T, 3])
        dst_q, dst_r = sb("dst_q", [P, T]), sb("dst_r", [P, T])
        basis = sb("basis", [P, T, 8])
        row1, row2 = sb("row1", [P, 2, T], I32), sb("row2", [P, 2, T], I32)
        iota16 = sb("iota16", [P, N + 1], F16)
        iota_q = sb("iota_q", [P, NP])
        ident = sb("ident", [P, P])
        fold = sb("fold", [M, D + 1])
        zeros_l = sb("zeros_l", [P, P], BF16)
        zeros_f = sb("zeros_f", [P, P])
        alphas = sb("alphas", [P, 4])
        arena = sb("arena", [P, 2 * HALF])
        OHW = (N + 2) // 2
        oh = arena[:, 0:NOH * OHW].bitcast(BF16).rearrange("p (s n) -> p s n", s=NOH)
        RAW0 = NOH * OHW
        raw = arena[:, RAW0:RAW0 + U * 2 * ROW].rearrange("p (u r) -> p u r", u=U)
        zs = arena[:, :].rearrange("p (h c) -> p h c", h=2)
        oneq = arena[:, 0:2 * B * NP].rearrange("p (b u q) -> p b u q", b=2, u=B)
        oner = arena[:, 1000:1000 + 2 * B * NJ].rearrange("p (b u r) -> p b u r", b=2, u=B)
        qval = arena[:, 1200:1200 + 2 * B * NJ * 3].rearrange("p (b u r v) -> p b u r v", b=2, u=B, v=3)
        parts = sb("parts", [P, U, M + 1], BF16)
        slots = sb("slots", [P, 2, 2, B], I32)
        msg = sb("msg", [P, 2, B, D])
        res = sb("res", [P, 2, B, D])
        tdiff = sb("tdiff", [P, T, 3])
        accS = sb("accS", [M, N])
        xs, hs, cur = (sb(n, [NP, NJ, D]) for n in ("xs", "hs", "cur"))
        agg = sb("agg", [NP, NJ, D + 1])
        tb = sb("tb", [NP, NJ, SPLITS * D], BF16)
        h64 = sb("h64", [NP, NJ, H])
        hT = sb("hT", [H, NJ * NP])
        hcur = sb("hcur", [H, NP])
        scal = sb("scal", [NP, NJ, 3])
        nvec = sb("nvec", [NP, NJ])
        st = sb("st", [NP, 12, NJ])
        t4 = sb("t4", [NP, NJ, 4])
        wbuf = sb("wbuf", [H, KS ** 3, H])
        gate_w = sb("gate_w", [D, LAYERS, 3, D])
        gate_b = sb("gate_b", [NP, LAYERS, 3, D])
        cb = sb("cb", [NP, LAYERS, 8, D])
        gbg = sb("gbg", [NP, LAYERS, 4, D])
        gwc = sb("gwc", [NP, LAYERS, 3, D])
        w3, w4 = sb("w3", [H, H]), sb("w4", [H, 3])
        b1, b2, b3 = sb("b1", [NP, H]), sb("b2", [NP, H]), sb("b3", [NP, H])
        b4, bc = sb("b4", [NP, 3]), sb("bc", [NP, D])

        def tmp(width, at):
            return arena[0:NP, at:at + NJ * width].rearrange("p (j d) -> p j d", j=NJ)

        tmpA, tmpB = tmp(H, 0), tmp(H, NJ * H)
        gates = tmp(3 * D, 2 * NJ * H)
        g3 = gates.rearrange("p j (g d) -> p j g d", g=3)

        prep_mem = sem("prep_mem")
        loaded = sem("loaded")
        loaded_w = sem("loaded_w")
        loaded_z = sem("loaded_z")
        w1_done = sem("w1_done")
        dve_chain = sem("dve_chain")
        qval_ready = sem("qval_ready")
        qval_free = sem("qval_free")
        scal_ready = sem("scal_ready")
        var_ready, std_ready = sem("var_ready"), sem("std_ready")
        table_built, table_stored = sem("table_built"), sem("table_stored")
        rows_ready = sem("rows_ready")
        edges_ready = sem("edges_ready")
        gathered = [sem(f"gathered{b}") for b in range(2)]
        raw_free = sem("raw_free")
        dve_loop = sem("dve_loop")
        parts_ready = sem("parts_ready")
        onehot_ready = sem("onehot_ready")
        tile_done = sem("tile_done")
        sum_done = sem("sum_done")
        sum_copied = sem("sum_copied")
        fold_done = sem("fold_done")
        agg_copied = sem("agg_copied")
        tr_ready, tr_done = sem("tr_ready"), sem("tr_done")
        mm_ready, mm_done = sem("mm_ready"), sem("mm_done")
        ax_ready, ax_done = sem("ax_ready"), sem("ax_done")
        z_in = sem("z_in")
        z_mm = sem("z_mm")
        z_dve, z_act = sem("z_dve"), sem("z_act")
        z_stored = [sem(f"z_stored{h}") for h in range(2)]
        t_stored = sem("t_stored")
        out_ready, out_stored = sem("out_ready"), sem("out_stored")
        gate_pass = {e: sem(f"gate_{e}") for e in ("pool", "act", "dve", "pe", "sp")}

        def gate(eng, name, s, value):
            eng.wait_ge(s, value)
            eng.sem_inc(gate_pass[name], 1)

        def node_rows(ap):
            return ap.rearrange("(p j) d -> p j d", p=NP)

        kinds = {}
        for k in range(PASSES):
            if k < L2:
                kinds[k] = ("parts", [dst_i], dst_c, tab_parts)
            elif k < C1:
                kinds[k] = ("weighted", [dst_i], dst_c, tab_feat)
            elif k < C2:
                kinds[k] = ("spline", [row1[:, 0, :], row1[:, 1, :]], src_c, tab_w1[k - C1])
            else:
                kinds[k] = ("spline", [row2[:, 0, :], row2[:, 1, :]], src_c, tab_z[k - C2])
        for k in range(C1):
            kinds[k] = (kinds[k][0], [src_i], dst_c, kinds[k][3])

        STAGES = [("pass", k) for k in range(C2)]
        STAGES += [("build", 0), ("build", 1), ("pass", C2), ("pass", C2 + 1), ("tgather", 0),
                   ("build", 2), ("pass", C3)]
        GATHERS = [s for s in STAGES if s[0] in ("pass", "tgather")]
        order = {s: n for n, s in enumerate(GATHERS)}
        raws = [s for s in GATHERS if s[0] == "tgather" or kinds[s[1]][0] != "parts"]
        raw_order = {s: n for n, s in enumerate(raws)}
        per_batch = {s: 16 * B * (1 if s[0] == "pass" and s[1] < C1 else 2) for s in GATHERS}
        landed0, n = {}, 0
        for s in GATHERS:
            landed0[s] = n
            n += TURNS * per_batch[s]

        def corner(h, d1, d2):
            to = zs[0:NP, h, :].rearrange("p (a b q f) -> p a b q f", a=2, b=CELLS * KS, q=4)[:, :, :, 2 * d1 + d2, :]
            planes = PS[0:NP, 0:KS ** 3 * D].rearrange("p (a b f) -> p a b f", a=KS, b=KS * KS)
            c1 = 2 * h + d1
            return to, planes[:, c1:c1 + 2, d2 * KS:d2 * KS + CELLS * KS, :]

        block = ctx.enter_context(nc.Block())

        @block.sync
        def _(sp):
            for h in range(2):
                sp.sem_inc(z_stored[h], 32)
            sp.wait_ge(prep_mem, 1)
            FULL = (P - 1) * T
            for a, d in ((src, src_i), (dst, dst_i), (edge_weight, weight)):
                sp.dma_start(d[0:P - 1, :],
                             a[0:FULL].rearrange("(p t) -> p t", p=P - 1)).then_inc(loaded, 16)
                sp.dma_start(d[P - 1:P, 0:TAIL],
                             a[FULL:E].rearrange("(p t) -> p t", p=1)).then_inc(loaded, 16)
            sp.dma_start(attr[0:P - 1, :, :],
                         edge_attr[0:FULL, :].rearrange("(p t) c -> p t c", p=P - 1)).then_inc(loaded, 16)
            sp.dma_start(attr[P - 1:P, 0:TAIL, :],
                         edge_attr[FULL:E, :].rearrange("(p t) c -> p t c", p=1)).then_inc(loaded, 16)
            sp.dma_start(xs[:], node_rows(x)).then_inc(loaded, 16)
            sp.dma_start(nvec[:], node_vec.rearrange("(p j) -> p j", p=NP)).then_inc(loaded, 16)
            for i, a in enumerate((alpha1, alpha2, alpha3, alpha4)):
                sp.dma_start(alphas[:, i:i + 1], a.partition_broadcast(P)).then_inc(loaded, 16)
            for l in range(LAYERS):
                for g, m in enumerate((0, 4, 6)):
                    sp.dma_start(gate_w[:, l, g, :], conv_w[l, m]).then_inc(loaded_w, 16)
            sp.dma_start(cb[:], conv_b.partition_broadcast(NP)).then_inc(loaded_w, 16)
            sp.dma_start(gbg[:], bg.partition_broadcast(NP)).then_inc(loaded_w, 16)
            sp.dma_start(gwc[:], wc.partition_broadcast(NP)).then_inc(loaded_w, 16)
            for d, a in ((b1, stn1_b), (b2, stn2_b), (b3, stn3_b), (b4, stn4_b), (bc, sconv_b)):
                sp.dma_start(d[:], a.partition_broadcast(NP)).then_inc(loaded_w, 16)
            sp.dma_start(w3[:], stn3_w).then_inc(loaded_w, 16)
            sp.dma_start(w4[:], stn4_w).then_inc(loaded_w, 16)
            sp.dma_start(wbuf[:], stn2_w.rearrange("k i o -> i k o")).then_inc(loaded_z, 16)
            w1 = stn1_w.rearrange("(a b c) one f -> a b c (one f)", a=KS, b=KS)
            for h in range(2):
                t5 = tab_w1[h].rearrange("(a b c) (q f) -> a b c q f", a=CELLS, b=CELLS, q=4)
                for q in range(4):
                    d1, d2 = q // 2, q % 2
                    for a in range(CELLS):
                        sp.dma_start(t5[a, :, :, q, :],
                                     w1[a + d1, d2:d2 + CELLS, :, h * D:(h + 1) * D]).then_inc(w1_done, 16)
            for k in range(C1):
                sp.wait_ge(table_built, k + 1)
                if k < L2:
                    sp.dma_start(node_rows(tab_parts), tb[:]).then_inc(table_stored, 16)
                else:
                    sp.dma_start(node_rows(tab_feat), cur[:]).then_inc(table_stored, 16)

            def store_table(n):
                zt = tab_z[n].rearrange("(p j h r) f -> j h p (r f)", p=NP, j=NJ, h=2)
                with sp.Fori(0, NJ) as j:
                    for h in range(2):
                        gate(sp, "sp", (z_dve, z_act)[h], NJ * n + j + 2)
                        for p0, p1 in ((0, 112), (112, NP)):
                            sp.dma_start(zt[bass.ds(j, 1), h, p0:p1].squeeze(0),
                                         zs[p0:p1, h, :]).then_inc(z_stored[h], 16)

            store_table(0)
            store_table(1)
            sp.wait_ge(z_mm, 2 * 2 * NJ + 1)
            sp.dma_start(wbuf[0:D].rearrange("i k o -> i (k o)")[:, 0:KS ** 3 * D]
                         .rearrange("i (k o) -> i k o", o=D),
                         sconv_w.rearrange("k i o -> i k o")).then_inc(loaded_z, 16)
            sp.wait_ge(table_built, C1 + 1)
            sp.dma_start(node_rows(tab_t), t4[:]).then_inc(t_stored, 16)
            store_table(2)
            sp.wait_ge(out_ready, 1)
            sp.dma_start(node_rows(out), xs[:]).then_inc(out_stored, 16)
            sp.wait_ge(out_stored, 16)

        @block.gpsimd
        def _(pool):
            own = 1
            for d in (src_i, dst_i):
                nc.gpsimd.memset(d[:, TAIL:T], -1)
            nc.gpsimd.memset(weight[:, TAIL:T], 0.0)
            nc.gpsimd.memset(attr[:, TAIL:T, :], 0.0)
            pool.drain().then_inc(prep_mem, 1)
            nc.gpsimd.memset(parts[:], 1.0)
            nc.gpsimd.memset(zeros_l[:], 0.0)
            nc.gpsimd.memset(zeros_f[:], 0.0)
            nc.gpsimd.memset(ident[:], 0.0)
            nc.gpsimd.memset(fold[:], 0.0)
            nc.gpsimd.iota(iota16[:], pattern=[[1, N + 1]], base=-MID, channel_multiplier=0,
                           allow_small_or_imprecise_dtypes=True)
            nc.gpsimd.iota(iota_q[:], pattern=[[1, NP]], base=0, channel_multiplier=0,
                           allow_small_or_imprecise_dtypes=True)
            pool.drain().then_inc(prep_mem, 1)
            pool.wait_ge(prep_mem, 2)
            nc.gpsimd.affine_select(out=ident[:], in_=ident[:], compare_op=ALU.not_equal, fill=1.0,
                                    base=0, pattern=[[-1, P]], channel_multiplier=1).then_inc(prep_mem, 1)

            def gathers(stage):
                if stage[0] == "tgather":
                    tables, outs = [tab_t, tab_t], lambda b, u, g: raw[:, b * B + u, 4 * g:4 * g + 4]
                    pool.wait_ge(t_stored, 16)
                elif kinds[stage[1]][0] == "parts":
                    tables, outs = [tab_parts], lambda b, u, g: parts[:, b * B + u, 0:SPLITS * D]
                    pool.wait_ge(table_stored, 16 * (stage[1] + 1))
                elif kinds[stage[1]][0] == "weighted":
                    tables, outs = [tab_feat], lambda b, u, g: raw[:, b * B + u, 0:D]
                    pool.wait_ge(table_stored, 16 * (stage[1] + 1))
                else:
                    tables, outs = [kinds[stage[1]][3]] * 2, lambda b, u, g: raw[:, b * B + u, g * ROW:(g + 1) * ROW]
                    if stage[1] < C2:
                        pool.wait_ge(w1_done, 16 * 8 * CELLS)
                    else:
                        for h in range(2):
                            pool.wait_ge(z_stored[h], 32 + 32 * NJ * (2 if stage[1] < C3 else 3))
                n0 = 2 * TURNS * order[stage]
                with pool.Fori(0, TURNS) as i:
                    for b in range(2):
                        gate(pool, "pool", rows_ready, n0 + 2 * i + b + 1)
                        for u in range(B):
                            for g, table in enumerate(tables):
                                nc.gpsimd.indirect_dma_start(
                                    out=outs(b, u, g), out_offset=None, in_=table,
                                    in_offset=bass.IndirectOffsetOnAxis(ap=slots[:, b, g, u:u + 1], axis=0),
                                ).then_inc(gathered[b], 16)

            for stage in GATHERS:
                gathers(stage)

        @block.tensor
        def _(pe):
            pe.sem_inc(tile_done, U)
            pe.sem_inc(qval_free, 2)
            pe.sem_inc(z_mm, 1)
            pe.wait_ge(prep_mem, 3)

            S0 = 7 * BANK
            psq = PS[0:NP, S0:S0 + NJ * 3]
            pe.matmul(psq, zeros_f[:, 0:NP], zeros_f[:, 0:NJ * 3], start=True, stop=False)
            with pe.Fori(0, TURNS) as i:
                for b in range(2):
                    gate(pe, "pe", qval_ready, 2 * i + b + 1)
                    for u in range(B):
                        mm = pe.matmul(psq, oneq[:, b, u, :], qval[:, b, u].rearrange("p r v -> p (r v)"),
                                       start=False, stop=False, skip_group_check=True)
                    mm.then_inc(qval_free, 1)
            pe.matmul(psq, zeros_f[:, 0:NP], zeros_f[:, 0:NJ * 3], start=False,
                      stop=True).then_inc(scal_ready, 1)

            n_tr = [0]
            n_mm = [0]

            def transposes(view, width):
                n_tr[0] += 1
                pe.wait_ge(tr_ready, n_tr[0])
                for j in range(NJ):
                    c = BANK * (j // 4) + NP * (j % 4)
                    mm = pe.transpose(PS[0:width, c:c + NP], view[:, j, :], ident[0:NP, 0:NP])
                mm.then_inc(tr_done, 1)

            def products(width, rhs, cout, per_bank):
                n_mm[0] += 1
                pe.wait_ge(mm_ready, n_mm[0])
                for j in range(NJ):
                    c = BANK * (j // per_bank) + cout * (j % per_bank)
                    mm = pe.matmul(PS[0:NP, c:c + cout], hT[0:width, NP * j:NP * j + NP], rhs,
                                   start=True, stop=True)
                mm.then_inc(mm_done, 1)

            def edge_pass(k):
                kind = kinds[k][0]
                t0, b0 = k * T, k * 2 * TURNS
                pe.wait_ge(agg_copied, k + 1)
                for c, w in CHUNKS:
                    pe.matmul(PS[0:M, c:c + w], zeros_l[:, 0:M], iota16[:, c:c + w], start=True, stop=False)
                s = ("pass", k)
                with pe.Fori(0, TURNS) as i:
                    for b in range(2):
                        if kind == "parts":
                            gate(pe, "pe", gathered[b], landed0[s] + per_batch[s] * i + per_batch[s])
                        else:
                            gate(pe, "pe", parts_ready, 2 * TURNS * (k - L2) + 2 * i + b + 1)
                        for u in range(b * B, b * B + B):
                            gate(pe, "pe", onehot_ready, t0 + U * i + u + 1)
                            for c, w in CHUNKS:
                                mm = pe.matmul(PS[0:M, c:c + w], parts[:, u, 0:M], oh[:, u % NOH, c:c + w],
                                               start=False, stop=False, skip_group_check=True)
                            mm.then_inc(tile_done, 1)
                for c, w in CHUNKS:
                    mm = pe.matmul(PS[0:M, c:c + w], zeros_l[:, 0:M], iota16[:, c:c + w], start=False, stop=True)
                mm.then_inc(sum_done, 1)
                pe.wait_ge(sum_copied, 2 * (k + 1))
                for j in range(NJ):
                    c = BANK * (j // 12) + 40 * (j % 12)
                    mm = pe.matmul(PS[0:NP, c:c + D + 1], accS[:, j:N:NJ], fold[:, :], start=True, stop=True)
                mm.then_inc(fold_done, 1)

            def build(n):
                width = H if n < 2 else D
                pe.wait_ge(loaded_z, 16 * (1 if n < 2 else 2))
                if n < 2:
                    wz = wbuf[:, :, n * D:(n + 1) * D]
                else:
                    wz = wbuf[0:D].rearrange("i k o -> i (k o)")[:, 0:KS ** 3 * D].rearrange("i (k o) -> i k o", o=D)
                per = BANK // D
                with pe.Fori(0, NJ) as j:
                    gate(pe, "pe", z_in, NJ * n + j + 1)
                    for h, chunks in enumerate((range(0, 5), range(5, 8))):
                        for c in chunks:
                            if c == 0:
                                gate(pe, "pe", z_dve, NJ * n + j + 1)
                            if c == 3:
                                gate(pe, "pe", z_act, NJ * n + j + 1)
                            k0, k1 = c * per, min((c + 1) * per, KS ** 3)
                            mm = pe.matmul(PS[0:NP, c * BANK:c * BANK + (k1 - k0) * D], hcur[0:width, :],
                                           wz[0:width, k0:k1, :], start=True, stop=True)
                        mm.then_inc(z_mm, 1)

            for stage in STAGES:
                if stage[0] == "pass":
                    k = stage[1]
                    edge_pass(k)
                    if L2 <= k < C1:
                        transposes(agg[:, :, 0:D], D)
                        products(D, gate_w[:, k - L2].rearrange("i g o -> i (g o)"), 3 * D, 5)
                    if k == C1 + 1:
                        transposes(h64, H)
                    if k == C2 + 1:
                        transposes(h64, H)
                        products(H, w3[:, :], H, 8)
                        transposes(h64, H)
                        products(H, w4[:, :], 3, 25)
                elif stage[0] == "build":
                    if stage[1] == 2:
                        transposes(hs, D)
                    build(stage[1])

        @block.scalar
        def _(act):
            n_ax = [0]

            def unary(pairs):
                n_ax[0] += 1
                act.wait_ge(ax_ready, n_ax[0])
                for out_, in_, f in pairs:
                    ins = nc.scalar.activation(out_, in_, f)
                ins.then_inc(ax_done, 1)

            def root(n):
                act.wait_ge(var_ready, n)
                nc.scalar.activation(st[:, 1, :], st[:, 0, :], ACT.Sqrt).then_inc(std_ready, 1)

            def set_rows(stage):
                if stage[0] == "tgather":
                    rows = [dst_i, src_i]
                else:
                    rows = kinds[stage[1]][1]
                n0 = 2 * TURNS * order[stage]
                parts_kind = stage[0] == "pass" and kinds[stage[1]][0] == "parts"
                with act.Fori(0, TURNS) as i:
                    for b in range(2):
                        if parts_kind:
                            gate(act, "act", tile_done, stage[1] * T + U * i + b * B + B)
                        else:
                            gate(act, "act", raw_free, 2 * TURNS * raw_order[stage] + 2 * i + b + 1)
                        for g, r in enumerate(rows):
                            cp = nc.scalar.copy(slots[:, b, g, :], r[:, bass.ds(U * i + b * B, B)])
                        cp.then_inc(rows_ready, 1)

            def copy_sums(k):
                act.wait_ge(sum_done, k + 1)
                nc.scalar.copy(accS[:, 1536:N], PS[0:M, 1536:N]).then_inc(sum_copied, 1)

            def build(n):
                with act.Fori(0, NJ) as j:
                    gate(act, "act", z_mm, 2 * NJ * n + 2 * j + 3)
                    gate(act, "act", z_dve, NJ * n + j + 2)
                    gate(act, "act", z_stored[1], 32 * (NJ * n + j) + 32)
                    for q in range(4):
                        cp = nc.scalar.copy(*corner(1, q // 2, q % 2))
                    cp.then_inc(z_act, 1)

            act.sem_inc(z_act, 1)
            act.wait_ge(edges_ready, 1)
            root(1)
            unary([(st[:, 7:9, :], st[:, 5:7, :], ACT.Sqrt)])
            for stage in STAGES:
                if stage[0] == "pass":
                    k = stage[1]
                    if k == C1:
                        act.wait_ge(edges_ready, 2)
                    if k == C3:
                        act.wait_ge(edges_ready, 3)
                    set_rows(stage)
                    copy_sums(k)
                    if k == L0:
                        root(2)
                    if k == L2 - 1:
                        root(3)
                    if L2 <= k < C1:
                        unary([(g3[:, :, 0, :], g3[:, :, 0, :], ACT.Sigmoid), (g3[:, :, 1, :], g3[:, :, 1, :], ACT.Tanh)])
                        unary([(g3[:, :, 2, :], g3[:, :, 2, :], ACT.Sigmoid), (tmpA[:, :, 0:D], tmpB[:, :, 0:D], ACT.Tanh)])
                    if k == C1 - 1:
                        root(4)
                    if k == C1 + 1 or k == C2 + 1:
                        unary([(tmpB, tmpA, ACT.Exp)])
                    if k == C2 + 1:
                        unary([(tmpB, tmpA, ACT.Exp)])
                elif stage[0] == "build":
                    build(stage[1])
                else:
                    set_rows(stage)

        @block.vector
        def _(dve):
            V = nc.vector
            chain = [0]

            def link(ins):
                chain[0] += 1
                ins.then_inc(dve_chain, 1)
                dve.wait_ge(dve_chain, chain[0])

            def signal(s):
                dve.sem_inc(s, 1)

            TT = lambda o, a, b_, op: link(V.tensor_tensor(o, a, b_, op))
            TS = lambda o, a, s1, op0, s2=None, op1=None: link(
                V.tensor_scalar(o, a, s1, s2, op0, op1) if op1 is not None else V.tensor_scalar(o, a, s1, None, op0))
            CP = lambda o, a: link(V.tensor_copy(o, a))

            dve.sem_inc(z_dve, 1)
            dve.sem_inc(raw_free, 2)
            dve.wait_ge(prep_mem, 3)
            for q in range(SPLITS):
                CP(fold[D * q:D * q + D, 0:D], ident[D * q:D * q + D, D * q:D * q + D])
            CP(fold[M - 1:M, D:D + 1], ident[M - 1:M, M - 1:M])
            dve.wait_ge(loaded, 16 * 14)

            eA = arena[:, 0:T]
            eB = arena[:, T:2 * T]
            eI = arena[:, 2 * T:3 * T].bitcast(I32)
            for ids, centred in ((src_i, src_c), (dst_i, dst_c)):
                CP(eA, ids[:])
                TS(centred[:], eA, -float(MID), ALU.add)
                if ids is dst_i:
                    TS(eB, eA, 1.0 / NJ, ALU.mult, 0.5 / NJ - 0.5, ALU.add)
                    CP(eI, eB)
                    CP(dst_q[:], eI)
                    link(V.scalar_tensor_tensor(dst_r[:], dst_q[:], -float(NJ), eA, ALU.mult, ALU.add))
                    TS(eB, dst_r[:], 0.0, ALU.is_lt)
                    TT(dst_q[:], dst_q[:], eB, ALU.subtract)
                    link(V.scalar_tensor_tensor(dst_r[:], dst_q[:], -float(NJ), eA, ALU.mult, ALU.add))
                    TS(eB, dst_r[:], float(NJ), ALU.is_ge)
                    TT(dst_q[:], dst_q[:], eB, ALU.add)
                    link(V.scalar_tensor_tensor(dst_r[:], dst_q[:], -float(NJ), eA, ALU.mult, ALU.add))
                TS(eA, eA, 0.0, ALU.max)
                CP(ids[:], eA)
            signal(edges_ready)
            link(V.memset(val[:, :, 0:1], 1.0))
            CP(val[:, :, 1], weight[:])
            TS(val[:, :, 2:3], val[:, :, 1:2], alphas[:, 2:3], ALU.mult, 0.0, ALU.max)

            qb = iota_q[:].unsqueeze(1).broadcast_to([P, B, NP])
            rb = iota_q[:, 0:NJ].unsqueeze(1).broadcast_to([P, B, NJ])
            with dve.Fori(0, TURNS) as i:
                for b in range(2):
                    at = bass.ds(U * i + b * B, B)
                    gate(dve, "dve", qval_free, 2 * i + b + 1)
                    V.tensor_tensor(oneq[:, b], dst_q[:, at].unsqueeze(2).broadcast_to([P, B, NP]), qb, ALU.is_equal)
                    V.tensor_tensor(oner[:, b], dst_r[:, at].unsqueeze(2).broadcast_to([P, B, NJ]), rb,
                                    ALU.is_equal).then_inc(dve_loop, 1)
                    gate(dve, "dve", dve_loop, 2 * i + b + 1)
                    V.tensor_tensor(qval[:, b], oner[:, b].unsqueeze(3).broadcast_to([P, B, NJ, 3]),
                                    val[:, at, :].unsqueeze(2).broadcast_to([P, B, NJ, 3]),
                                    ALU.mult).then_inc(qval_ready, 1)
            loop0 = [2 * TURNS]

            def layernorm(n):
                m, v = st[:, 2, :], st[:, 0, :]
                tA, tB = tmpA[:, :, 0:D], tmpB[:, :, 0:D]
                link(V.tensor_reduce(m, xs[:], AX.X, ALU.add))
                TS(m, m, -1.0 / D, ALU.mult)
                TT(tA, xs[:], m.unsqueeze(2).broadcast_to([NP, NJ, D]), ALU.add)
                TT(tB, tA, tA, ALU.mult)
                link(V.tensor_reduce(v, tB, AX.X, ALU.add))
                TS(v, v, 1.0 / D, ALU.mult, EPS, ALU.add)
                signal(var_ready)
                dve.wait_ge(std_ready, n)
                link(V.reciprocal(m, st[:, 1, :]))
                TS(tA, tA, 0.0, ALU.max)
                TT(hs[:], tA, m.unsqueeze(2).broadcast_to([NP, NJ, D]), ALU.mult)

            def split_nodes(v):
                r = tmpA[:, :, 0:D]
                CP(tb[:, :, 0:D], v)
                TT(r, v, tb[:, :, 0:D], ALU.subtract)
                CP(tb[:, :, D:2 * D], r)
                TT(tb[:, :, 2 * D:3 * D], r, tb[:, :, D:2 * D], ALU.subtract)
                signal(table_built)

            def bcn(col, width=D):
                return col.unsqueeze(2).broadcast_to([NP, NJ, width])

            DI, DW, DW2, RC, BI = 9, 10, 4, 11, 3

            def edge_pass(k):
                kind, _, seg, _ = kinds[k]
                s = ("pass", k)
                t0 = k * T
                signal(agg_copied)
                steps = {"parts": 0, "weighted": 3, "spline": 4}[kind]
                base = loop0[0]
                with dve.Fori(0, TURNS) as i:
                    for b in range(2):
                        at = bass.ds(U * i + b * B, B)
                        us = slice(b * B, b * B + B)
                        if kind != "parts":
                            n = base + (2 * i + b) * steps
                            r0 = 2 + 2 * TURNS * raw_order[s] + 2 * i + b + 1
                            gate(dve, "dve", gathered[b], landed0[s] + per_batch[s] * i + per_batch[s])
                            mb, rb_ = msg[:, b], res[:, b]
                            if kind == "weighted":
                                V.tensor_tensor(mb, raw[:, us, 0:D], val[:, at, 1:2].broadcast_to([P, B, D]),
                                                ALU.mult).then_inc(raw_free, 1)
                                gate(dve, "dve", raw_free, r0)
                            else:
                                rr = raw[:, us].rearrange("p u (c f) -> p u c f", f=D)
                                V.tensor_tensor(rr, rr, basis[:, at, :].unsqueeze(3).broadcast_to([P, B, 8, D]),
                                                ALU.mult).then_inc(dve_loop, 1)
                                gate(dve, "dve", dve_loop, n + 1)
                                V.tensor_reduce(mb, raw[:, us].rearrange("p u (c f) -> p u f c", f=D), AX.X,
                                                ALU.add).then_inc(raw_free, 1)
                                gate(dve, "dve", raw_free, r0)
                                n = n + 1
                            gate(dve, "dve", tile_done, t0 + U * i + b * B + B)
                            V.tensor_copy(parts[:, us, 0:D], mb).then_inc(dve_loop, 1)
                            gate(dve, "dve", dve_loop, n + 1)
                            V.tensor_tensor(rb_, mb, parts[:, us, 0:D], ALU.subtract).then_inc(dve_loop, 1)
                            gate(dve, "dve", dve_loop, n + 2)
                            V.tensor_copy(parts[:, us, D:2 * D], rb_).then_inc(dve_loop, 1)
                            gate(dve, "dve", dve_loop, n + 3)
                            V.tensor_tensor(parts[:, us, 2 * D:3 * D], rb_, parts[:, us, D:2 * D],
                                            ALU.subtract).then_inc(parts_ready, 1)
                        for u in range(b * B, b * B + B):
                            gate(dve, "dve", tile_done, t0 + U * i + u + 1 + U - NOH)
                            V.tensor_scalar(oh[:, u % NOH, 0:N + 1], iota16[:], seg[:, bass.ds(U * i + u, 1)], None,
                                            ALU.is_equal).then_inc(onehot_ready, 1)
                loop0[0] = base + 2 * TURNS * steps
                dve.wait_ge(sum_done, k + 1)
                V.tensor_copy(accS[:, 0:1536], PS[0:M, 0:1536]).then_inc(sum_copied, 1)
                dve.wait_ge(fold_done, k + 1)
                CP(agg[:, 0:24, :].rearrange("p (a j) d -> p a j d", a=2),
                   PS[0:NP, 0:2 * BANK].rearrange("p (a c) -> p a c", a=2)[:, :, 0:480]
                   .rearrange("p a (j d) -> p a j d", d=40)[:, :, :, 0:D + 1])
                CP(agg[:, 24, :], PS[0:NP, 2 * BANK:2 * BANK + D + 1])

            n_tr, n_mm, n_ax = [0], [0], [0]

            def transposed(width):
                signal(tr_ready)
                n_tr[0] += 1
                dve.wait_ge(tr_done, n_tr[0])
                CP(hT[0:width, 0:24 * NP].rearrange("c (a n) -> c a n", a=6),
                   PS[0:width, 0:6 * BANK].rearrange("c (a n) -> c a n", a=6)[:, :, 0:4 * NP])
                CP(hT[0:width, 24 * NP:25 * NP], PS[0:width, 6 * BANK:6 * BANK + NP])

            def product(to, cout, per_bank, bias):
                signal(mm_ready)
                n_mm[0] += 1
                dve.wait_ge(mm_done, n_mm[0])
                for a in range(0, NJ, per_bank):
                    n = min(per_bank, NJ - a)
                    c = BANK * (a // per_bank)
                    TT(to[:, a:a + n, :], PS[0:NP, c:c + n * cout].rearrange("p (j d) -> p j d", d=cout),
                       bias.unsqueeze(1).broadcast_to([NP, n, cout]), ALU.add)

            def asked():
                signal(ax_ready)
                n_ax[0] += 1
                dve.wait_ge(ax_done, n_ax[0])

            def elu(v):
                TS(tmpA, v, 0.0, ALU.min)
                asked()
                TS(v, v, 0.0, ALU.max, -1.0, ALU.add)
                TT(v, v, tmpB, ALU.add)

            def spline_basis(ps):
                pos = arena[:, 0:3 * T].rearrange("p (t c) -> p t c", c=3)
                i0 = arena[:, 3 * T:6 * T].rearrange("p (t c) -> p t c", c=3)
                one = arena[:, 6 * T:9 * T].rearrange("p (t c) -> p t c", c=3)
                q12 = arena[:, 9 * T:13 * T].rearrange("p (t q) -> p t q", q=4)
                rowf = arena[:, 13 * T:14 * T]
                TS(pos, ps, float(KS - 1), ALU.mult)
                TS(i0, pos, 1.0, ALU.is_ge)
                for step in range(2, CELLS):
                    link(V.scalar_tensor_tensor(i0, pos, float(step), i0, ALU.is_ge, ALU.add))
                TT(pos, pos, i0, ALU.subtract)
                TS(one, pos, -1.0, ALU.mult, 1.0, ALU.add)
                side = (one, pos)
                for q in range(4):
                    TT(q12[:, :, q], side[q // 2][:, :, 0], side[q % 2][:, :, 1], ALU.mult)
                for g in range(2):
                    TT(basis[:, :, 4 * g:4 * g + 4], q12, side[g][:, :, 2:3].broadcast_to([P, T, 4]), ALU.mult)
                link(V.scalar_tensor_tensor(rowf, i0[:, :, 0], float(CELLS), i0[:, :, 1], ALU.mult, ALU.add))
                link(V.scalar_tensor_tensor(rowf, rowf, float(KS), i0[:, :, 2], ALU.mult, ALU.add))
                rows = arena[:, 14 * T:15 * T]
                CP(row1[:, 0, :], rowf)
                TS(rows, rowf, 1.0, ALU.add)
                CP(row1[:, 1, :], rows)
                CP(rows, dst_i[:])
                link(V.scalar_tensor_tensor(rowf, rows, float(NODE_ROWS), rowf, ALU.mult, ALU.add))
                CP(row2[:, 0, :], rowf)
                TS(rowf, rowf, 1.0, ALU.add)
                CP(row2[:, 1, :], rowf)

            def build(n):
                width = H if n < 2 else D
                with dve.Fori(0, NJ) as j:
                    gate(dve, "dve", z_mm, 2 * NJ * n + 2 * j + 1)
                    V.tensor_copy(hcur[0:width, :], hT[0:width, bass.ds(NP * j, NP)]).then_inc(z_in, 1)
                    gate(dve, "dve", z_mm, 2 * NJ * n + 2 * j + 2)
                    gate(dve, "dve", z_stored[0], 32 * (NJ * n + j) + 32)
                    for q in range(4):
                        cp = V.tensor_copy(*corner(0, q // 2, q % 2))
                    cp.then_inc(z_dve, 1)
                for h in range(2):
                    dve.wait_ge(z_stored[h], 32 + 32 * NJ * (n + 1))

            dve.wait_ge(scal_ready, 1)
            CP(scal[:], PS[0:NP, 7 * BANK:7 * BANK + NJ * 3].rearrange("p (j v) -> p j v", v=3))
            layernorm(1)
            dve.wait_ge(loaded_w, 16 * (LAYERS * 3 + 10))
            TS(st[:, 5, :], scal[:, :, 0], 1.0, ALU.max)
            TS(scal[:, :, 1], scal[:, :, 1], 1.0, ALU.add)
            TS(st[:, 6, :], scal[:, :, 1], 1e-30, ALU.max)
            asked()
            link(V.reciprocal(st[:, DI:DI + 2, :], st[:, 7:9, :]))
            for c, row in ((0, DI), (1, DW)):
                TS(st[:, 0, :], scal[:, :, c], 0.0, ALU.is_gt)
                TT(st[:, row, :], st[:, row, :], st[:, 0, :], ALU.mult)
            TT(st[:, DW2, :], st[:, DW, :], st[:, DW, :], ALU.mult)
            TS(st[:, BI, :], scal[:, :, 2], alphas[0:NP, 1:2], ALU.mult)
            TS(st[:, 0, :], nvec[:], alphas[0:NP, 3:4], ALU.mult)
            TT(st[:, BI, :], st[:, BI, :], st[:, 0, :], ALU.add)
            for g, (m, own) in enumerate(((0, 0), (4, 2), (6, 3))):
                TT(gate_b[:, :, g, :], cb[:, :, m, :], cb[:, :, m + 1, :], ALU.add)
                TT(gate_b[:, :, g, :], gate_b[:, :, g, :], gbg[:, :, own, :], ALU.add)

            TT(cur[:], hs[:], bcn(st[:, DI, :]), ALU.mult)
            split_nodes(cur[:])
            edge_pass(L0)
            TT(cur[:], agg[:, :, 0:D], bcn(st[:, DI, :]), ALU.mult)
            TT(xs[:], xs[:], cur[:], ALU.add)

            layernorm(2)
            CP(cur[:], hs[:])
            for r in range(ITERS):
                split_nodes(cur[:])
                edge_pass(L1 + r)
                TS(cur[:], agg[:, :, 0:D], alphas[0:NP, 0:1], ALU.mult)
                TT(cur[:], cur[:], bcn(st[:, BI, :]), ALU.add)
                TS(cur[:], cur[:], 0.0, ALU.max)
            TT(xs[:], xs[:], cur[:], ALU.add)

            layernorm(3)
            CP(cur[:], hs[:])
            for l in range(LAYERS):
                TT(cur[:], cur[:], bcn(st[:, DW, :]), ALU.mult)
                signal(table_built)
                edge_pass(L2 + l)
                TT(cur[:], cur[:], agg[:, :, 0:D], ALU.add)
                TT(agg[:, :, 0:D], cur[:], bcn(st[:, DW, :]), ALU.mult)
                transposed(D)
                product(gates, 3 * D, 5, gate_b[:, l].rearrange("p g d -> p (g d)"))
                asked()
                TT(cur[:], g3[:, :, 0, :], g3[:, :, 1, :], ALU.mult)
                TT(tmpB[:, :, 0:D], cur[:], gwc[:, l, 2:3, :].broadcast_to([NP, NJ, D]), ALU.mult)
                TT(g3[:, :, 2, :], g3[:, :, 2, :], tmpB[:, :, 0:D], ALU.add)
                CP(tmpB[:, :, 0:D], cur[:])
                asked()
                TT(cur[:], g3[:, :, 2, :], tmpA[:, :, 0:D], ALU.mult)
            TT(xs[:], xs[:], cur[:], ALU.add)
            layernorm(4)

            spline_basis(attr[:])
            signal(edges_ready)
            for k0, bias in ((C1, b1), (C2, b2)):
                if k0 == C2:
                    build(0)
                    build(1)
                for h in range(2):
                    edge_pass(k0 + h)
                    if k0 + h == C1:
                        TS(st[:, RC, :], agg[:, :, D], 1.0, ALU.max)
                        link(V.reciprocal(st[:, RC, :], st[:, RC, :]))
                    TT(h64[:, :, h * D:(h + 1) * D], agg[:, :, 0:D], bcn(st[:, RC, :]), ALU.mult)
                TT(h64[:], h64[:], bias[:].unsqueeze(1).broadcast_to([NP, NJ, H]), ALU.add)
                elu(h64[:])
                transposed(H)
            product(h64, H, 8, b3[:])
            elu(h64[:])
            transposed(H)
            product(t4[:, :, 0:3], 3, 25, b4[:])
            link(V.memset(t4[:, :, 3:4], 0.0))
            signal(table_built)

            s = ("tgather", 0)
            with dve.Fori(0, TURNS) as i:
                for b in range(2):
                    gate(dve, "dve", gathered[b], landed0[s] + per_batch[s] * i + per_batch[s])
                    us = slice(b * B, b * B + B)
                    V.tensor_tensor(tdiff[:, bass.ds(U * i + b * B, B), :], raw[:, us, 0:3], raw[:, us, 4:7],
                                    ALU.subtract).then_inc(raw_free, 1)
            dve.wait_ge(raw_free, 2 + 2 * TURNS * (raw_order[s] + 1))
            TT(tdiff[:], tdiff[:], attr[:], ALU.add)
            TS(tdiff[:], tdiff[:], 0.0, ALU.max, 1.0, ALU.min)
            spline_basis(tdiff[:])
            signal(edges_ready)
            transposed(D)
            build(2)
            edge_pass(C3)
            TT(cur[:], agg[:, :, 0:D], bcn(st[:, RC, :]), ALU.mult)
            TT(cur[:], cur[:], bc[:].unsqueeze(1).broadcast_to([NP, NJ, D]), ALU.add)
            TT(xs[:], xs[:], cur[:], ALU.add)
            signal(out_ready)


_INS = ["x", "src", "dst", "edge_attr_3", "edge_weight", "node_vec", "L1_gnn_alpha1", "L1_gnn_alpha2",
        "L1_gnn_alpha3", "L1_gnn_alpha4", "L2_gnn_conv_w", "L2_gnn_conv_b", "L2_gnn_wc", "L2_gnn_bg",
        "L3_gnn_stn1_w", "L3_gnn_stn1_b", "L3_gnn_stn2_w", "L3_gnn_stn2_b", "L3_gnn_stn3_w",
        "L3_gnn_stn3_b", "L3_gnn_stn4_w", "L3_gnn_stn4_b", "L3_gnn_conv_w", "L3_gnn_conv_b"]


def kernel(**inputs):
    import concourse.bacc as bacc
    from concourse.bass_utils import run_bass_kernel_spmd

    nc = bacc.Bacc("TRN2", target_bir_lowering=False, num_devices=1)
    arrays, args = {}, []
    for name in _INS:
        a = np.ascontiguousarray(inputs[name])
        arrays[f"in_{name}"] = a
        args.append(nc.dram_tensor(f"in_{name}", a.shape, mybir.dt.from_np(a.dtype), kind="ExternalInput").ap())
    out = nc.dram_tensor("out_x", inputs["x"].shape, F32, kind="ExternalOutput").ap()
    gnn_kernel(nc, *args, out)
    r = run_bass_kernel_spmd(nc, [arrays], core_ids=[0])
    return r.results[0]["out_x"]
```

```python
from contextlib import ExitStack

import numpy as np

import concourse.bass as bass
from concourse import mybir

ALU = mybir.AluOpType
ACT = mybir.ActivationFunctionType
AX = mybir.AxisListType
F32 = mybir.dt.float32
F16 = mybir.dt.float16
BF16 = mybir.dt.bfloat16
I32 = mybir.dt.int32

P = 128
D = 32
SPLITS = 3
EPS = 1e-5
ITERS = 4
KS = 5
CELLS = KS - 1
NODE_ROWS = CELLS * CELLS * KS


def gnn_kernel(nc, x, src, dst, edge_attr, edge_weight, node_vec, alpha1, alpha2, alpha3, alpha4,
               conv_w, conv_b, wc, bg, stn1_w, stn1_b, stn2_w, stn2_b, stn3_w, stn3_b, stn4_w,
               stn4_b, sconv_w, sconv_b, out):
    N = x.shape[0]
    E = src.shape[0]
    LAYERS = conv_w.shape[0]
    H = stn2_w.shape[1]
    NP = 125
    NJ = N // NP
    assert NP * NJ == N and H == 2 * D
    U = 8
    B = U // 2
    TURNS = -(-E // (P * U))
    T = TURNS * U
    TAIL = E - (P - 1) * T
    MID = N // 2
    BANK = 512
    CHUNKS = [(c, min(BANK, N - c)) for c in range(0, N, BANK)]
    M = SPLITS * D + 1
    NOH = 4
    G = -(-(E + P * NJ) // (P * U)) * U
    GTURNS = G // U
    PC = 9
    ZROWS = CELLS * KS
    ZS = ZROWS * 4 * H
    SIDE = CELLS
    ZBANKS = 4
    KP1 = KS ** 3 + 1

    PASSES = LAYERS
    ROUNDS = 1 + ITERS
    RING = 5
    DB = 448
    DPARTS = [(n, c, min(DB, N - c)) for n, c in enumerate(range(0, N, DB))]

    ctx = ExitStack()
    with ctx:
        def sb(name, shape, dt=F32):
            return ctx.enter_context(nc.sbuf_tensor(name, shape, dt))

        def sem(name):
            return ctx.enter_context(nc.semaphore(name))

        tab_feat = nc.dram_tensor("tab_feat", (N, D), F32).ap()
        tab_t = nc.dram_tensor("tab_t", (N, 4), F32).ap()
        tab_z = [nc.dram_tensor(f"tab_z_{n}", (N * NODE_ROWS, 4 * c), F32).ap() for n, c in enumerate((H, D))]
        adj = nc.dram_tensor("adj", (NJ, NP, N), F32).ap()
        rows_dram = nc.dram_tensor("rows_dram", (P * G + T, PC), F32).ap()

        PS = ctx.enter_context(nc.psum_tensor("PS", [P, 8 * BANK], F32))

        src_i, dst_i = sb("src_i", [P, T], I32), sb("dst_i", [P, T], I32)
        dst_c = sb("dst_c", [P, T])
        weight = sb("weight", [P, T])
        val = sb("val", [P, T, 3])
        dst_q, dst_r = sb("dst_q", [P, T]), sb("dst_r", [P, T])
        pay = sb("pay", [P, G, PC])
        basis = sb("basis", [P, G, 8])
        row2 = sb("row2", [P, 2, G], I32)
        dstg = sb("dstg", [P, G])
        block_of = sb("block_of", [1, G], I32)
        first_of = sb("first_of", [1, NJ + 1], I32)
        iota16 = sb("iota16", [P, N + 1], F16)
        iota_q = sb("iota_q", [P, NP])
        iota_c = sb("iota_c", [P, G])
        ident = sb("ident", [P, P])
        upper = sb("upper", [P, P])
        ones_f = sb("ones_f", [P, P])
        fold = sb("fold", [M, D + 1])
        zeros_l = sb("zeros_l", [P, P], BF16)
        zeros_f = sb("zeros_f", [P, P])
        alphas = sb("alphas", [P, 4])
        arena = sb("arena", [P, 2 * ZS])
        OHW = (N + 2) // 2
        oh2 = arena[:, 0:2 * OHW].bitcast(BF16)
        srch2 = arena[:, NOH * OHW:NOH * OHW + P].bitcast(BF16)
        oh = arena[:, 0:NOH * OHW].bitcast(BF16).rearrange("p (s n) -> p s n", s=NOH)
        RAW0 = NOH * OHW
        rawf = arena[:, RAW0:RAW0 + U * D].rearrange("p (u r) -> p u r", u=U)
        raw = arena[:, 0:U * 8 * H].rearrange("p (u r) -> p u r", u=U)
        grq = arena[:, U * 8 * H:U * 8 * H + 2 * B * NP].rearrange("p (b u q) -> p b u q", b=2, u=B)
        GM0 = U * 8 * H + 2 * B * NP
        gmsg = arena[:, GM0:GM0 + 2 * B * H].rearrange("p (b u f) -> p b u f", b=2, u=B)
        FREE0 = ZROWS * 4 * D
        rawt = arena[:, FREE0:FREE0 + U * 4].rearrange("p (u r) -> p u r", u=U)
        hotT = arena[0:NP, FREE0 + U * 4:FREE0 + U * 4 + 2 * BANK].rearrange("p (b n) -> p b n", b=2)
        assert FREE0 + U * 4 + 2 * BANK <= U * 8 * H and GM0 <= ZS
        hats = arena[:, 9 * G:24 * G].rearrange("p (c g k) -> p c g k", c=3, k=KS)
        HB0 = 0
        hat12 = arena[:, HB0:HB0 + 2 * B * KS * KS].rearrange("p (b u k) -> p b u k", b=2, u=B)
        HC0 = HB0 + 2 * B * KS * KS
        hat123 = arena[:, HC0:HC0 + 2 * B * KP1].rearrange("p (b u k) -> p b u k", b=2, u=B)
        HQ0 = HC0 + 2 * B * KP1
        hatq = arena[:, HQ0:HQ0 + 2 * B * NP].rearrange("p (b u q) -> p b u q", b=2, u=B)
        zs = arena[:, :].rearrange("p (h c) -> p h c", h=2)
        oneq = arena[:, 0:2 * B * NP].rearrange("p (b u q) -> p b u q", b=2, u=B)
        oner = arena[:, 1000:1000 + 2 * B * NJ].rearrange("p (b u r) -> p b u r", b=2, u=B)
        qval = arena[:, 1200:1200 + 2 * B * NJ * 3].rearrange("p (b u r v) -> p b u r v", b=2, u=B, v=3)
        parts = sb("parts", [P, U, M + 1], BF16)
        pslot = sb("pslot", [P, 2, B, PC])
        slots = sb("slots", [P, 2, 2, B], I32)
        msg = sb("msg", [P, 2, B, D])
        res = sb("res", [P, 2, B, D])
        acc = sb("acc", [P, PC * T])
        accS = acc[0:M, 0:N]
        accA = acc[0:NP, 0:N]
        pay0 = acc[:, 0:PC * T].rearrange("p (t c) -> p t c", c=PC)
        pos_i = sb("pos_i", [P, T], I32)
        xs, hs, cur = (sb(n, [NP, NJ, D]) for n in ("xs", "hs", "cur"))
        agg = sb("agg", [NP, NJ, D + 1])
        lcur = sb("lcur", [NP, RING, D])
        h64 = sb("h64", [NP, NJ, H])
        hT = sb("hT", [P, NJ * NP])
        hcur = sb("hcur", [H, NP])
        scal = sb("scal", [NP, NJ, 3])
        nvec = sb("nvec", [NP, NJ])
        st = sb("st", [NP, 12, NJ])
        t4 = sb("t4", [NP, NJ, 4])
        t4f = t4[:].rearrange("p j c -> p (j c)")
        wb = sb("wb", [P, KS ** 3 * H])
        wbuf = wb[0:H, :].rearrange("i (k o) -> i k o", o=H)
        hot_g = arena[:, 6 * T:6 * T + NJ * T // 2].bitcast(F16)
        run_g = wb[:, 0:NJ * T // 2].bitcast(F16)
        attr0 = wb[:, NJ * T // 2:NJ * T // 2 + 3 * T].rearrange("p (t c) -> p t c", c=3)
        ring = [arena[0:NP, n * N:(n + 1) * N] for n in range(3)] + [wb[0:NP, n * N:(n + 1) * N] for n in range(2)]
        st128 = sb("st128", [P, 6, NJ])
        hsum = arena[0:NP, 0:NJ * KP1].rearrange("p (j k) -> p j k", k=KP1)
        gate_w = sb("gate_w", [D, LAYERS, 3, D])
        gate_b = sb("gate_b", [NP, LAYERS, 3, D])
        cb = sb("cb", [NP, LAYERS, 8, D])
        gbg = sb("gbg", [NP, LAYERS, 4, D])
        gwc = sb("gwc", [NP, LAYERS, 3, D])
        w1 = sb("w1", [KS ** 3, H])
        w3, w4 = sb("w3", [H, H]), sb("w4", [H, 3])
        b1, b2, b3 = sb("b1", [NP, H]), sb("b2", [NP, H]), sb("b3", [NP, H])
        b4, bc = sb("b4", [NP, 3]), sb("bc", [NP, D])

        def tmp(width, at):
            return arena[0:NP, at:at + NJ * width].rearrange("p (j d) -> p j d", j=NJ)

        tmpA, tmpB = tmp(H, 0), tmp(H, NJ * H)
        gates = tmp(3 * D, 2 * NJ * H)
        g3 = gates.rearrange("p j (g d) -> p j g d", g=3)

        prep_mem = sem("prep_mem")
        loaded = sem("loaded")
        loaded_w = sem("loaded_w")
        loaded_z = sem("loaded_z")
        holes_stored = sem("holes_stored")
        pay_ready = sem("pay_ready")
        rank_in, rank_mm = sem("rank_in"), sem("rank_mm")
        pslot_ready = sem("pslot_ready")
        scattered = [sem(f"scattered{b}") for b in range(2)]
        pay_loaded = sem("pay_loaded")
        blocks_ready = sem("blocks_ready")
        ahot_ready, ahot_used = sem("ahot_ready"), sem("ahot_used")
        a_sum = sem("a_sum")
        a_copied = sem("a_copied")
        a_stored = sem("a_stored")
        a_loaded = [sem(f"a_loaded{n}") for n in range(RING)]
        a_used = sem("a_used")
        dense_in = sem("dense_in")
        lcur_ready, dense_done = sem("lcur_ready"), sem("dense_done")
        hat_ready, hat_done = sem("hat_ready"), sem("hat_done")
        hat_sum = sem("hat_sum")
        gmsg_ready, gmsg_done = sem("gmsg_ready"), sem("gmsg_done")
        hot_ready = sem("hot_ready")
        hot_turned = sem("hot_turned")
        hot_copied = sem("hot_copied")
        tsrc_ready = sem("tsrc_ready")
        gsum_done = sem("gsum_done")
        dve_chain = sem("dve_chain")
        qval_ready = sem("qval_ready")
        qval_free = sem("qval_free")
        scal_ready = sem("scal_ready")
        var_ready, std_ready = sem("var_ready"), sem("std_ready")
        table_built, table_stored = sem("table_built"), sem("table_stored")
        rows_ready = sem("rows_ready")
        edges_ready = sem("edges_ready")
        gathered = [sem(f"gathered{b}") for b in range(2)]
        raw_free = sem("raw_free")
        dve_loop = sem("dve_loop")
        parts_ready = sem("parts_ready")
        onehot_ready = sem("onehot_ready")
        tile_done = sem("tile_done")
        sum_done = sem("sum_done")
        sum_copied = sem("sum_copied")
        fold_done = sem("fold_done")
        agg_copied = sem("agg_copied")
        tr_ready, tr_done = sem("tr_ready"), sem("tr_done")
        mm_ready, mm_done = sem("mm_ready"), sem("mm_done")
        ax_ready, ax_done = sem("ax_ready"), sem("ax_done")
        z_in = sem("z_in")
        z_mm = sem("z_mm")
        z_dve, z_act = sem("z_dve"), sem("z_act")
        z_stored = [sem(f"z_stored{h}") for h in range(2)]
        t_stored = sem("t_stored")
        out_ready, out_stored = sem("out_ready"), sem("out_stored")
        gate_pass = {e: sem(f"gate_{e}") for e in ("pool", "act", "dve", "pe", "sp")}

        def gate(eng, name, s, value):
            eng.wait_ge(s, value)
            eng.sem_inc(gate_pass[name], 1)

        def node_rows(ap):
            return ap.rearrange("(p j) d -> p j d", p=NP)

        STAGES = [("adj", 0)] + [("dense", k) for k in range(ROUNDS)] + [("pass", k) for k in range(PASSES)]
        STAGES += [("hats", 0), ("build", 0), ("grouped", 0), ("offsets", 1), ("grouped", 1)]
        GATHERS = [s for s in STAGES if s[0] in ("pass", "offsets", "grouped")]
        turns_of = {s: TURNS if s[0] == "pass" else GTURNS for s in GATHERS}
        order, landed0, raw0 = {}, {}, {}
        n_rows = n_landed = n_raw = 0
        per_batch = {s: 16 * B * (2 if s[0] == "grouped" else 1) for s in GATHERS}
        for s in GATHERS:
            order[s], landed0[s], raw0[s] = n_rows, n_landed, n_raw
            n_rows += 2 * turns_of[s]
            n_landed += turns_of[s] * per_batch[s]
            n_raw += 2 * turns_of[s]

        def corner(plane, c1, d1, d2, width):
            to = zs[0:NP, c1 % 2, 0:ZROWS * 4 * width].rearrange("p (b q f) -> p b q f", b=ZROWS, q=4)
            c0 = (plane % 2) * ZBANKS * BANK + d2 * KS * width
            return to[:, :, 2 * d1 + d2, :], PS[0:NP, c0:c0 + ZROWS * width].rearrange("p (b f) -> p b f", f=width)

        block = ctx.enter_context(nc.Block())

        @block.sync
        def _(sp):
            for h in range(2):
                sp.sem_inc(z_stored[h], 32)
            sp.sem_inc(a_stored, 32)
            sp.wait_ge(prep_mem, 2)
            FULL = (P - 1) * T
            for a, d in ((src, src_i), (dst, dst_i), (edge_weight, weight)):
                sp.dma_start(d[0:P - 1, :],
                             a[0:FULL].rearrange("(p t) -> p t", p=P - 1)).then_inc(loaded, 16)
                sp.dma_start(d[P - 1:P, 0:TAIL],
                             a[FULL:E].rearrange("(p t) -> p t", p=1)).then_inc(loaded, 16)
            sp.dma_start(attr0[0:P - 1, :, :],
                         edge_attr[0:FULL, :].rearrange("(p t) c -> p t c", p=P - 1)).then_inc(loaded, 16)
            sp.dma_start(attr0[P - 1:P, 0:TAIL, :],
                         edge_attr[FULL:E, :].rearrange("(p t) c -> p t c", p=1)).then_inc(loaded, 16)
            sp.dma_start(xs[:], node_rows(x)).then_inc(loaded, 16)
            sp.dma_start(nvec[:], node_vec.rearrange("(p j) -> p j", p=NP)).then_inc(loaded, 16)
            for i, a in enumerate((alpha1, alpha2, alpha3, alpha4)):
                sp.dma_start(alphas[:, i:i + 1], a.partition_broadcast(P)).then_inc(loaded, 16)
            grouped_dram = rows_dram[0:P * G, :].rearrange("(p g) c -> p (g c)", p=P)
            sp.dma_start(grouped_dram, pay[:].rearrange("p g c -> p (g c)")).then_inc(holes_stored, 16)
            for l in range(LAYERS):
                for g, m in enumerate((0, 4, 6)):
                    sp.dma_start(gate_w[:, l, g, :], conv_w[l, m]).then_inc(loaded_w, 16)
            sp.dma_start(cb[:], conv_b.partition_broadcast(NP)).then_inc(loaded_w, 16)
            sp.dma_start(gbg[:], bg.partition_broadcast(NP)).then_inc(loaded_w, 16)
            sp.dma_start(gwc[:], wc.partition_broadcast(NP)).then_inc(loaded_w, 16)
            for d, a in ((b1, stn1_b), (b2, stn2_b), (b3, stn3_b), (b4, stn4_b), (bc, sconv_b)):
                sp.dma_start(d[:], a.partition_broadcast(NP)).then_inc(loaded_w, 16)
            sp.dma_start(w1[:], stn1_w.rearrange("k one f -> k (one f)")).then_inc(loaded_w, 16)
            sp.dma_start(w3[:], stn3_w).then_inc(loaded_w, 16)
            sp.dma_start(w4[:], stn4_w).then_inc(loaded_w, 16)
            for b in range(2):
                sp.wait_ge(scattered[b], 16 * B * TURNS)
            sp.dma_start(pay[:].rearrange("p g c -> p (g c)"), grouped_dram).then_inc(pay_loaded, 16)
            with sp.Fori(0, NJ) as j:
                sp.wait_ge(a_copied, 2 * j + 4)
                for p0, p1 in ((0, 112), (112, NP)):
                    sp.dma_start(adj[bass.ds(j, 1), p0:p1].squeeze(0), accA[p0:p1]).then_inc(a_stored, 16)
            sp.wait_ge(a_stored, 32 * NJ + 32)
            sp.sem_inc(a_used, RING)
            for k in range(ROUNDS):
                with sp.Fori(0, NJ // RING) as i:
                    for n in range(RING):
                        sp.wait_ge(a_used, k * NJ + RING * i + n + 1)
                        for p0, p1 in ((0, 112), (112, NP)):
                            sp.dma_start(ring[n][p0:p1], adj[bass.ds(RING * i + n, 1), p0:p1].squeeze(0)
                                         ).then_inc(a_loaded[n], 16)
            sp.wait_ge(a_used, RING + NJ * ROUNDS)
            sp.dma_start(wbuf[:], stn2_w.rearrange("k i o -> i k o")).then_inc(loaded_z, 16)
            for k in range(PASSES):
                sp.wait_ge(table_built, k + 1)
                sp.dma_start(node_rows(tab_feat), cur[:]).then_inc(table_stored, 16)

            def store_table(n, width):
                zt = tab_z[n].rearrange("(p j c r) f -> j c p (r f)", p=NP, j=NJ, c=CELLS)
                with sp.Fori(0, NJ) as j:
                    for c1 in range(CELLS):
                        sp.wait_ge(z_act, CELLS * (NJ * n + j) + c1 + 2)
                        for p0, p1 in ((0, 112), (112, NP)):
                            sp.dma_start(zt[bass.ds(j, 1), c1, p0:p1].squeeze(0),
                                         zs[p0:p1, c1 % 2, 0:ZROWS * 4 * width]).then_inc(z_stored[c1 % 2], 16)

            store_table(0, H)
            sp.wait_ge(z_mm, KS * NJ + 1)
            sp.dma_start(wbuf[0:D].rearrange("i k o -> i (k o)")[:, 0:KS ** 3 * D]
                         .rearrange("i (k o) -> i k o", o=D),
                         sconv_w.rearrange("k i o -> i k o")).then_inc(loaded_z, 16)
            sp.wait_ge(table_built, PASSES + 1)
            sp.dma_start(node_rows(tab_t), t4[:]).then_inc(t_stored, 16)
            store_table(1, D)
            sp.wait_ge(out_ready, 1)
            sp.dma_start(node_rows(out), xs[:]).then_inc(out_stored, 16)
            sp.wait_ge(out_stored, 16)

        @block.gpsimd
        def _(pool):
            for d in (src_i, dst_i):
                nc.gpsimd.memset(d[:, TAIL:T], -1)
            nc.gpsimd.memset(weight[:, TAIL:T], 0.0)
            nc.gpsimd.memset(attr0[:, TAIL:T, :], 0.0)
            nc.gpsimd.memset(pay[:], 0.0)
            pool.drain().then_inc(prep_mem, 1)
            pool.wait_ge(prep_mem, 1)
            nc.gpsimd.memset(pay[:, :, 0:1], -1.0)
            pool.drain().then_inc(prep_mem, 1)
            nc.gpsimd.memset(parts[:], 1.0)
            nc.gpsimd.memset(zeros_l[:], 0.0)
            nc.gpsimd.memset(zeros_f[:], 0.0)
            nc.gpsimd.memset(ident[:], 0.0)
            nc.gpsimd.memset(ones_f[:], 1.0)
            nc.gpsimd.memset(fold[:], 0.0)
            nc.gpsimd.iota(iota16[:], pattern=[[1, N + 1]], base=-MID, channel_multiplier=0,
                           allow_small_or_imprecise_dtypes=True)
            nc.gpsimd.iota(iota_c[:], pattern=[[1, G]], base=0, channel_multiplier=0,
                           allow_small_or_imprecise_dtypes=True)
            nc.gpsimd.iota(iota_q[:], pattern=[[1, NP]], base=0, channel_multiplier=0,
                           allow_small_or_imprecise_dtypes=True)
            pool.drain().then_inc(prep_mem, 1)
            pool.wait_ge(prep_mem, 3)
            nc.gpsimd.affine_select(out=upper[:], in_=ones_f[:], compare_op=ALU.is_gt, fill=0.0,
                                    base=0, pattern=[[1, P]], channel_multiplier=-1)
            nc.gpsimd.affine_select(out=ident[:], in_=ident[:], compare_op=ALU.not_equal, fill=1.0,
                                    base=0, pattern=[[-1, P]], channel_multiplier=1).then_inc(prep_mem, 1)

            pool.wait_ge(holes_stored, 16)
            with pool.Fori(0, TURNS) as i:
                for b in range(2):
                    gate(pool, "pool", pslot_ready, 2 * i + b + 1)
                    for u in range(B):
                        nc.gpsimd.indirect_dma_start(
                            out=rows_dram, out_offset=bass.IndirectOffsetOnAxis(ap=slots[:, b, 0, u:u + 1], axis=0),
                            in_=pslot[:, b, u, :], in_offset=None).then_inc(scattered[b], 16)

            def gathers(stage):
                if stage[0] == "offsets":
                    tables, outs = [tab_t], lambda b, u, g: rawt[:, b * B + u, :]
                    pool.wait_ge(t_stored, 16)
                elif stage[0] == "grouped":
                    n = stage[1]
                    w = 4 * (H, D)[n]
                    tables, outs = [tab_z[n]] * 2, lambda b, u, g: raw[:, b * B + u, g * w:(g + 1) * w]
                    for h in range(2):
                        pool.wait_ge(z_stored[h], 32 + 32 * 2 * NJ * (n + 1))
                else:
                    pool.wait_ge(table_stored, 16 * (stage[1] + 1))
                    tables, outs = [tab_feat], lambda b, u, g: rawf[:, b * B + u, :]
                with pool.Fori(0, turns_of[stage]) as i:
                    for b in range(2):
                        gate(pool, "pool", rows_ready, order[stage] + 2 * i + b + 1)
                        for u in range(B):
                            for g, table in enumerate(tables):
                                nc.gpsimd.indirect_dma_start(
                                    out=outs(b, u, g), out_offset=None, in_=table,
                                    in_offset=bass.IndirectOffsetOnAxis(ap=slots[:, b, g, u:u + 1], axis=0),
                                ).then_inc(gathered[b], 16)

            for stage in GATHERS:
                gathers(stage)

        @block.tensor
        def _(pe):
            pe.sem_inc(tile_done, U)
            pe.sem_inc(qval_free, 2)
            pe.sem_inc(z_mm, 1)
            pe.wait_ge(prep_mem, 4)

            pe.wait_ge(rank_in, 1)
            pe.matmul(PS[:, 6 * BANK:6 * BANK + NJ], ones_f[:, :], st128[:, 0, :], start=True, stop=True)
            pe.matmul(PS[:, 6 * BANK + 64:6 * BANK + 64 + NJ], upper[:, :], st128[:, 0, :], start=True,
                      stop=True).then_inc(rank_mm, 1)

            S0 = 7 * BANK
            psq = PS[0:NP, S0:S0 + NJ * 3]
            pe.matmul(psq, zeros_f[:, 0:NP], zeros_f[:, 0:NJ * 3], start=True, stop=False)
            with pe.Fori(0, TURNS) as i:
                for b in range(2):
                    pe.wait_ge(qval_ready, 2 * i + b + 1)
                    for u in range(B):
                        mm = pe.matmul(psq, oneq[:, b, u, :], qval[:, b, u].rearrange("p r v -> p (r v)"),
                                       start=False, stop=False, skip_group_check=True)
                    mm.then_inc(qval_free, 1)
            pe.matmul(psq, zeros_f[:, 0:NP], zeros_f[:, 0:NJ * 3], start=False,
                      stop=True).then_inc(scal_ready, 1)

            n_tr = [0]
            n_mm = [0]

            def transposes(view, width):
                n_tr[0] += 1
                pe.wait_ge(tr_ready, n_tr[0])
                for j in range(NJ):
                    c = BANK * (j // 4) + NP * (j % 4)
                    mm = pe.transpose(PS[0:width, c:c + NP], view[:, j, :], ident[0:NP, 0:NP])
                mm.then_inc(tr_done, 1)

            def products(lhs, rhs, cout, per_bank):
                n_mm[0] += 1
                pe.wait_ge(mm_ready, n_mm[0])
                for j in range(NJ):
                    c = BANK * (j // per_bank) + cout * (j % per_bank)
                    mm = pe.matmul(PS[0:NP, c:c + cout], lhs[:, NP * j:NP * j + NP], rhs,
                                   start=True, stop=True)
                mm.then_inc(mm_done, 1)

            def edge_pass(k):
                t0 = k * T
                pe.wait_ge(agg_copied, 2 + ROUNDS + k)
                for c, w in CHUNKS:
                    pe.matmul(PS[0:M, c:c + w], zeros_l[:, 0:M], iota16[:, c:c + w], start=True, stop=False)
                s = ("pass", k)
                with pe.Fori(0, TURNS) as i:
                    for b in range(2):
                        pe.wait_ge(parts_ready, 2 * TURNS * k + 2 * i + b + 1)
                        for u in range(b * B, b * B + B):
                            pe.wait_ge(onehot_ready, t0 + U * i + u + 1)
                            for c, w in CHUNKS:
                                mm = pe.matmul(PS[0:M, c:c + w], parts[:, u, 0:M], oh[:, u % NOH, c:c + w],
                                               start=False, stop=False, skip_group_check=True)
                            mm.then_inc(tile_done, 1)
                for c, w in CHUNKS:
                    mm = pe.matmul(PS[0:M, c:c + w], zeros_l[:, 0:M], iota16[:, c:c + w], start=False, stop=True)
                mm.then_inc(sum_done, 1)
                pe.wait_ge(sum_copied, 2 * (ROUNDS + k + 1))
                for j in range(NJ):
                    c = BANK * (j // 12) + 40 * (j % 12)
                    mm = pe.matmul(PS[0:NP, c:c + D + 1], accS[:, j:N:NJ], fold[:, :], start=True, stop=True)
                mm.then_inc(fold_done, 1)

            def adjacency():
                pe.sem_inc(ahot_used, 2)
                pe.wait_ge(blocks_ready, 1)
                pe.wait_ge(agg_copied, 1)
                with pe.Fori(0, NJ) as j:
                    g0, g1 = nc.values_load_multi_w_load_instructions(
                        first_of[0:1, bass.ds(j, 2)], engines=(mybir.EngineType.PE,), min_val=0, max_val=G)[1]
                    pe.wait_ge(a_copied, 2 * j + 2)
                    for c, w in CHUNKS:
                        pe.matmul(PS[0:NP, c:c + w], zeros_l[:, 0:NP], iota16[:, c:c + w], start=True, stop=True)
                    with pe.Fori(g0, g1) as g:
                        pe.wait_ge(ahot_ready, g + 1)
                        for c, w in CHUNKS:
                            mm = pe.matmul(PS[0:NP, c:c + w], srch2[:, bass.ds((g % 2) * P, NP)],
                                           oh2[:, bass.ds((g % 2) * 2 * OHW + c, w)],
                                           start=False, stop=True, skip_group_check=True)
                        mm.then_inc(ahot_used, 1)
                    pe.matmul(PS[0:1, 7 * BANK:7 * BANK + 1], zeros_l[:, 0:1], iota16[:, 0:1], start=True,
                              stop=True).then_inc(a_sum, 1)

            def dense_round(k):
                pe.wait_ge(agg_copied, 2 + k)
                with pe.Fori(0, NJ // RING) as i:
                    pe.wait_ge(lcur_ready, k * (NJ // RING) + i + 1)
                    for n in range(RING):
                        pe.wait_ge(a_loaded[n], 32 * (k * (NJ // RING) + i) + 32)
                        for m, c, w in DPARTS:
                            o = PS[D * (m % 4):D * (m % 4) + D, (m // 4) * BANK:(m // 4) * BANK + w]
                            mm = pe.matmul(o, lcur[:, n, :], ring[n][:, c:c + w], start=False, stop=True,
                                           skip_group_check=True)
                        mm.then_inc(a_used, 1)
                pe.matmul(PS[0:1, 7 * BANK:7 * BANK + 1], zeros_l[:, 0:1], iota16[:, 0:1], start=True,
                          stop=True).then_inc(dense_done, 1)
                pe.wait_ge(sum_copied, 2 * (k + 1))
                for j in range(NJ):
                    c = BANK * (j // 12) + 40 * (j % 12)
                    mm = pe.transpose(PS[0:NP, c:c + D], acc[0:D, j:N:NJ], ident[0:D, 0:D])
                mm.then_inc(fold_done, 1)

            def group_of(turn):
                return nc.values_load_multi_w_load_instructions(
                    block_of[0:1, bass.ds(U * turn, U)], engines=(mybir.EngineType.PE,), min_val=0,
                    max_val=NJ - 1)[1]

            def zero_banks(first, last):
                for c in range(0, 7 * BANK, BANK):
                    mm = pe.matmul(PS[0:NP, c:c + BANK], zeros_l[:, 0:NP], iota16[:, 0:BANK], start=first, stop=last)
                return mm

            def hat_sums():
                pe.wait_ge(blocks_ready, 1)
                pe.wait_ge(agg_copied, 2 + ROUNDS + PASSES)
                zero_banks(True, False)
                with pe.Fori(0, GTURNS) as i:
                    group = group_of(i)
                    for b in range(2):
                        pe.wait_ge(hat_ready, 2 * i + b + 1)
                        for u in range(B):
                            mm = pe.matmul(PS[0:NP, bass.ds(group[b * B + u] * P, KP1)], hatq[:, b, u, :],
                                           hat123[:, b, u, :], start=False, stop=False, skip_group_check=True)
                        mm.then_inc(hat_done, 1)
                zero_banks(False, True).then_inc(hat_sum, 1)

            def grouped_pass(n):
                width = (H, D)[n]
                pe.wait_ge(agg_copied, 3 + ROUNDS + PASSES + n)
                zero_banks(True, False)
                with pe.Fori(0, GTURNS) as i:
                    group = group_of(i)
                    for b in range(2):
                        pe.wait_ge(gmsg_ready, 2 * (GTURNS * n + i) + b + 1)
                        for u in range(B):
                            mm = pe.matmul(PS[0:NP, bass.ds(group[b * B + u] * width, width)], grq[:, b, u, :],
                                           gmsg[:, b, u, 0:width], start=False, stop=False, skip_group_check=True)
                        mm.then_inc(gmsg_done, 1)
                zero_banks(False, True).then_inc(gsum_done, 1)

            def turn_sources(i, q):
                pe.wait_ge(hot_ready, i + q + 1)
                for u in range(B):
                    c = (2 + 4 * (q % 2)) * BANK + u * P
                    mm = pe.transpose(PS[0:NP, c:c + P], grq[:, q % 2, u, :], ident[:, :])
                mm.then_inc(hot_turned, 1)

            def source_offsets(i, q):
                group = nc.values_load_multi_w_load_instructions(
                    block_of[0:1, bass.ds(B * i + B * q, B)], engines=(mybir.EngineType.PE,), min_val=0,
                    max_val=NJ - 1)[1]
                pe.wait_ge(hot_copied, i + q + 1)
                for u in range(B):
                    c = (3 + 4 * (q % 2)) * BANK + 4 * u
                    mm = pe.matmul(PS[:, c:c + 4], hotT[:, q % 2, u * P:(u + 1) * P],
                                   t4f[:, bass.ds(group[u] * 4, 4)], start=True, stop=True)
                mm.then_inc(tsrc_ready, 1)

            def build(n):
                width = (H, D)[n]
                pe.wait_ge(loaded_z, 16 * (n + 1))
                wz = wbuf if n == 0 else \
                    wbuf[0:D].rearrange("i k o -> i (k o)")[:, 0:KS ** 3 * D].rearrange("i (k o) -> i k o", o=D)
                per = BANK // width
                with pe.Fori(0, NJ) as j:
                    pe.wait_ge(z_in, NJ * n + j + 1)
                    for plane in range(KS):
                        if plane >= 1:
                            pe.wait_ge(z_dve, CELLS * (NJ * n + j) + max(plane - 1, 0) + 1)
                        if plane != 1:
                            pe.wait_ge(z_act, CELLS * (NJ * n + j) + max(plane - 2, 0) + 1)
                        for k0 in range(0, KS * KS, per):
                            k1 = min(k0 + per, KS * KS)
                            c = (plane % 2) * ZBANKS * BANK + k0 * width
                            mm = pe.matmul(PS[0:NP, c:c + (k1 - k0) * width], hcur[0:width, :],
                                           wz[0:width, plane * KS * KS + k0:plane * KS * KS + k1, :],
                                           start=True, stop=True)
                        mm.then_inc(z_mm, 1)
                        if n == 1 and plane >= 1:
                            source_offsets(SIDE * j, plane - 1)
                        if n == 1 and plane < SIDE:
                            turn_sources(SIDE * j, plane)
                if n == 1:
                    for q in range(SIDE * NJ, 2 * GTURNS):
                        turn_sources(0, q)
                        source_offsets(0, q)

            for stage in STAGES:
                if stage[0] == "adj":
                    adjacency()
                elif stage[0] == "dense":
                    dense_round(stage[1])
                elif stage[0] == "pass":
                    k = stage[1]
                    edge_pass(k)
                    transposes(agg[:, :, 0:D], D)
                    products(hT[0:D], gate_w[:, k].rearrange("i g o -> i (g o)"), 3 * D, 5)
                elif stage[0] == "hats":
                    hat_sums()
                    transposes(hsum[:, :, 0:KS ** 3], KS ** 3)
                    products(hT[0:KS ** 3], w1[:, :], H, 8)
                    transposes(h64, H)
                elif stage[0] == "grouped":
                    grouped_pass(stage[1])
                    if stage[1] == 0:
                        transposes(h64, H)
                        products(hT[0:H], w3[:, :], H, 8)
                        transposes(h64, H)
                        products(hT[0:H], w4[:, :], 3, 25)
                elif stage[0] == "build":
                    build(0)
                elif stage[0] == "offsets":
                    transposes(hs, D)
                    build(1)

        @block.scalar
        def _(act):
            n_ax = [0]

            def unary(pairs):
                n_ax[0] += 1
                act.wait_ge(ax_ready, n_ax[0])
                for out_, in_, f in pairs:
                    ins = nc.scalar.activation(out_, in_, f)
                ins.then_inc(ax_done, 1)

            def root(n):
                act.wait_ge(var_ready, n)
                nc.scalar.activation(st[:, 1, :], st[:, 0, :], ACT.Sqrt).then_inc(std_ready, 1)

            def set_rows(stage):
                if stage[0] == "pass":
                    rows = [src_i]
                else:
                    rows = [row2[:, 0, :], row2[:, 1, :]]
                with act.Fori(0, turns_of[stage]) as i:
                    for b in range(2):
                        gate(act, "act", raw_free, raw0[stage] + 2 * i + b + 1)
                        for g, r in enumerate(rows):
                            cp = nc.scalar.copy(slots[:, b, g, :], r[:, bass.ds(U * i + b * B, B)])
                        cp.then_inc(rows_ready, 1)

            def copy_sums(k):
                act.wait_ge(sum_done, k + 1)
                nc.scalar.copy(accS[:, 1536:N], PS[0:M, 1536:N]).then_inc(sum_copied, 1)

            def offset_rows(i, q):
                gate(act, "act", raw_free, raw0[("offsets", 1)] + i + q + 1)
                nc.scalar.copy(slots[:, q % 2, 0, :],
                               row2[:, 0, bass.ds(B * i + B * q, B)]).then_inc(rows_ready, 1)

            def hot_back(i, q):
                act.wait_ge(hot_turned, i + q + 1)
                c = (2 + 4 * (q % 2)) * BANK
                nc.scalar.copy(hotT[:, q % 2], PS[0:NP, c:c + BANK]).then_inc(hot_copied, 1)

            def build(n):
                width = (H, D)[n]
                if n == 1:
                    offset_rows(0, 0)
                with act.Fori(0, NJ) as j:
                    for plane in range(1, KS):
                        if n == 1:
                            hot_back(SIDE * j, plane - 1)
                            offset_rows(SIDE * j, plane)
                        act.wait_ge(z_mm, KS * (NJ * n + j) + plane + 2)
                        act.wait_ge(z_dve, CELLS * (NJ * n + j) + plane + 1)
                        for d2 in range(2):
                            cp = nc.scalar.copy(*corner(plane, plane - 1, 1, d2, width))
                        cp.then_inc(z_act, 1)
                if n == 1:
                    for q in range(SIDE * NJ, 2 * GTURNS):
                        hot_back(0, q)
                        if q + 1 < 2 * GTURNS:
                            offset_rows(0, q + 1)

            act.sem_inc(z_act, 1)
            act.wait_ge(pay_ready, 1)

            def hand_edges(i, first):
                for b in range(2):
                    if not first:
                        gate(act, "act", scattered[b], 16 * B * i)
                    at = bass.ds(U * i + b * B, B)
                    nc.scalar.copy(pslot[:, b], pay0[:, at, :])
                    nc.scalar.copy(slots[:, b, 0, :], pos_i[:, at]).then_inc(pslot_ready, 1)

            hand_edges(0, True)
            with act.Fori(1, TURNS) as i:
                hand_edges(i, False)
            for b in range(2):
                act.wait_ge(scattered[b], 16 * B * TURNS)
            act.wait_ge(edges_ready, 1)
            root(1)
            unary([(st[:, 7:9, :], st[:, 5:7, :], ACT.Sqrt)])
            for stage in STAGES:
                if stage[0] == "adj":
                    with act.Fori(0, NJ) as j:
                        act.wait_ge(a_sum, j + 1)
                        act.wait_ge(a_stored, 32 * j + 32)
                        nc.scalar.copy(accA[:, 3 * BANK:N], PS[0:NP, 3 * BANK:N]).then_inc(a_copied, 1)
                elif stage[0] == "dense":
                    k = stage[1]
                    act.wait_ge(dense_in, k + 1)
                    with act.Fori(0, NJ // RING) as i:
                        gate(act, "act", a_used, k * NJ + RING * i + RING)
                        nc.scalar.copy(lcur[:], cur[:, bass.ds(RING * i, RING), :]).then_inc(lcur_ready, 1)
                    act.wait_ge(dense_done, k + 1)
                    for m, c, w in DPARTS[4:]:
                        cp = nc.scalar.copy(acc[0:D, c:c + w], PS[D * (m % 4):D * (m % 4) + D, BANK:BANK + w])
                    cp.then_inc(sum_copied, 1)
                    if k == 0:
                        root(2)
                    if k == ROUNDS - 1:
                        root(3)
                elif stage[0] == "pass":
                    k = stage[1]
                    set_rows(stage)
                    copy_sums(k)
                    unary([(g3[:, :, 0, :], g3[:, :, 0, :], ACT.Sigmoid), (g3[:, :, 1, :], g3[:, :, 1, :], ACT.Tanh)])
                    unary([(g3[:, :, 2, :], g3[:, :, 2, :], ACT.Sigmoid), (tmpA[:, :, 0:D], tmpB[:, :, 0:D], ACT.Tanh)])
                    if k == PASSES - 1:
                        root(4)
                elif stage[0] == "build":
                    build(0)
                elif stage[0] == "offsets":
                    act.wait_ge(edges_ready, 3)
                    build(1)
                else:
                    if stage[0] != "hats":
                        act.wait_ge(edges_ready, {("grouped", 0): 2, ("grouped", 1): 4}[stage])
                        set_rows(stage)
                    if stage == ("hats", 0):
                        unary([(tmpB, tmpA, ACT.Exp)])
                    if stage == ("grouped", 0):
                        unary([(tmpB, tmpA, ACT.Exp)])
                        unary([(tmpB, tmpA, ACT.Exp)])

        @block.vector
        def _(dve):
            V = nc.vector
            chain = [0]

            def link(ins):
                chain[0] += 1
                ins.then_inc(dve_chain, 1)
                dve.wait_ge(dve_chain, chain[0])

            def signal(s):
                dve.sem_inc(s, 1)

            TT = lambda o, a, b_, op: link(V.tensor_tensor(o, a, b_, op))
            TS = lambda o, a, s1, op0, s2=None, op1=None: link(
                V.tensor_scalar(o, a, s1, s2, op0, op1) if op1 is not None else V.tensor_scalar(o, a, s1, None, op0))
            CP = lambda o, a: link(V.tensor_copy(o, a))

            dve.sem_inc(dve_loop, 1)
            dve.sem_inc(hat_done, 2)
            dve.sem_inc(gmsg_done, 2)
            dve.sem_inc(z_dve, 1)
            dve.sem_inc(raw_free, 2)
            dve.wait_ge(prep_mem, 4)
            for q in range(SPLITS):
                CP(fold[D * q:D * q + D, 0:D], ident[D * q:D * q + D, D * q:D * q + D])
            CP(fold[M - 1:M, D:D + 1], ident[M - 1:M, M - 1:M])
            dve.wait_ge(loaded, 16 * 14)

            eA = arena[:, 0:T]
            eB = arena[:, T:2 * T]
            eI = arena[:, 2 * T:3 * T].bitcast(I32)
            def quotient(q, rem, ids):
                TS(eB, ids, 1.0 / NJ, ALU.mult, 0.5 / NJ - 0.5, ALU.add)
                CP(eI, eB)
                CP(q, eI)
                link(V.scalar_tensor_tensor(rem, q, -float(NJ), ids, ALU.mult, ALU.add))
                TS(eB, rem, 0.0, ALU.is_lt)
                TT(q, q, eB, ALU.subtract)
                link(V.scalar_tensor_tensor(rem, q, -float(NJ), ids, ALU.mult, ALU.add))
                TS(eB, rem, float(NJ), ALU.is_ge)
                TT(q, q, eB, ALU.add)
                link(V.scalar_tensor_tensor(rem, q, -float(NJ), ids, ALU.mult, ALU.add))

            CP(eA, dst_i[:])
            TS(dst_c[:], eA, -float(MID), ALU.add)
            quotient(dst_q[:], dst_r[:], eA)
            TS(pay0[:, :, 2], eA, 0.0, ALU.max)
            CP(eA, src_i[:])
            src_q, src_r, pad = (arena[:, n * T:(n + 1) * T] for n in (3, 4, 5))
            quotient(src_q, src_r, eA)
            TS(pad, eA, 0.0, ALU.is_lt)
            TS(pay0[:, :, 1], eA, 0.0, ALU.max)
            CP(src_i[:], pay0[:, :, 1])
            CP(pay0[:, :, 0], src_q)
            CP(pay0[:, :, 3:6], attr0)
            link(V.memset(pay0[:, :, 6:9], 0.0))
            signal(edges_ready)

            TS(eA, pad, 100.0, ALU.mult)
            TT(src_r, src_r, eA, ALU.add)
            og = hot_g.rearrange("p (r t) -> p r t", r=NJ)
            TT(og, src_r.unsqueeze(1).broadcast_to([P, NJ, T]), iota_q[:, 0:NJ].unsqueeze(2).broadcast_to([P, NJ, T]),
               ALU.is_equal)
            link(V.tensor_tensor_scan(run_g, hot_g, hot_g, 0.0, ALU.add, ALU.max))
            rg = run_g.rearrange("p (r t) -> p r t", r=NJ)
            cnt, before, low, tiles, start = (st128[:, n, :] for n in range(5))
            link(V.memset(before[:, 0:1], 0.0))
            CP(before[:, 1:NJ], rg[:, 0:NJ - 1, T - 1])
            TT(cnt, rg[:, :, T - 1], before, ALU.subtract)
            signal(rank_in)
            dve.wait_ge(rank_mm, 1)
            CP(tiles, PS[:, 6 * BANK:6 * BANK + NJ])
            CP(low, PS[:, 6 * BANK + 64:6 * BANK + 64 + NJ])
            TS(tiles, tiles, float(P - 1), ALU.add)
            tiles_i = st128[:, 5, :].bitcast(I32)
            CP(tiles_i, tiles)
            TS(tiles_i, tiles_i, 7, ALU.arith_shift_right)
            CP(tiles, tiles_i)
            TS(tiles, tiles, 1.0, ALU.max)
            link(V.tensor_tensor_scan(start, tiles, tiles, 0.0, ALU.add, ALU.max))
            TT(start, start, tiles, ALU.subtract)
            TT(low, low, before, ALU.subtract)
            TS(low, low, -1.0, ALU.add)
            link(V.scalar_tensor_tensor(low, start, float(P), low, ALU.mult, ALU.add))
            posf = eA
            link(V.memset(posf, 0.0))
            with dve.Fori(0, NJ) as r:
                rt = bass.ds(r * T, T)
                dve.wait_ge(dve_loop, 2 * r + 1)
                V.scalar_tensor_tensor(eB, run_g[:, rt], low[:, bass.ds(r, 1)], hot_g[:, rt], ALU.add,
                                       ALU.mult).then_inc(dve_loop, 1)
                dve.wait_ge(dve_loop, 2 * r + 2)
                V.tensor_tensor(posf, posf, eB, ALU.add).then_inc(dve_loop, 1)
            dve.wait_ge(dve_loop, 2 * NJ + 1)
            pi, lane = eB.bitcast(I32), arena[:, 3 * T:4 * T].bitcast(I32)
            CP(pi, posf)
            TS(lane, pi, P - 1, ALU.bitwise_and)
            TS(pi, pi, 7, ALU.arith_shift_right)
            CP(posf, pi)
            lanef = arena[:, 4 * T:5 * T]
            CP(lanef, lane)
            link(V.scalar_tensor_tensor(posf, lanef, float(G), posf, ALU.mult, ALU.add))
            TS(eB, iota_c[:, 0:T], float(P * G), ALU.add)
            TT(eB, eB, posf, ALU.subtract)
            TT(eB, eB, pad, ALU.mult)
            TT(posf, posf, eB, ALU.add)
            CP(pos_i[:], posf)
            signal(pay_ready)
            bo = wb[0:1, 0:NJ * G // 2].bitcast(BF16).rearrange("p (g r) -> p g r", r=NJ)
            TT(bo, iota_c[0:1, :].unsqueeze(2).broadcast_to([1, G, NJ]), start[0:1, :].unsqueeze(1).broadcast_to([1, G, NJ]),
               ALU.is_ge)
            link(V.tensor_reduce(arena[0:1, 0:G], bo, AX.X, ALU.add))
            TS(arena[0:1, 0:G], arena[0:1, 0:G], -1.0, ALU.add)
            CP(block_of[:], arena[0:1, 0:G])
            CP(first_of[:, 0:NJ], start[0:1, :])
            TT(start[0:1, NJ - 1:NJ], start[0:1, NJ - 1:NJ], tiles[0:1, NJ - 1:NJ], ALU.add)
            CP(first_of[:, NJ:NJ + 1], start[0:1, NJ - 1:NJ])
            signal(blocks_ready)

            link(V.memset(val[:, :, 0:1], 1.0))
            CP(val[:, :, 1], weight[:])
            TS(val[:, :, 2:3], val[:, :, 1:2], alphas[:, 2:3], ALU.mult, 0.0, ALU.max)

            qb = iota_q[:].unsqueeze(1).broadcast_to([P, B, NP])
            rb = iota_q[:, 0:NJ].unsqueeze(1).broadcast_to([P, B, NJ])
            with dve.Fori(0, TURNS) as i:
                for b in range(2):
                    at = bass.ds(U * i + b * B, B)
                    dve.wait_ge(qval_free, 2 * i + b + 1)
                    V.tensor_tensor(oneq[:, b], dst_q[:, at].unsqueeze(2).broadcast_to([P, B, NP]), qb, ALU.is_equal)
                    V.tensor_tensor(oner[:, b], dst_r[:, at].unsqueeze(2).broadcast_to([P, B, NJ]), rb,
                                    ALU.is_equal).then_inc(dve_loop, 1)
                    dve.wait_ge(dve_loop, 2 * NJ + 1 + 2 * i + b + 1)
                    V.tensor_tensor(qval[:, b], oner[:, b].unsqueeze(3).broadcast_to([P, B, NJ, 3]),
                                    val[:, at, :].unsqueeze(2).broadcast_to([P, B, NJ, 3]),
                                    ALU.mult).then_inc(qval_ready, 1)
            loop0 = [2 * NJ + 1 + 2 * TURNS]

            def layernorm(n):
                m, v = st[:, 2, :], st[:, 0, :]
                tA, tB = (hT[0:NP, n * NJ * D:(n + 1) * NJ * D].rearrange("p (j d) -> p j d", j=NJ) for n in range(2))
                link(V.tensor_reduce(m, xs[:], AX.X, ALU.add))
                TS(m, m, -1.0 / D, ALU.mult)
                TT(tA, xs[:], m.unsqueeze(2).broadcast_to([NP, NJ, D]), ALU.add)
                TT(tB, tA, tA, ALU.mult)
                link(V.tensor_reduce(v, tB, AX.X, ALU.add))
                TS(v, v, 1.0 / D, ALU.mult, EPS, ALU.add)
                signal(var_ready)
                dve.wait_ge(std_ready, n)
                link(V.reciprocal(m, st[:, 1, :]))
                TS(tA, tA, 0.0, ALU.max)
                TT(hs[:], tA, m.unsqueeze(2).broadcast_to([NP, NJ, D]), ALU.mult)

            def bcn(col, width=D):
                return col.unsqueeze(2).broadcast_to([NP, NJ, width])

            def adjacency():
                dve.sem_inc(a_copied, 2)
                signal(agg_copied)
                with dve.Fori(0, NJ) as j:
                    g0, g1 = nc.values_load_multi_w_load_instructions(
                        first_of[0:1, bass.ds(j, 2)], engines=(mybir.EngineType.DVE,), min_val=0, max_val=G)[1]
                    with dve.Fori(g0, g1) as g:
                        dve.wait_ge(ahot_used, g + 1)
                        V.tensor_scalar(srch2[:, bass.ds((g % 2) * P, NP)], iota_q[:], pay[:, bass.ds(g, 1), 0], None,
                                        ALU.is_equal)
                        V.tensor_scalar(oh2[:, bass.ds((g % 2) * 2 * OHW, N + 1)], iota16[:], dstg[:, bass.ds(g, 1)],
                                        None, ALU.is_equal).then_inc(ahot_ready, 1)
                    dve.wait_ge(a_sum, j + 1)
                    dve.wait_ge(a_stored, 32 * j + 32)
                    V.tensor_copy(accA[:, 0:3 * BANK], PS[0:NP, 0:3 * BANK]).then_inc(a_copied, 1)
                dve.wait_ge(a_stored, 32 * NJ + 32)

            def dense_round(k):
                link(V.memset(PS[:, 0:2 * BANK], 0.0))
                signal(agg_copied)
                signal(dense_in)
                dve.wait_ge(dense_done, k + 1)
                for m, c, w in DPARTS[:4]:
                    cp = V.tensor_copy(acc[0:D, c:c + w], PS[D * m:D * m + D, 0:w])
                cp.then_inc(sum_copied, 1)
                dve.wait_ge(fold_done, k + 1)
                CP(agg[:, 0:24, 0:D].rearrange("p (a j) d -> p a j d", a=2),
                   PS[0:NP, 0:2 * BANK].rearrange("p (a c) -> p a c", a=2)[:, :, 0:480]
                   .rearrange("p a (j d) -> p a j d", d=40)[:, :, :, 0:D])
                CP(agg[:, 24, 0:D], PS[0:NP, 2 * BANK:2 * BANK + D])

            DI, DW, DW2, RC, BI = 9, 10, 4, 11, 3

            def edge_pass(k):
                s = ("pass", k)
                t0 = k * T
                signal(agg_copied)
                steps = 3
                base = loop0[0]
                with dve.Fori(0, TURNS) as i:
                    for b in range(2):
                        at = bass.ds(U * i + b * B, B)
                        us = slice(b * B, b * B + B)
                        n = base + (2 * i + b) * steps
                        r0 = 2 + raw0[s] + 2 * i + b + 1
                        dve.wait_ge(gathered[b], landed0[s] + per_batch[s] * i + per_batch[s])
                        mb, rb_ = msg[:, b], res[:, b]
                        V.tensor_tensor(mb, rawf[:, us], val[:, at, 1:2].broadcast_to([P, B, D]),
                                        ALU.mult).then_inc(raw_free, 1)
                        dve.wait_ge(raw_free, r0)
                        dve.wait_ge(tile_done, t0 + U * i + b * B + B)
                        V.tensor_copy(parts[:, us, 0:D], mb).then_inc(dve_loop, 1)
                        dve.wait_ge(dve_loop, n + 1)
                        V.tensor_tensor(rb_, mb, parts[:, us, 0:D], ALU.subtract).then_inc(dve_loop, 1)
                        dve.wait_ge(dve_loop, n + 2)
                        V.tensor_copy(parts[:, us, D:2 * D], rb_).then_inc(dve_loop, 1)
                        dve.wait_ge(dve_loop, n + 3)
                        V.tensor_tensor(parts[:, us, 2 * D:3 * D], rb_, parts[:, us, D:2 * D],
                                        ALU.subtract).then_inc(parts_ready, 1)
                        for u in range(b * B, b * B + B):
                            dve.wait_ge(tile_done, t0 + U * i + u + 1 + U - NOH)
                            V.tensor_scalar(oh[:, u % NOH, 0:N + 1], iota16[:], dst_c[:, bass.ds(U * i + u, 1)], None,
                                            ALU.is_equal).then_inc(onehot_ready, 1)
                loop0[0] = base + 2 * TURNS * steps
                dve.wait_ge(sum_done, k + 1)
                V.tensor_copy(accS[:, 0:1536], PS[0:M, 0:1536]).then_inc(sum_copied, 1)
                dve.wait_ge(fold_done, ROUNDS + k + 1)
                CP(agg[:, 0:24, :].rearrange("p (a j) d -> p a j d", a=2),
                   PS[0:NP, 0:2 * BANK].rearrange("p (a c) -> p a c", a=2)[:, :, 0:480]
                   .rearrange("p a (j d) -> p a j d", d=40)[:, :, :, 0:D + 1])
                CP(agg[:, 24, :], PS[0:NP, 2 * BANK:2 * BANK + D + 1])

            n_tr, n_mm, n_ax = [0], [0], [0]

            def transposed(width):
                signal(tr_ready)
                n_tr[0] += 1
                dve.wait_ge(tr_done, n_tr[0])
                CP(hT[0:width, 0:24 * NP].rearrange("c (a n) -> c a n", a=6),
                   PS[0:width, 0:6 * BANK].rearrange("c (a n) -> c a n", a=6)[:, :, 0:4 * NP])
                CP(hT[0:width, 24 * NP:25 * NP], PS[0:width, 6 * BANK:6 * BANK + NP])

            def product(to, cout, per_bank, bias):
                signal(mm_ready)
                n_mm[0] += 1
                dve.wait_ge(mm_done, n_mm[0])
                for a in range(0, NJ, per_bank):
                    n = min(per_bank, NJ - a)
                    c = BANK * (a // per_bank)
                    got = PS[0:NP, c:c + n * cout].rearrange("p (j d) -> p j d", d=cout)
                    if bias is None:
                        CP(to[:, a:a + n, :], got)
                    else:
                        TT(to[:, a:a + n, :], got, bias.unsqueeze(1).broadcast_to([NP, n, cout]), ALU.add)

            def bias_of(b_):
                return b_[:].unsqueeze(1).broadcast_to([NP, NJ, H])

            def asked():
                signal(ax_ready)
                n_ax[0] += 1
                dve.wait_ge(ax_done, n_ax[0])

            def elu(v):
                TS(tmpA, v, 0.0, ALU.min)
                asked()
                TS(v, v, 0.0, ALU.max, -1.0, ALU.add)
                TT(v, v, tmpB, ALU.add)

            def knots(ps):
                pos = arena[:, 0:3 * G].rearrange("p (t c) -> p t c", c=3)
                i0 = arena[:, 3 * G:6 * G].rearrange("p (t c) -> p t c", c=3)
                one = arena[:, 6 * G:9 * G].rearrange("p (t c) -> p t c", c=3)
                TS(pos, ps, float(KS - 1), ALU.mult)
                TS(i0, pos, 1.0, ALU.is_ge)
                for step in range(2, CELLS):
                    link(V.scalar_tensor_tensor(i0, pos, float(step), i0, ALU.is_ge, ALU.add))
                TT(pos, pos, i0, ALU.subtract)
                TS(one, pos, -1.0, ALU.mult, 1.0, ALU.add)
                return pos, i0, one

            def spline_basis(ps):
                pos, i0, one = knots(ps)
                q12 = arena[:, 9 * G:13 * G].rearrange("p (t q) -> p t q", q=4)
                rowf = arena[:, 13 * G:14 * G]
                side = (one, pos)
                for q in range(4):
                    TT(q12[:, :, q], side[q // 2][:, :, 0], side[q % 2][:, :, 1], ALU.mult)
                for g in range(2):
                    TT(basis[:, :, 4 * g:4 * g + 4], q12, side[g][:, :, 2:3].broadcast_to([P, G, 4]), ALU.mult)
                link(V.scalar_tensor_tensor(rowf, i0[:, :, 0], float(CELLS), i0[:, :, 1], ALU.mult, ALU.add))
                link(V.scalar_tensor_tensor(rowf, rowf, float(KS), i0[:, :, 2], ALU.mult, ALU.add))
                link(V.scalar_tensor_tensor(rowf, pay[:, :, 2], float(NODE_ROWS), rowf, ALU.mult, ALU.add))
                CP(row2[:, 0, :], rowf)
                TS(rowf, rowf, 1.0, ALU.add)
                CP(row2[:, 1, :], rowf)

            def hat_messages():
                pos, i0, one = knots(pay[:, :, 3:6])
                kk = iota_q[:, 0:KS].unsqueeze(1).broadcast_to([P, G, KS])
                tk = hT[:, 0:G * KS].rearrange("p (g k) -> p g k", k=KS)
                for c in range(3):
                    h = hats[:, c]
                    TT(tk, kk, i0[:, :, c:c + 1].broadcast_to([P, G, KS]), ALU.is_equal)
                    TT(h, tk, one[:, :, c:c + 1].broadcast_to([P, G, KS]), ALU.mult)
                    TS(i0[:, :, c:c + 1], i0[:, :, c:c + 1], 1.0, ALU.add)
                    TT(tk, kk, i0[:, :, c:c + 1].broadcast_to([P, G, KS]), ALU.is_equal)
                    TT(tk, tk, pos[:, :, c:c + 1].broadcast_to([P, G, KS]), ALU.mult)
                    TT(h, h, tk, ALU.add)
                link(V.memset(hat123[:, :, :, KS ** 3:KP1], 1.0))
                signal(agg_copied)
                base = loop0[0]
                with dve.Fori(0, GTURNS) as i:
                    for b in range(2):
                        at = bass.ds(U * i + b * B, B)
                        dve.wait_ge(hat_done, 2 * i + b + 1)
                        V.tensor_tensor(hatq[:, b], pay[:, at, 0:1].broadcast_to([P, B, NP]),
                                        iota_q[:].unsqueeze(1).broadcast_to([P, B, NP]), ALU.is_equal)
                        V.tensor_tensor(hat12[:, b].rearrange("p u (k l) -> p u k l", k=KS),
                                        hats[:, 0, at, :].unsqueeze(3).broadcast_to([P, B, KS, KS]),
                                        hats[:, 1, at, :].unsqueeze(2).broadcast_to([P, B, KS, KS]),
                                        ALU.mult).then_inc(dve_loop, 1)
                        dve.wait_ge(dve_loop, base + 2 * i + b + 1)
                        V.tensor_tensor(hat123[:, b, :, 0:KS ** 3].rearrange("p u (k l) -> p u k l", l=KS),
                                        hat12[:, b].unsqueeze(3).broadcast_to([P, B, KS * KS, KS]),
                                        hats[:, 2, at, :].unsqueeze(2).broadcast_to([P, B, KS * KS, KS]),
                                        ALU.mult).then_inc(hat_ready, 1)
                loop0[0] = base + 2 * GTURNS
                dve.wait_ge(hat_sum, 1)
                CP(hsum[:, 0:24, :].rearrange("p (a j) d -> p a j d", a=6),
                   PS[0:NP, 0:6 * BANK].rearrange("p (a j d) -> p a j d", a=6, j=4)[:, :, :, 0:KP1])
                CP(hsum[:, 24, :], PS[0:NP, 6 * BANK:6 * BANK + KP1])

            def grouped_pass(n):
                width = (H, D)[n]
                s = ("grouped", n)
                signal(agg_copied)
                base = loop0[0]
                with dve.Fori(0, GTURNS) as i:
                    for b in range(2):
                        at = bass.ds(U * i + b * B, B)
                        us = slice(b * B, b * B + B)
                        dve.wait_ge(gmsg_done, 2 * (GTURNS * n + i) + b + 1)
                        V.tensor_tensor(grq[:, b], pay[:, at, 0:1].broadcast_to([P, B, NP]),
                                        iota_q[:].unsqueeze(1).broadcast_to([P, B, NP]), ALU.is_equal)
                        dve.wait_ge(gathered[b], landed0[s] + per_batch[s] * i + per_batch[s])
                        rr = raw[:, us, 0:8 * width].rearrange("p u (c f) -> p u c f", f=width)
                        V.tensor_tensor(rr, rr, basis[:, at, :].unsqueeze(3).broadcast_to([P, B, 8, width]),
                                        ALU.mult).then_inc(dve_loop, 1)
                        dve.wait_ge(dve_loop, base + 2 * i + b + 1)
                        V.tensor_reduce(gmsg[:, b, :, 0:width],
                                        raw[:, us, 0:8 * width].rearrange("p u (c f) -> p u f c", f=width), AX.X,
                                        ALU.add).then_inc(raw_free, 1)
                        dve.wait_ge(raw_free, 2 + raw0[s] + 2 * i + b + 1)
                        dve.sem_inc(gmsg_ready, 1)
                loop0[0] = base + 2 * GTURNS
                dve.wait_ge(gsum_done, n + 1)

            def source_onehots(i, q):
                V.tensor_tensor(grq[:, q % 2], pay[:, bass.ds(B * i + B * q, B), 0:1].broadcast_to([P, B, NP]),
                                iota_q[:].unsqueeze(1).broadcast_to([P, B, NP]), ALU.is_equal).then_inc(hot_ready, 1)

            def offsets(i, q):
                s = ("offsets", 1)
                b = q % 2
                us = slice(b * B, b * B + B)
                dve.wait_ge(tsrc_ready, i + q + 1)
                dve.wait_ge(gathered[b], landed0[s] + per_batch[s] // 2 * i + per_batch[s] * (q // 2 + 1))
                c = (3 + 4 * b) * BANK
                V.tensor_tensor(pay[:, bass.ds(B * i + B * q, B), 6:9], rawt[:, us, 0:3],
                                PS[:, c:c + 4 * B].rearrange("p (u c) -> p u c", c=4)[:, :, 0:3],
                                ALU.subtract).then_inc(raw_free, 1)

            def build(n):
                width = (H, D)[n]
                if n == 1:
                    source_onehots(0, 0)
                with dve.Fori(0, NJ) as j:
                    gate(dve, "dve", z_mm, KS * (NJ * n + j) + 1)
                    V.tensor_copy(hcur[0:width, :], hT[0:width, bass.ds(NP * j, NP)]).then_inc(z_in, 1)
                    for c1 in range(CELLS):
                        dve.wait_ge(z_mm, KS * (NJ * n + j) + c1 + 2)
                        if c1 >= 1:
                            dve.wait_ge(z_act, CELLS * (NJ * n + j) + c1 + 1)
                        dve.wait_ge(z_stored[c1 % 2], 32 * (2 * (NJ * n + j) + c1 // 2) + 32)
                        for d2 in range(2):
                            cp = V.tensor_copy(*corner(c1, c1, 0, d2, width))
                        cp.then_inc(z_dve, 1)
                        if n == 1:
                            source_onehots(SIDE * j, c1 + 1)
                            offsets(SIDE * j, c1)
                if n == 1:
                    for q in range(SIDE * NJ, 2 * GTURNS):
                        if q + 1 < 2 * GTURNS:
                            source_onehots(0, q + 1)
                        offsets(0, q)
                for h in range(2):
                    dve.wait_ge(z_stored[h], 32 + 32 * 2 * NJ * (n + 1))

            dve.wait_ge(scal_ready, 1)
            CP(scal[:], PS[0:NP, 7 * BANK:7 * BANK + NJ * 3].rearrange("p (j v) -> p j v", v=3))
            layernorm(1)
            dve.wait_ge(loaded_w, 16 * (LAYERS * 3 + 11))
            TS(st[:, 5, :], scal[:, :, 0], 1.0, ALU.max)
            TS(scal[:, :, 1], scal[:, :, 1], 1.0, ALU.add)
            TS(st[:, 6, :], scal[:, :, 1], 1e-30, ALU.max)
            asked()
            link(V.reciprocal(st[:, DI:DI + 2, :], st[:, 7:9, :]))
            for c, row in ((0, DI), (1, DW)):
                TS(st[:, 0, :], scal[:, :, c], 0.0, ALU.is_gt)
                TT(st[:, row, :], st[:, row, :], st[:, 0, :], ALU.mult)
            TT(st[:, DW2, :], st[:, DW, :], st[:, DW, :], ALU.mult)
            TS(st[:, BI, :], scal[:, :, 2], alphas[0:NP, 1:2], ALU.mult)
            TS(st[:, 0, :], nvec[:], alphas[0:NP, 3:4], ALU.mult)
            TT(st[:, BI, :], st[:, BI, :], st[:, 0, :], ALU.add)
            for g, (m, own) in enumerate(((0, 0), (4, 2), (6, 3))):
                TT(gate_b[:, :, g, :], cb[:, :, m, :], cb[:, :, m + 1, :], ALU.add)
                TT(gate_b[:, :, g, :], gate_b[:, :, g, :], gbg[:, :, own, :], ALU.add)

            dve.wait_ge(pay_loaded, 16)
            TS(dstg[:], pay[:, :, 2], -float(MID), ALU.add)
            adjacency()

            TT(cur[:], hs[:], bcn(st[:, DI, :]), ALU.mult)
            dense_round(0)
            TT(cur[:], agg[:, :, 0:D], bcn(st[:, DI, :]), ALU.mult)
            TT(xs[:], xs[:], cur[:], ALU.add)

            layernorm(2)
            CP(cur[:], hs[:])
            for r in range(ITERS):
                dense_round(1 + r)
                TS(cur[:], agg[:, :, 0:D], alphas[0:NP, 0:1], ALU.mult)
                TT(cur[:], cur[:], bcn(st[:, BI, :]), ALU.add)
                TS(cur[:], cur[:], 0.0, ALU.max)
            TT(xs[:], xs[:], cur[:], ALU.add)

            layernorm(3)
            CP(cur[:], hs[:])
            for l in range(LAYERS):
                TT(cur[:], cur[:], bcn(st[:, DW, :]), ALU.mult)
                signal(table_built)
                edge_pass(l)
                TT(cur[:], cur[:], agg[:, :, 0:D], ALU.add)
                TT(agg[:, :, 0:D], cur[:], bcn(st[:, DW, :]), ALU.mult)
                transposed(D)
                product(gates, 3 * D, 5, gate_b[:, l].rearrange("p g d -> p (g d)"))
                asked()
                TT(cur[:], g3[:, :, 0, :], g3[:, :, 1, :], ALU.mult)
                TT(tmpB[:, :, 0:D], cur[:], gwc[:, l, 2:3, :].broadcast_to([NP, NJ, D]), ALU.mult)
                TT(g3[:, :, 2, :], g3[:, :, 2, :], tmpB[:, :, 0:D], ALU.add)
                CP(tmpB[:, :, 0:D], cur[:])
                asked()
                TT(cur[:], g3[:, :, 2, :], tmpA[:, :, 0:D], ALU.mult)
            TT(xs[:], xs[:], cur[:], ALU.add)
            layernorm(4)

            hat_messages()
            TS(st[:, RC, :], hsum[:, :, KS ** 3], 1.0, ALU.max)
            link(V.reciprocal(st[:, RC, :], st[:, RC, :]))
            transposed(KS ** 3)
            product(h64, H, 8, None)
            TT(h64[:], h64[:], bcn(st[:, RC, :], H), ALU.mult)
            TT(h64[:], h64[:], bias_of(b1), ALU.add)
            elu(h64[:])
            transposed(H)
            build(0)
            spline_basis(pay[:, :, 3:6])
            signal(edges_ready)
            grouped_pass(0)
            TT(h64[:], PS[0:NP, 0:NJ * H].rearrange("p (j f) -> p j f", f=H), bcn(st[:, RC, :], H), ALU.mult)
            TT(h64[:], h64[:], bias_of(b2), ALU.add)
            elu(h64[:])
            transposed(H)
            product(h64, H, 8, b3[:])
            elu(h64[:])
            transposed(H)
            product(t4[:, :, 0:3], 3, 25, b4[:])
            link(V.memset(t4[:, :, 3:4], 0.0))
            signal(table_built)

            CP(row2[:, 0, :], pay[:, :, 2])
            signal(edges_ready)
            transposed(D)
            build(1)
            dve.wait_ge(raw_free, 2 + raw0[("offsets", 1)] + 2 * GTURNS)
            TT(pay[:, :, 3:6], pay[:, :, 3:6], pay[:, :, 6:9], ALU.add)
            TS(pay[:, :, 3:6], pay[:, :, 3:6], 0.0, ALU.max, 1.0, ALU.min)
            spline_basis(pay[:, :, 3:6])
            signal(edges_ready)
            grouped_pass(1)
            TT(cur[:], PS[0:NP, 0:NJ * D].rearrange("p (j f) -> p j f", f=D), bcn(st[:, RC, :]), ALU.mult)
            TT(cur[:], cur[:], bc[:].unsqueeze(1).broadcast_to([NP, NJ, D]), ALU.add)
            TT(xs[:], xs[:], cur[:], ALU.add)
            signal(out_ready)


_INS = ["x", "src", "dst", "edge_attr_3", "edge_weight", "node_vec", "L1_gnn_alpha1", "L1_gnn_alpha2",
        "L1_gnn_alpha3", "L1_gnn_alpha4", "L2_gnn_conv_w", "L2_gnn_conv_b", "L2_gnn_wc", "L2_gnn_bg",
        "L3_gnn_stn1_w", "L3_gnn_stn1_b", "L3_gnn_stn2_w", "L3_gnn_stn2_b", "L3_gnn_stn3_w",
        "L3_gnn_stn3_b", "L3_gnn_stn4_w", "L3_gnn_stn4_b", "L3_gnn_conv_w", "L3_gnn_conv_b"]


def kernel(**inputs):
    import concourse.bacc as bacc
    from concourse.bass_utils import run_bass_kernel_spmd

    nc = bacc.Bacc("TRN2", target_bir_lowering=False, num_devices=1)
    arrays, args = {}, []
    for name in _INS:
        a = np.ascontiguousarray(inputs[name])
        arrays[f"in_{name}"] = a
        args.append(nc.dram_tensor(f"in_{name}", a.shape, mybir.dt.from_np(a.dtype), kind="ExternalInput").ap())
    out = nc.dram_tensor("out_x", inputs["x"].shape, F32, kind="ExternalOutput").ap()
    gnn_kernel(nc, *args, out)
    r = run_bass_kernel_spmd(nc, [arrays], core_ids=[0])
    return r.results[0]["out_x"]
```

```python
from contextlib import ExitStack

import numpy as np

import concourse.bass as bass
from concourse import mybir

ALU = mybir.AluOpType
ACT = mybir.ActivationFunctionType
AX = mybir.AxisListType
F32 = mybir.dt.float32
F16 = mybir.dt.float16
BF16 = mybir.dt.bfloat16
I32 = mybir.dt.int32

P = 128
D = 32
EPS = 1e-5
ITERS = 4
KS = 5
CELLS = KS - 1
K3 = (KS, CELLS)
ROW_CORNERS = (4, 8)


def gnn_kernel(nc, x, src, dst, edge_attr, edge_weight, node_vec, alpha1, alpha2, alpha3, alpha4,
               conv_w, conv_b, wc, bg, stn1_w, stn1_b, stn2_w, stn2_b, stn3_w, stn3_b, stn4_w,
               stn4_b, sconv_w, sconv_b, out):
    N = x.shape[0]
    E = src.shape[0]
    LAYERS = conv_w.shape[0]
    H = stn2_w.shape[1]
    NP = 125
    NJ = N // NP
    assert NP * NJ == N and H == 2 * D
    U = 8
    B = U // 2
    TURNS = -(-E // (P * U))
    T = TURNS * U
    TAIL = E - (P - 1) * T
    MID = N // 2
    BANK = 512
    CHUNKS = [(c, min(BANK, N - c)) for c in range(0, N, BANK)]
    G = -(-(E + P * NJ) // (P * U)) * U
    GTURNS = G // U
    PD = 3
    PC = 9
    NOH = 4
    ZT = [CELLS * K3[n] * ROW_CORNERS[n] * c for n, c in enumerate((H, D))]
    ZS = max(ZT)
    ZBANKS = 4
    KP1 = KS ** 3 + 1

    PASSES = LAYERS
    ROUNDS = 1 + ITERS
    RING = 5
    DB = 448
    DPARTS = [(n, c, min(DB, N - c)) for n, c in enumerate(range(0, N, DB))]
    SIDE = RING - 1
    SLOTS = NJ // RING * SIDE
    assert SIDE == CELLS and SIDE % 2 == 0 and 2 * GTURNS >= 2 + ROUNDS * SLOTS and GTURNS * 2 >= NJ * SIDE
    GSUM0 = 4

    ctx = ExitStack()
    with ctx:
        def sb(name, shape, dt=F32):
            return ctx.enter_context(nc.sbuf_tensor(name, shape, dt))

        def sem(name):
            return ctx.enter_context(nc.semaphore(name))

        tab_feat = nc.dram_tensor("tab_feat", (N, D), F32).ap()
        tab_t = nc.dram_tensor("tab_t", (N, 4), F32).ap()
        tab_z = [nc.dram_tensor(f"tab_z_{n}", (N * CELLS * CELLS * K3[n], ROW_CORNERS[n] * c), F32).ap()
                 for n, c in enumerate((H, D))]
        adj = nc.dram_tensor("adj", (NJ, NP, N), F32).ap()
        rows_by_dst = nc.dram_tensor("rows_by_dst", (P * G + T, PD), F32).ap()
        rows_dram = nc.dram_tensor("rows_dram", (P * G + T, PC), F32).ap()

        PS = ctx.enter_context(nc.psum_tensor("PS", [P, 8 * BANK], F32))

        src_i, dst_i = sb("src_i", [P, T], I32), sb("dst_i", [P, T], I32)
        pos_by_dst = sb("pos_by_dst", [P, T], I32)
        weight = sb("weight", [P, T])
        val = sb("val", [P, T, 3])
        dst_q, dst_r = sb("dst_q", [P, T]), sb("dst_r", [P, T])
        pay = sb("pay", [P, G, PC])
        basis = sb("basis", [P, G, 8])
        payd = basis[:].rearrange("p g c -> p (g c)")[:, 0:G * PD].rearrange("p (g c) -> p g c", c=PD)
        row2 = sb("row2", [P, 2, G], I32)
        dstg = sb("dstg", [P, G])
        block_of = sb("block_of", [1, G], I32)
        block_by_dst = sb("block_by_dst", [1, G], I32)
        first_of = sb("first_of", [1, NJ + 1], I32)
        iota16 = sb("iota16", [P, N + 1], F16)
        iota_q = sb("iota_q", [P, NP])
        iota_c = sb("iota_c", [P, G])
        ident = sb("ident", [P, P])
        upper = sb("upper", [P, P])
        ones_f = sb("ones_f", [P, P])
        zeros_l = sb("zeros_l", [P, P], BF16)
        zeros_f = sb("zeros_f", [P, P])
        alphas = sb("alphas", [P, 4])
        arena = sb("arena", [P, max(2 * ZS, U * 8 * H + 2 * N)])
        wb = sb("wb", [P, KS ** 3 * H])
        hT = sb("hT", [P, NJ * NP])
        OHW = (N + 2) // 2
        ahot = arena[:, 0:NOH * OHW].bitcast(BF16)
        asrc = arena[:, NOH * OHW:NOH * (OHW + P // 2)].bitcast(BF16)
        rawf = arena[:, 0:U * D].rearrange("p (u r) -> p u r", u=U)
        raw = arena[:, 0:U * 8 * H].rearrange("p (u r) -> p u r", u=U)
        grq = wb[:, 2 * N:2 * N + 2 * B * NP].rearrange("p (b u q) -> p b u q", b=2, u=B)
        gmsg = wb[:, 2 * N + 2 * B * NP:2 * N + 2 * B * (NP + H)].rearrange("p (b u f) -> p b u f", b=2, u=B)
        rawt = arena[:, ZT[1]:ZT[1] + U * 4].rearrange("p (u r) -> p u r", u=U)
        hotT = arena[0:NP, ZS + ZT[1]:ZS + ZT[1] + 2 * BANK].rearrange("p (b n) -> p b n", b=2)
        assert ZT[1] + 2 * BANK <= ZS
        hats = arena[:, 9 * G:24 * G].rearrange("p (c g k) -> p c g k", c=3, k=KS)
        HB0 = 0
        hat12 = arena[:, HB0:HB0 + 2 * B * KS * KS].rearrange("p (b u k) -> p b u k", b=2, u=B)
        HC0 = HB0 + 2 * B * KS * KS
        hat123 = arena[:, HC0:HC0 + 2 * B * KP1].rearrange("p (b u k) -> p b u k", b=2, u=B)
        HQ0 = HC0 + 2 * B * KP1
        hatq = arena[:, HQ0:HQ0 + 2 * B * NP].rearrange("p (b u q) -> p b u q", b=2, u=B)
        zs = arena[:, 0:2 * ZS].rearrange("p (h c) -> p h c", h=2)
        oneq = arena[:, 0:2 * B * NP].rearrange("p (b u q) -> p b u q", b=2, u=B)
        oner = arena[:, 1000:1000 + 2 * B * NJ].rearrange("p (b u r) -> p b u r", b=2, u=B)
        qval = arena[:, 1200:1200 + 2 * B * NJ * 3].rearrange("p (b u r v) -> p b u r v", b=2, u=B, v=3)
        pslot = sb("pslot", [P, 2, B, PC])
        slots = sb("slots", [P, 2, 2, B], I32)
        acc = sb("acc", [P, PC * T])
        accA = acc[0:NP, 0:N]
        pay0 = acc[:, 0:PC * T].rearrange("p (t c) -> p t c", c=PC)
        pos_i = sb("pos_i", [P, T], I32)
        xs, hs, cur = (sb(n, [NP, NJ, D]) for n in ("xs", "hs", "cur"))
        agg = sb("agg", [NP, NJ, D])
        lcur = sb("lcur", [NP, RING, D])
        h64 = sb("h64", [NP, NJ, H])
        hcur = sb("hcur", [H, NP])
        scal = sb("scal", [NP, NJ, 3])
        nvec = sb("nvec", [NP, NJ])
        st = sb("st", [NP, 12, NJ])
        t4 = sb("t4", [NP, NJ, 4])
        t4f = t4[:].rearrange("p j c -> p (j c)")
        wbuf = wb[0:H, :].rearrange("i (k o) -> i k o", o=H)
        hot_g = arena[:, 6 * T:6 * T + NJ * T // 2].bitcast(F16)
        run_g = wb[:, 0:NJ * T // 2].bitcast(F16)
        attr0 = wb[:, NJ * T // 2:NJ * T // 2 + 3 * T].rearrange("p (t c) -> p t c", c=3)
        ring = [arena[0:NP, U * 8 * H + n * N:U * 8 * H + (n + 1) * N] for n in range(2)] + \
            [wb[0:NP, n * N:(n + 1) * N] for n in range(2)] + [hT[0:NP, 0:N]]
        st128 = sb("st128", [P, 6, NJ])
        hsum = arena[0:NP, 0:NJ * KP1].rearrange("p (j k) -> p j k", k=KP1)
        gate_w = sb("gate_w", [D, LAYERS, 3, D])
        gate_b = sb("gate_b", [NP, LAYERS, 3, D])
        cb = sb("cb", [NP, LAYERS, 8, D])
        gbg = sb("gbg", [NP, LAYERS, 4, D])
        gwc = sb("gwc", [NP, LAYERS, 3, D])
        w1 = sb("w1", [KS ** 3, H])
        w3, w4 = sb("w3", [H, H]), sb("w4", [H, 3])
        b1, b2, b3 = sb("b1", [NP, H]), sb("b2", [NP, H]), sb("b3", [NP, H])
        b4, bc = sb("b4", [NP, 3]), sb("bc", [NP, D])

        def tmp(width, at):
            return arena[0:NP, at:at + NJ * width].rearrange("p (j d) -> p j d", j=NJ)

        tmpA, tmpB = tmp(H, 0), tmp(H, NJ * H)
        gates = tmp(3 * D, 2 * NJ * H)
        g3 = gates.rearrange("p j (g d) -> p j g d", g=3)

        prep_mem = sem("prep_mem")
        loaded = sem("loaded")
        loaded_w = sem("loaded_w")
        loaded_z = sem("loaded_z")
        holes_stored = sem("holes_stored")
        pay_ready = sem("pay_ready")
        rank_in, rank_mm = sem("rank_in"), sem("rank_mm")
        pslot_ready = sem("pslot_ready")
        byd_ready = sem("byd_ready")
        byd_copied = sem("byd_copied")
        scattered_byd = [sem(f"scattered_byd{b}") for b in range(2)]
        payd_loaded = sem("payd_loaded")
        scattered = [sem(f"scattered{b}") for b in range(2)]
        pay_loaded = sem("pay_loaded")
        blocks_ready = sem("blocks_ready")
        ahot_ready, ahot_used = sem("ahot_ready"), sem("ahot_used")
        a_sum = sem("a_sum")
        a_copied = sem("a_copied")
        a_stored = sem("a_stored")
        a_loaded = [sem(f"a_loaded{n}") for n in range(RING)]
        a_used = sem("a_used")
        dense_in = sem("dense_in")
        lcur_ready, dense_done = sem("lcur_ready"), sem("dense_done")
        hat_ready, hat_done = sem("hat_ready"), sem("hat_done")
        hat_sum = sem("hat_sum")
        gmsg_ready, gmsg_done = sem("gmsg_ready"), sem("gmsg_done")
        hot_ready = sem("hot_ready")
        hot_turned = sem("hot_turned")
        hot_copied = sem("hot_copied")
        tsrc_ready = sem("tsrc_ready")
        gsum_done = sem("gsum_done")
        dve_chain = sem("dve_chain")
        qval_ready = sem("qval_ready")
        qval_free = sem("qval_free")
        scal_ready = sem("scal_ready")
        var_ready, std_ready = sem("var_ready"), sem("std_ready")
        table_built, table_stored = sem("table_built"), sem("table_stored")
        rows_ready = sem("rows_ready")
        edges_ready = sem("edges_ready")
        gathered = [sem(f"gathered{b}") for b in range(2)]
        raw_free = sem("raw_free")
        dve_loop = sem("dve_loop")
        sum_done = sem("sum_done")
        sum_copied = sem("sum_copied")
        fold_done = sem("fold_done")
        agg_copied = sem("agg_copied")
        tr_ready, tr_done = sem("tr_ready"), sem("tr_done")
        mm_ready, mm_done = sem("mm_ready"), sem("mm_done")
        ax_ready, ax_done = sem("ax_ready"), sem("ax_done")
        z_in = sem("z_in")
        z_mm = sem("z_mm")
        z_dve, z_act = sem("z_dve"), sem("z_act")
        z_stored = [sem(f"z_stored{h}") for h in range(2)]
        t_stored = sem("t_stored")
        out_ready, out_stored = sem("out_ready"), sem("out_stored")
        gate_pass = {e: sem(f"gate_{e}") for e in ("pool", "act", "dve", "pe", "sp")}

        def gate(eng, name, s, value):
            eng.wait_ge(s, value)
            eng.sem_inc(gate_pass[name], 1)

        def node_rows(ap):
            return ap.rearrange("(p j) d -> p j d", p=NP)

        STAGES = [("adj", 0), ("hats", 0), ("build", 0)] + [("dense", k) for k in range(ROUNDS)] + [("grouped", 0)]
        STAGES += [("pass", k) for k in range(PASSES)] + [("offsets", 1), ("grouped", 1)]
        GATHERS = [s for s in STAGES if s[0] in ("pass", "offsets", "grouped")]
        turns_of = {s: GTURNS for s in GATHERS}
        order, landed0, raw0 = {}, {}, {}
        n_rows = n_landed = n_raw = 0
        per_batch = {s: 16 * B * (2 if s == ("grouped", 0) else 1) for s in GATHERS}
        for s in GATHERS:
            order[s], landed0[s], raw0[s] = n_rows, n_landed, n_raw
            n_rows += 2 * turns_of[s]
            n_landed += turns_of[s] * per_batch[s]
            n_raw += 2 * turns_of[s]

        def corners(n, plane, c1, d1):
            width = (H, D)[n]
            to = zs[0:NP, c1 % 2, 0:ZT[n]].rearrange("p (b q f) -> p b q f", q=ROW_CORNERS[n], f=width)
            c0 = (plane % 2) * ZBANKS * BANK
            points = PS[0:NP, c0:c0 + KS * KS * width]
            if n == 0:
                return [(to[:, :, 2 * d1 + d2, :], points[:, d2 * KS * width:(d2 + CELLS) * KS * width]
                         .rearrange("p (b f) -> p b f", f=width)) for d2 in range(2)]
            grid = points.rearrange("p (k l f) -> p k l f", k=KS, l=KS)
            return [(to[:, :, 4 * d3 + 2 * d1 + d2, :].rearrange("p (k l) f -> p k l f", l=CELLS),
                     grid[:, d2:d2 + CELLS, d3:d3 + CELLS, :]) for d2 in range(2) for d3 in range(2)]

        block = ctx.enter_context(nc.Block())

        @block.sync
        def _(sp):
            for h in range(2):
                sp.sem_inc(z_stored[h], 32)
            sp.sem_inc(a_stored, 32)
            sp.wait_ge(prep_mem, 2)
            FULL = (P - 1) * T
            for a, d in ((src, src_i), (dst, dst_i), (edge_weight, weight)):
                sp.dma_start(d[0:P - 1, :],
                             a[0:FULL].rearrange("(p t) -> p t", p=P - 1)).then_inc(loaded, 16)
                sp.dma_start(d[P - 1:P, 0:TAIL],
                             a[FULL:E].rearrange("(p t) -> p t", p=1)).then_inc(loaded, 16)
            sp.dma_start(attr0[0:P - 1, :, :],
                         edge_attr[0:FULL, :].rearrange("(p t) c -> p t c", p=P - 1)).then_inc(loaded, 16)
            sp.dma_start(attr0[P - 1:P, 0:TAIL, :],
                         edge_attr[FULL:E, :].rearrange("(p t) c -> p t c", p=1)).then_inc(loaded, 16)
            sp.dma_start(xs[:], node_rows(x)).then_inc(loaded, 16)
            sp.dma_start(nvec[:], node_vec.rearrange("(p j) -> p j", p=NP)).then_inc(loaded, 16)
            for i, a in enumerate((alpha1, alpha2, alpha3, alpha4)):
                sp.dma_start(alphas[:, i:i + 1], a.partition_broadcast(P)).then_inc(loaded, 16)
            grouped_dram = rows_dram[0:P * G, :].rearrange("(p g) c -> p (g c)", p=P)
            sp.dma_start(grouped_dram, pay[:].rearrange("p g c -> p (g c)")).then_inc(holes_stored, 16)
            sp.dma_start(rows_by_dst[0:P * G, :].rearrange("(p g) c -> p (g c)", p=P),
                         basis[:].rearrange("p g c -> p (g c)")[:, 0:G * PD]).then_inc(holes_stored, 16)
            for l in range(LAYERS):
                for g, m in enumerate((0, 4, 6)):
                    sp.dma_start(gate_w[:, l, g, :], conv_w[l, m]).then_inc(loaded_w, 16)
            sp.dma_start(cb[:], conv_b.partition_broadcast(NP)).then_inc(loaded_w, 16)
            sp.dma_start(gbg[:], bg.partition_broadcast(NP)).then_inc(loaded_w, 16)
            sp.dma_start(gwc[:], wc.partition_broadcast(NP)).then_inc(loaded_w, 16)
            for d, a in ((b1, stn1_b), (b2, stn2_b), (b3, stn3_b), (b4, stn4_b), (bc, sconv_b)):
                sp.dma_start(d[:], a.partition_broadcast(NP)).then_inc(loaded_w, 16)
            sp.dma_start(w1[:], stn1_w.rearrange("k one f -> k (one f)")).then_inc(loaded_w, 16)
            sp.dma_start(w3[:], stn3_w).then_inc(loaded_w, 16)
            sp.dma_start(w4[:], stn4_w).then_inc(loaded_w, 16)
            for b in range(2):
                sp.wait_ge(scattered[b], 16 * B * TURNS)
            sp.dma_start(pay[:].rearrange("p g c -> p (g c)"), grouped_dram).then_inc(pay_loaded, 16)
            sp.wait_ge(blocks_ready, 2)
            sp.dma_start(wbuf[:], stn2_w.rearrange("k i o -> i k o")).then_inc(loaded_z, 16)
            with sp.Fori(0, NJ) as j:
                sp.wait_ge(a_copied, 2 * j + 4)
                for p0, p1 in ((0, 112), (112, NP)):
                    sp.dma_start(adj[bass.ds(j, 1), p0:p1].squeeze(0), accA[p0:p1]).then_inc(a_stored, 16)

            def store_table(n):
                zt = tab_z[n].rearrange("(p j c r) f -> j c p (r f)", p=NP, j=NJ, c=CELLS)
                with sp.Fori(0, NJ) as j:
                    for c1 in range(CELLS):
                        sp.wait_ge(z_act, CELLS * (NJ * n + j) + c1 + 2)
                        for p0, p1 in ((0, 112), (112, NP)):
                            sp.dma_start(zt[bass.ds(j, 1), c1, p0:p1].squeeze(0),
                                         zs[p0:p1, c1 % 2, 0:ZT[n]]).then_inc(z_stored[c1 % 2], 16)

            store_table(0)
            sp.wait_ge(a_stored, 32 * NJ + 32)
            sp.wait_ge(edges_ready, 2)
            sp.sem_inc(a_used, RING)
            for k in range(ROUNDS):
                with sp.Fori(0, NJ // RING) as i:
                    for n in range(RING):
                        sp.wait_ge(a_used, k * NJ + RING * i + n + 1)
                        for p0, p1 in ((0, 112), (112, NP)):
                            sp.dma_start(ring[n][p0:p1], adj[bass.ds(RING * i + n, 1), p0:p1].squeeze(0)
                                         ).then_inc(a_loaded[n], 16)
            sp.wait_ge(a_used, RING + NJ * ROUNDS)
            sp.dma_start(wbuf[0:D].rearrange("i k o -> i (k o)")[:, 0:KS ** 3 * D]
                         .rearrange("i (k o) -> i k o", o=D),
                         sconv_w.rearrange("k i o -> i k o")).then_inc(loaded_z, 16)
            sp.wait_ge(gsum_done, 1)
            for b in range(2):
                sp.wait_ge(scattered_byd[b], 16 * B * TURNS)
            sp.dma_start(basis[:].rearrange("p g c -> p (g c)")[:, 0:G * PD],
                         rows_by_dst[0:P * G, :].rearrange("(p g) c -> p (g c)", p=P)).then_inc(payd_loaded, 16)
            sp.wait_ge(table_built, 1)
            sp.dma_start(node_rows(tab_t), t4[:]).then_inc(t_stored, 16)
            for k in range(PASSES):
                sp.wait_ge(table_built, k + 2)
                sp.dma_start(node_rows(tab_feat), cur[:]).then_inc(table_stored, 16)
            store_table(1)
            sp.wait_ge(out_ready, 1)
            sp.dma_start(node_rows(out), xs[:]).then_inc(out_stored, 16)
            sp.wait_ge(out_stored, 16)

        @block.gpsimd
        def _(pool):
            for d in (src_i, dst_i):
                nc.gpsimd.memset(d[:, TAIL:T], -1)
            nc.gpsimd.memset(weight[:, TAIL:T], 0.0)
            nc.gpsimd.memset(attr0[:, TAIL:T, :], 0.0)
            nc.gpsimd.memset(pay[:], 0.0)
            nc.gpsimd.memset(payd, 0.0)
            pool.drain().then_inc(prep_mem, 1)
            pool.wait_ge(prep_mem, 1)
            nc.gpsimd.memset(pay[:, :, 0:1], -1.0)
            nc.gpsimd.memset(payd[:, :, 0:1], -1.0)
            pool.drain().then_inc(prep_mem, 1)
            nc.gpsimd.memset(zeros_l[:], 0.0)
            nc.gpsimd.memset(zeros_f[:], 0.0)
            nc.gpsimd.memset(ident[:], 0.0)
            nc.gpsimd.memset(ones_f[:], 1.0)
            nc.gpsimd.iota(iota16[:], pattern=[[1, N + 1]], base=-MID, channel_multiplier=0,
                           allow_small_or_imprecise_dtypes=True)
            nc.gpsimd.iota(iota_c[:], pattern=[[1, G]], base=0, channel_multiplier=0,
                           allow_small_or_imprecise_dtypes=True)
            nc.gpsimd.iota(iota_q[:], pattern=[[1, NP]], base=0, channel_multiplier=0,
                           allow_small_or_imprecise_dtypes=True)
            pool.drain().then_inc(prep_mem, 1)
            pool.wait_ge(prep_mem, 3)
            nc.gpsimd.affine_select(out=upper[:], in_=ones_f[:], compare_op=ALU.is_gt, fill=0.0,
                                    base=0, pattern=[[1, P]], channel_multiplier=-1)
            nc.gpsimd.affine_select(out=ident[:], in_=ident[:], compare_op=ALU.not_equal, fill=1.0,
                                    base=0, pattern=[[-1, P]], channel_multiplier=1).then_inc(prep_mem, 1)

            pool.wait_ge(holes_stored, 32)
            with pool.Fori(0, TURNS) as i:
                for b in range(2):
                    gate(pool, "pool", pslot_ready, 2 * i + b + 1)
                    for u in range(B):
                        nc.gpsimd.indirect_dma_start(
                            out=rows_dram, out_offset=bass.IndirectOffsetOnAxis(ap=slots[:, b, 0, u:u + 1], axis=0),
                            in_=pslot[:, b, u, :], in_offset=None).then_inc(scattered[b], 16)

            for b in range(2):
                pool.wait_ge(scattered[b], 16 * B * TURNS)
            pool.wait_ge(byd_ready, 1)

            def scatter_by_dst(i, first):
                for b in range(2):
                    if not first:
                        gate(pool, "pool", scattered_byd[b], 16 * B * i)
                    at = bass.ds(U * i + b * B, B)
                    for c, column in enumerate((dst_q, src_i, weight)):
                        nc.gpsimd.tensor_copy(pslot[:, b, :, c], column[:, at])
                    nc.gpsimd.tensor_copy(slots[:, b, 0, :], pos_by_dst[:, at]).then_inc(byd_copied, 1)
                    gate(pool, "pool", byd_copied, 2 * i + b + 1)
                    for u in range(B):
                        nc.gpsimd.indirect_dma_start(
                            out=rows_by_dst, out_offset=bass.IndirectOffsetOnAxis(ap=slots[:, b, 0, u:u + 1], axis=0),
                            in_=pslot[:, b, u, 0:PD], in_offset=None).then_inc(scattered_byd[b], 16)

            scatter_by_dst(0, True)
            with pool.Fori(1, TURNS) as i:
                scatter_by_dst(i, False)

            def gathers(stage):
                if stage[0] == "offsets":
                    tables, outs = [tab_t], lambda b, u, g: rawt[:, b * B + u, :]
                    pool.wait_ge(t_stored, 16)
                elif stage[0] == "grouped":
                    n = stage[1]
                    w = ROW_CORNERS[n] * (H, D)[n]
                    tables = [tab_z[n]] * (8 // ROW_CORNERS[n])
                    outs = lambda b, u, g: raw[:, b * B + u, g * w:(g + 1) * w]
                    for h in range(2):
                        pool.wait_ge(z_stored[h], 32 + 32 * 2 * NJ * (n + 1))
                else:
                    pool.wait_ge(table_stored, 16 * (stage[1] + 1))
                    tables, outs = [tab_feat], lambda b, u, g: rawf[:, b * B + u, :]
                with pool.Fori(0, turns_of[stage]) as i:
                    for b in range(2):
                        gate(pool, "pool", rows_ready, order[stage] + 2 * i + b + 1)
                        for u in range(B):
                            for g, table in enumerate(tables):
                                nc.gpsimd.indirect_dma_start(
                                    out=outs(b, u, g), out_offset=None, in_=table,
                                    in_offset=bass.IndirectOffsetOnAxis(ap=slots[:, b, g, u:u + 1], axis=0),
                                ).then_inc(gathered[b], 16)

            for stage in GATHERS:
                gathers(stage)

        @block.tensor
        def _(pe):
            pe.sem_inc(qval_free, 2)
            pe.sem_inc(z_mm, 1)
            pe.wait_ge(prep_mem, 4)

            def count_groups(n):
                pe.wait_ge(rank_in, n)
                pe.matmul(PS[:, 6 * BANK:6 * BANK + NJ], ones_f[:, :], st128[:, 0, :], start=True, stop=True)
                pe.matmul(PS[:, 6 * BANK + 64:6 * BANK + 64 + NJ], upper[:, :], st128[:, 0, :], start=True,
                          stop=True).then_inc(rank_mm, 1)

            count_groups(1)

            S0 = 7 * BANK
            psq = PS[0:NP, S0:S0 + NJ * 3]
            pe.matmul(psq, zeros_f[:, 0:NP], zeros_f[:, 0:NJ * 3], start=True, stop=False)
            with pe.Fori(0, TURNS) as i:
                for b in range(2):
                    pe.wait_ge(qval_ready, 2 * i + b + 1)
                    for u in range(B):
                        mm = pe.matmul(psq, oneq[:, b, u, :], qval[:, b, u].rearrange("p r v -> p (r v)"),
                                       start=False, stop=False, skip_group_check=True)
                    mm.then_inc(qval_free, 1)
            pe.matmul(psq, zeros_f[:, 0:NP], zeros_f[:, 0:NJ * 3], start=False,
                      stop=True).then_inc(scal_ready, 1)
            count_groups(2)

            n_tr = [0]
            n_mm = [0]

            def transposes(view, width):
                n_tr[0] += 1
                pe.wait_ge(tr_ready, n_tr[0])
                for j in range(NJ):
                    c = BANK * (j // 4) + NP * (j % 4)
                    mm = pe.transpose(PS[0:width, c:c + NP], view[:, j, :], ident[0:NP, 0:NP])
                mm.then_inc(tr_done, 1)

            def products(lhs, rhs, cout, per_bank):
                n_mm[0] += 1
                pe.wait_ge(mm_ready, n_mm[0])
                for j in range(NJ):
                    c = BANK * (j // per_bank) + cout * (j % per_bank)
                    mm = pe.matmul(PS[0:NP, c:c + cout], lhs[:, NP * j:NP * j + NP], rhs,
                                   start=True, stop=True)
                mm.then_inc(mm_done, 1)

            def edge_pass(k):
                pe.wait_ge(agg_copied, 4 + ROUNDS + k)
                zero_banks(0, 2, True, False)
                m0 = 2 * GTURNS * (k + 1)
                with pe.Fori(0, GTURNS) as i:
                    group = group_of(i, block_by_dst)
                    for b in range(2):
                        pe.wait_ge(gmsg_ready, m0 + 2 * i + b + 1)
                        for u in range(B):
                            mm = pe.matmul(PS[0:NP, bass.ds(group[b * B + u] * D, D)], grq[:, b, u, :],
                                           gmsg[:, b, u, 0:D], start=False, stop=False, skip_group_check=True)
                        mm.then_inc(gmsg_done, 1)
                zero_banks(0, 2, False, True).then_inc(sum_done, 1)

            def adjacency():
                pe.sem_inc(ahot_used, NOH)
                pe.wait_ge(blocks_ready, 1)
                pe.wait_ge(agg_copied, 1)
                with pe.Fori(0, NJ) as j:
                    g0, g1 = nc.values_load_multi_w_load_instructions(
                        first_of[0:1, bass.ds(j, 2)], engines=(mybir.EngineType.PE,), min_val=0, max_val=G)[1]
                    for h, chunks in enumerate((CHUNKS[:4], CHUNKS[4:])):
                        pe.wait_ge(a_copied, 2 * j + h + 1)
                        for c, w in chunks:
                            pe.matmul(PS[0:NP, c:c + w], zeros_l[:, 0:NP], iota16[:, c:c + w], start=True, stop=True)
                    with pe.Fori(g0, g1) as g:
                        pe.wait_ge(ahot_ready, g + 1)
                        for c, w in CHUNKS:
                            mm = pe.matmul(PS[0:NP, c:c + w], asrc[:, bass.ds((g % NOH) * P, NP)],
                                           ahot[:, bass.ds((g % NOH) * 2 * OHW + c, w)],
                                           start=False, stop=True, skip_group_check=True)
                        mm.then_inc(ahot_used, 1)
                    pe.matmul(PS[0:1, 7 * BANK:7 * BANK + 1], zeros_l[:, 0:1], iota16[:, 0:1], start=True,
                              stop=True).then_inc(a_sum, 1)

            def dense_round(k):
                pe.wait_ge(agg_copied, 4 + k)
                with pe.Fori(0, NJ // RING) as i:
                    pe.wait_ge(lcur_ready, k * (NJ // RING) + i + 1)
                    for n in range(RING):
                        pe.wait_ge(a_loaded[n], 32 * (k * (NJ // RING) + i) + 32)
                        for m, c, w in DPARTS:
                            o = PS[D * (m % 4):D * (m % 4) + D, (m // 4) * BANK:(m // 4) * BANK + w]
                            mm = pe.matmul(o, lcur[:, n, :], ring[n][:, c:c + w], start=False, stop=True,
                                           skip_group_check=True)
                        mm.then_inc(a_used, 1)
                        if n < SIDE:
                            grouped_batch(SIDE * i + k * SLOTS, n)
                pe.matmul(PS[0:1, 3 * BANK:3 * BANK + 1], zeros_l[:, 0:1], iota16[:, 0:1], start=True,
                          stop=True).then_inc(dense_done, 1)
                pe.wait_ge(sum_copied, 2 * (k + 1))
                for j in range(NJ):
                    c = BANK * (j // 12) + 40 * (j % 12)
                    mm = pe.transpose(PS[0:NP, c:c + D], acc[0:D, j:N:NJ], ident[0:D, 0:D])
                mm.then_inc(fold_done, 1)

            def group_of(turn, blocks=block_of):
                return nc.values_load_multi_w_load_instructions(
                    blocks[0:1, bass.ds(U * turn, U)], engines=(mybir.EngineType.PE,), min_val=0,
                    max_val=NJ - 1)[1]

            def zero_banks(b0, b1, first, last):
                for c in range(b0 * BANK, b1 * BANK, BANK):
                    mm = pe.matmul(PS[0:NP, c:c + BANK], zeros_l[:, 0:NP], iota16[:, 0:BANK], start=first, stop=last)
                return mm

            def hat_sums():
                pe.wait_ge(blocks_ready, 1)
                pe.wait_ge(agg_copied, 2)
                zero_banks(0, 7, True, False)
                with pe.Fori(0, GTURNS) as i:
                    group = group_of(i)
                    for b in range(2):
                        pe.wait_ge(hat_ready, 2 * i + b + 1)
                        for u in range(B):
                            mm = pe.matmul(PS[0:NP, bass.ds(group[b * B + u] * P, KP1)], hatq[:, b, u, :],
                                           hat123[:, b, u, :], start=False, stop=False, skip_group_check=True)
                        mm.then_inc(hat_done, 1)
                zero_banks(0, 7, False, True).then_inc(hat_sum, 1)

            def grouped_batch(i, q):
                group = nc.values_load_multi_w_load_instructions(
                    block_of[0:1, bass.ds(B * i + B * q, B)], engines=(mybir.EngineType.PE,), min_val=0,
                    max_val=NJ - 1)[1]
                pe.wait_ge(gmsg_ready, i + q + 1)
                for u in range(B):
                    mm = pe.matmul(PS[0:NP, bass.ds(group[u] * H + GSUM0 * BANK, H)], grq[:, q % 2, u, :],
                                   gmsg[:, q % 2, u, :], start=False, stop=False, skip_group_check=True)
                mm.then_inc(gmsg_done, 1)

            def grouped_rest():
                for q in range(ROUNDS * SLOTS, 2 * GTURNS):
                    grouped_batch(0, q)
                zero_banks(GSUM0, 8, False, True).then_inc(gsum_done, 1)

            def grouped_last():
                pe.wait_ge(agg_copied, 4 + ROUNDS + PASSES)
                zero_banks(0, 2, True, False)
                with pe.Fori(0, GTURNS) as i:
                    group = group_of(i)
                    for b in range(2):
                        pe.wait_ge(gmsg_ready, 2 * (GTURNS * (PASSES + 1) + i) + b + 1)
                        for u in range(B):
                            mm = pe.matmul(PS[0:NP, bass.ds(group[b * B + u] * D, D)], grq[:, b, u, :],
                                           gmsg[:, b, u, 0:D], start=False, stop=False, skip_group_check=True)
                        mm.then_inc(gmsg_done, 1)
                zero_banks(0, 2, False, True).then_inc(gsum_done, 1)

            def turn_sources(i, q):
                pe.wait_ge(hot_ready, i + q + 1)
                for u in range(B):
                    c = (2 + 4 * (q % 2)) * BANK + u * P
                    mm = pe.transpose(PS[0:NP, c:c + P], grq[:, q % 2, u, :], ident[:, :])
                mm.then_inc(hot_turned, 1)

            def source_offsets(i, q):
                group = nc.values_load_multi_w_load_instructions(
                    block_of[0:1, bass.ds(B * i + B * q, B)], engines=(mybir.EngineType.PE,), min_val=0,
                    max_val=NJ - 1)[1]
                pe.wait_ge(hot_copied, i + q + 1)
                for u in range(B):
                    c = (3 + 4 * (q % 2)) * BANK + 4 * u
                    mm = pe.matmul(PS[:, c:c + 4], hotT[:, q % 2, u * P:(u + 1) * P],
                                   t4f[:, bass.ds(group[u] * 4, 4)], start=True, stop=True)
                mm.then_inc(tsrc_ready, 1)

            def build(n):
                width = (H, D)[n]
                pe.wait_ge(loaded_z, 16 * (n + 1))
                wz = wbuf if n == 0 else \
                    wbuf[0:D].rearrange("i k o -> i (k o)")[:, 0:KS ** 3 * D].rearrange("i (k o) -> i k o", o=D)
                per = BANK // width
                with pe.Fori(0, NJ) as j:
                    pe.wait_ge(z_in, NJ * n + j + 1)
                    for plane in range(KS):
                        if plane >= 1:
                            pe.wait_ge(z_dve, CELLS * (NJ * n + j) + max(plane - 1, 0) + 1)
                        if plane != 1:
                            pe.wait_ge(z_act, CELLS * (NJ * n + j) + max(plane - 2, 0) + 1)
                        for k0 in range(0, KS * KS, per):
                            k1 = min(k0 + per, KS * KS)
                            c = (plane % 2) * ZBANKS * BANK + k0 * width
                            mm = pe.matmul(PS[0:NP, c:c + (k1 - k0) * width], hcur[0:width, :],
                                           wz[0:width, plane * KS * KS + k0:plane * KS * KS + k1, :],
                                           start=True, stop=True)
                        mm.then_inc(z_mm, 1)
                        if n == 1 and plane >= 1:
                            source_offsets(SIDE * j, plane - 1)
                        if n == 1 and plane < SIDE:
                            turn_sources(SIDE * j, plane)
                if n == 1:
                    for q in range(SIDE * NJ, 2 * GTURNS):
                        turn_sources(0, q)
                        source_offsets(0, q)

            for stage in STAGES:
                if stage[0] == "adj":
                    adjacency()
                elif stage[0] == "dense":
                    dense_round(stage[1])
                elif stage[0] == "pass":
                    k = stage[1]
                    edge_pass(k)
                    transposes(agg[:], D)
                    products(hT[0:D], gate_w[:, k].rearrange("i g o -> i (g o)"), 3 * D, 5)
                elif stage[0] == "hats":
                    hat_sums()
                    transposes(hsum[:, :, 0:KS ** 3], KS ** 3)
                    products(hT[0:KS ** 3], w1[:, :], H, 8)
                    transposes(h64, H)
                elif stage[0] == "grouped":
                    if stage[1] == 1:
                        grouped_last()
                    else:
                        grouped_rest()
                        transposes(h64, H)
                        products(hT[0:H], w3[:, :], H, 8)
                        transposes(h64, H)
                        products(hT[0:H], w4[:, :], 3, 25)
                elif stage[0] == "build":
                    build(0)
                    pe.wait_ge(agg_copied, 3)
                    zero_banks(GSUM0, 8, True, False)
                elif stage[0] == "offsets":
                    transposes(hs, D)
                    build(1)

        @block.scalar
        def _(act):
            n_ax = [0]

            def unary(pairs):
                n_ax[0] += 1
                act.wait_ge(ax_ready, n_ax[0])
                for out_, in_, f in pairs:
                    ins = nc.scalar.activation(out_, in_, f)
                ins.then_inc(ax_done, 1)

            def root(n):
                act.wait_ge(var_ready, n)
                nc.scalar.activation(st[:, 1, :], st[:, 0, :], ACT.Sqrt).then_inc(std_ready, 1)

            def set_rows(stage):
                rows = [payd[:, :, 1] if stage[0] == "pass" else row2[:, 0, :]]
                with act.Fori(0, turns_of[stage]) as i:
                    for b in range(2):
                        gate(act, "act", raw_free, raw0[stage] + 2 * i + b + 1)
                        for g, r in enumerate(rows):
                            cp = nc.scalar.copy(slots[:, b, g, :], r[:, bass.ds(U * i + b * B, B)])
                        cp.then_inc(rows_ready, 1)

            def grouped_rows(i, q):
                gate(act, "act", raw_free, raw0[("grouped", 0)] + i + q + 1)
                at = bass.ds(B * i + B * q, B)
                nc.scalar.copy(slots[:, q % 2, 0, :], row2[:, 0, at])
                nc.scalar.copy(slots[:, q % 2, 1, :], row2[:, 1, at]).then_inc(rows_ready, 1)

            def offset_rows(i, q):
                gate(act, "act", raw_free, raw0[("offsets", 1)] + i + q + 1)
                nc.scalar.copy(slots[:, q % 2, 0, :],
                               row2[:, 0, bass.ds(B * i + B * q, B)]).then_inc(rows_ready, 1)

            def hot_back(i, q):
                act.wait_ge(hot_turned, i + q + 1)
                c = (2 + 4 * (q % 2)) * BANK
                nc.scalar.copy(hotT[:, q % 2], PS[0:NP, c:c + BANK]).then_inc(hot_copied, 1)

            def build(n):
                if n == 1:
                    offset_rows(0, 0)
                with act.Fori(0, NJ) as j:
                    for plane in range(1, KS):
                        if n == 1:
                            hot_back(SIDE * j, plane - 1)
                            offset_rows(SIDE * j, plane)
                        act.wait_ge(z_mm, KS * (NJ * n + j) + plane + 2)
                        act.wait_ge(z_dve, CELLS * (NJ * n + j) + plane + 1)
                        for to, points in corners(n, plane, plane - 1, 1):
                            cp = nc.scalar.copy(to, points)
                        cp.then_inc(z_act, 1)
                if n == 1:
                    for q in range(SIDE * NJ, 2 * GTURNS):
                        hot_back(0, q)
                        if q + 1 < 2 * GTURNS:
                            offset_rows(0, q + 1)

            act.sem_inc(z_act, 1)
            act.wait_ge(pay_ready, 1)

            def hand_edges(i, first):
                for b in range(2):
                    if not first:
                        gate(act, "act", scattered[b], 16 * B * i)
                    at = bass.ds(U * i + b * B, B)
                    nc.scalar.copy(pslot[:, b], pay0[:, at, :])
                    nc.scalar.copy(slots[:, b, 0, :], pos_i[:, at]).then_inc(pslot_ready, 1)

            hand_edges(0, True)
            with act.Fori(1, TURNS) as i:
                hand_edges(i, False)
            for b in range(2):
                act.wait_ge(scattered[b], 16 * B * TURNS)
            act.wait_ge(edges_ready, 1)
            root(1)
            unary([(st[:, 7:9, :], st[:, 5:7, :], ACT.Sqrt)])
            for stage in STAGES:
                if stage[0] == "adj":
                    with act.Fori(0, NJ) as j:
                        act.wait_ge(a_sum, j + 1)
                        act.wait_ge(a_stored, 32 * j + 32)
                        nc.scalar.copy(accA[:, 0:4 * BANK], PS[0:NP, 0:4 * BANK]).then_inc(a_copied, 1)
                        nc.scalar.copy(accA[:, 4 * BANK:N], PS[0:NP, 4 * BANK:N]).then_inc(a_copied, 1)
                elif stage[0] == "dense":
                    k = stage[1]
                    if k == 0:
                        act.wait_ge(edges_ready, 2)
                        for b in range(2):
                            act.wait_ge(scattered_byd[b], 16 * B * TURNS)
                        grouped_rows(0, 0)
                        grouped_rows(0, 1)
                    act.wait_ge(dense_in, k + 1)
                    with act.Fori(0, NJ // RING) as i:
                        gate(act, "act", a_used, k * NJ + RING * i + RING)
                        nc.scalar.copy(lcur[:], cur[:, bass.ds(RING * i, RING), :]).then_inc(lcur_ready, 1)
                        for q in range(2, 2 + SIDE):
                            grouped_rows(SIDE * i + k * SLOTS, q)
                    act.wait_ge(dense_done, k + 1)
                    for m, c, w in DPARTS[4:]:
                        cp = nc.scalar.copy(acc[0:D, c:c + w], PS[D * (m % 4):D * (m % 4) + D, BANK:BANK + w])
                    cp.then_inc(sum_copied, 1)
                    if k == 0:
                        root(2)
                elif stage[0] == "pass":
                    k = stage[1]
                    act.wait_ge(payd_loaded, 16)
                    set_rows(stage)
                    unary([(g3[:, :, 0, :], g3[:, :, 0, :], ACT.Sigmoid), (g3[:, :, 1, :], g3[:, :, 1, :], ACT.Tanh)])
                    unary([(g3[:, :, 2, :], g3[:, :, 2, :], ACT.Sigmoid), (tmpA[:, :, 0:D], tmpB[:, :, 0:D], ACT.Tanh)])
                    if k == PASSES - 1:
                        root(4)
                elif stage[0] == "build":
                    build(0)
                elif stage[0] == "offsets":
                    act.wait_ge(edges_ready, 3)
                    build(1)
                elif stage == ("hats", 0):
                    unary([(tmpB, tmpA, ACT.Exp)])
                elif stage == ("grouped", 0):
                    for q in range(ROUNDS * SLOTS + 2, 2 * GTURNS):
                        grouped_rows(0, q)
                    unary([(tmpB, tmpA, ACT.Exp)])
                    unary([(tmpB, tmpA, ACT.Exp)])
                    root(3)
                elif stage == ("grouped", 1):
                    act.wait_ge(edges_ready, 4)
                    set_rows(stage)

        @block.vector
        def _(dve):
            V = nc.vector
            chain = [0]

            def link(ins):
                chain[0] += 1
                ins.then_inc(dve_chain, 1)
                dve.wait_ge(dve_chain, chain[0])

            def signal(s):
                dve.sem_inc(s, 1)

            TT = lambda o, a, b_, op: link(V.tensor_tensor(o, a, b_, op))
            TS = lambda o, a, s1, op0, s2=None, op1=None: link(
                V.tensor_scalar(o, a, s1, s2, op0, op1) if op1 is not None else V.tensor_scalar(o, a, s1, None, op0))
            CP = lambda o, a: link(V.tensor_copy(o, a))

            dve.sem_inc(dve_loop, 1)
            dve.sem_inc(hat_done, 2)
            dve.sem_inc(gmsg_done, 2)
            dve.sem_inc(z_dve, 1)
            dve.sem_inc(raw_free, 2)
            dve.wait_ge(prep_mem, 4)
            dve.wait_ge(loaded, 16 * 14)

            eA = arena[:, 0:T]
            eB = arena[:, T:2 * T]
            eI = arena[:, 2 * T:3 * T].bitcast(I32)
            def quotient(q, rem, ids):
                TS(eB, ids, 1.0 / NJ, ALU.mult, 0.5 / NJ - 0.5, ALU.add)
                CP(eI, eB)
                CP(q, eI)
                link(V.scalar_tensor_tensor(rem, q, -float(NJ), ids, ALU.mult, ALU.add))
                TS(eB, rem, 0.0, ALU.is_lt)
                TT(q, q, eB, ALU.subtract)
                link(V.scalar_tensor_tensor(rem, q, -float(NJ), ids, ALU.mult, ALU.add))
                TS(eB, rem, float(NJ), ALU.is_ge)
                TT(q, q, eB, ALU.add)
                link(V.scalar_tensor_tensor(rem, q, -float(NJ), ids, ALU.mult, ALU.add))

            CP(eA, dst_i[:])
            quotient(dst_q[:], dst_r[:], eA)
            TS(pay0[:, :, 2], eA, 0.0, ALU.max)
            CP(eA, src_i[:])
            src_q, src_r, pad = (arena[:, n * T:(n + 1) * T] for n in (3, 4, 5))
            quotient(src_q, src_r, eA)
            TS(pad, eA, 0.0, ALU.is_lt)
            TS(pay0[:, :, 1], eA, 0.0, ALU.max)
            CP(src_i[:], pay0[:, :, 1])
            CP(pay0[:, :, 0], src_q)
            CP(pay0[:, :, 3:6], attr0)
            link(V.memset(pay0[:, :, 6:9], 0.0))
            signal(edges_ready)

            def group_edges(n, rem, steps, position, blocks):
                TS(eA, pad, 100.0, ALU.mult)
                TT(rem, rem, eA, ALU.add)
                og = hot_g.rearrange("p (r t) -> p r t", r=NJ)
                TT(og, rem.unsqueeze(1).broadcast_to([P, NJ, T]), iota_q[:, 0:NJ].unsqueeze(2).broadcast_to([P, NJ, T]),
                   ALU.is_equal)
                link(V.tensor_tensor_scan(run_g, hot_g, hot_g, 0.0, ALU.add, ALU.max))
                rg = run_g.rearrange("p (r t) -> p r t", r=NJ)
                cnt, before, low, tiles, start = (st128[:, n, :] for n in range(5))
                link(V.memset(before[:, 0:1], 0.0))
                CP(before[:, 1:NJ], rg[:, 0:NJ - 1, T - 1])
                TT(cnt, rg[:, :, T - 1], before, ALU.subtract)
                signal(rank_in)
                dve.wait_ge(rank_mm, n + 1)
                CP(tiles, PS[:, 6 * BANK:6 * BANK + NJ])
                CP(low, PS[:, 6 * BANK + 64:6 * BANK + 64 + NJ])
                TS(tiles, tiles, float(P - 1), ALU.add)
                tiles_i = st128[:, 5, :].bitcast(I32)
                CP(tiles_i, tiles)
                TS(tiles_i, tiles_i, 7, ALU.arith_shift_right)
                CP(tiles, tiles_i)
                TS(tiles, tiles, 1.0, ALU.max)
                link(V.tensor_tensor_scan(start, tiles, tiles, 0.0, ALU.add, ALU.max))
                TT(start, start, tiles, ALU.subtract)
                TT(low, low, before, ALU.subtract)
                TS(low, low, -1.0, ALU.add)
                link(V.scalar_tensor_tensor(low, start, float(P), low, ALU.mult, ALU.add))
                posf = eA
                link(V.memset(posf, 0.0))
                with dve.Fori(0, NJ) as r:
                    rt = bass.ds(r * T, T)
                    dve.wait_ge(dve_loop, 2 * r + steps + 1)
                    V.scalar_tensor_tensor(eB, run_g[:, rt], low[:, bass.ds(r, 1)], hot_g[:, rt], ALU.add,
                                           ALU.mult).then_inc(dve_loop, 1)
                    dve.wait_ge(dve_loop, 2 * r + steps + 2)
                    V.tensor_tensor(posf, posf, eB, ALU.add).then_inc(dve_loop, 1)
                dve.wait_ge(dve_loop, 2 * NJ + steps + 1)
                pi, lane = eB.bitcast(I32), arena[:, 3 * T:4 * T].bitcast(I32)
                CP(pi, posf)
                TS(lane, pi, P - 1, ALU.bitwise_and)
                TS(pi, pi, 7, ALU.arith_shift_right)
                CP(posf, pi)
                lanef = arena[:, 4 * T:5 * T]
                CP(lanef, lane)
                link(V.scalar_tensor_tensor(posf, lanef, float(G), posf, ALU.mult, ALU.add))
                TS(eB, iota_c[:, 0:T], float(P * G), ALU.add)
                TT(eB, eB, posf, ALU.subtract)
                TT(eB, eB, pad, ALU.mult)
                TT(posf, posf, eB, ALU.add)
                CP(position, posf)
                signal((pay_ready, byd_ready)[n])
                bo = wb[0:1, 0:NJ * G // 2].bitcast(BF16).rearrange("p (g r) -> p g r", r=NJ)
                TT(bo, iota_c[0:1, :].unsqueeze(2).broadcast_to([1, G, NJ]),
                   start[0:1, :].unsqueeze(1).broadcast_to([1, G, NJ]),
                   ALU.is_ge)
                link(V.tensor_reduce(arena[0:1, 0:G], bo, AX.X, ALU.add))
                TS(arena[0:1, 0:G], arena[0:1, 0:G], -1.0, ALU.add)
                CP(blocks, arena[0:1, 0:G])
                if n == 0:
                    CP(first_of[:, 0:NJ], start[0:1, :])
                    TT(start[0:1, NJ - 1:NJ], start[0:1, NJ - 1:NJ], tiles[0:1, NJ - 1:NJ], ALU.add)
                    CP(first_of[:, NJ:NJ + 1], start[0:1, NJ - 1:NJ])
                signal(blocks_ready)

            group_edges(0, src_r, 0, pos_i[:], block_of[:])

            link(V.memset(val[:, :, 0:1], 1.0))
            CP(val[:, :, 1], weight[:])
            TS(val[:, :, 2:3], val[:, :, 1:2], alphas[:, 2:3], ALU.mult, 0.0, ALU.max)

            qb = iota_q[:].unsqueeze(1).broadcast_to([P, B, NP])
            rb = iota_q[:, 0:NJ].unsqueeze(1).broadcast_to([P, B, NJ])
            with dve.Fori(0, TURNS) as i:
                for b in range(2):
                    at = bass.ds(U * i + b * B, B)
                    dve.wait_ge(qval_free, 2 * i + b + 1)
                    V.tensor_tensor(oneq[:, b], dst_q[:, at].unsqueeze(2).broadcast_to([P, B, NP]), qb, ALU.is_equal)
                    V.tensor_tensor(oner[:, b], dst_r[:, at].unsqueeze(2).broadcast_to([P, B, NJ]), rb,
                                    ALU.is_equal).then_inc(dve_loop, 1)
                    dve.wait_ge(dve_loop, 2 * NJ + 1 + 2 * i + b + 1)
                    V.tensor_tensor(qval[:, b], oner[:, b].unsqueeze(3).broadcast_to([P, B, NJ, 3]),
                                    val[:, at, :].unsqueeze(2).broadcast_to([P, B, NJ, 3]),
                                    ALU.mult).then_inc(qval_ready, 1)
            loop0 = [2 * NJ + 1 + 2 * TURNS]

            def layernorm(n):
                m, v = st[:, 2, :], st[:, 0, :]
                tA, tB = (h64[:].rearrange("p j f -> p (j f)")[:, h * NJ * D:(h + 1) * NJ * D]
                          .rearrange("p (j d) -> p j d", j=NJ) for h in range(2))
                link(V.tensor_reduce(m, xs[:], AX.X, ALU.add))
                TS(m, m, -1.0 / D, ALU.mult)
                TT(tA, xs[:], m.unsqueeze(2).broadcast_to([NP, NJ, D]), ALU.add)
                TT(tB, tA, tA, ALU.mult)
                link(V.tensor_reduce(v, tB, AX.X, ALU.add))
                TS(v, v, 1.0 / D, ALU.mult, EPS, ALU.add)
                signal(var_ready)
                dve.wait_ge(std_ready, n)
                link(V.reciprocal(m, st[:, 1, :]))
                TS(tA, tA, 0.0, ALU.max)
                TT(hs[:], tA, m.unsqueeze(2).broadcast_to([NP, NJ, D]), ALU.mult)

            def bcn(col, width=D):
                return col.unsqueeze(2).broadcast_to([NP, NJ, width])

            def adjacency():
                dve.sem_inc(a_copied, 2)
                signal(agg_copied)
                with dve.Fori(0, NJ) as j:
                    g0, g1 = nc.values_load_multi_w_load_instructions(
                        first_of[0:1, bass.ds(j, 2)], engines=(mybir.EngineType.DVE,), min_val=0, max_val=G)[1]
                    with dve.Fori(g0, g1) as g:
                        dve.wait_ge(ahot_used, g + 1)
                        V.tensor_scalar(asrc[:, bass.ds((g % NOH) * P, NP)], iota_q[:], pay[:, bass.ds(g, 1), 0], None,
                                        ALU.is_equal)
                        V.tensor_scalar(ahot[:, bass.ds((g % NOH) * 2 * OHW, N + 1)], iota16[:], dstg[:, bass.ds(g, 1)],
                                        None, ALU.is_equal).then_inc(ahot_ready, 1)
                dve.wait_ge(a_stored, 32 * NJ + 32)

            def dense_round(k):
                link(V.memset(PS[:, 0:2 * BANK], 0.0))
                signal(agg_copied)
                signal(dense_in)
                with dve.Fori(0, NJ // RING) as i:
                    for q in range(SIDE):
                        grouped_batch(SIDE * i + k * SLOTS, q)
                dve.wait_ge(dense_done, k + 1)
                for m, c, w in DPARTS[:4]:
                    cp = V.tensor_copy(acc[0:D, c:c + w], PS[D * m:D * m + D, 0:w])
                cp.then_inc(sum_copied, 1)
                dve.wait_ge(fold_done, k + 1)
                CP(agg[:, 0:24, 0:D].rearrange("p (a j) d -> p a j d", a=2),
                   PS[0:NP, 0:2 * BANK].rearrange("p (a c) -> p a c", a=2)[:, :, 0:480]
                   .rearrange("p a (j d) -> p a j d", d=40)[:, :, :, 0:D])
                CP(agg[:, 24, 0:D], PS[0:NP, 2 * BANK:2 * BANK + D])

            DI, DW, DW2, RC, BI = 9, 10, 4, 11, 3

            def edge_pass(k):
                s = ("pass", k)
                signal(agg_copied)
                m0 = 2 * GTURNS * (k + 1)
                with dve.Fori(0, GTURNS) as i:
                    for b in range(2):
                        at = bass.ds(U * i + b * B, B)
                        us = slice(b * B, b * B + B)
                        dve.wait_ge(gmsg_done, m0 + 2 * i + b + 1)
                        V.tensor_tensor(grq[:, b], payd[:, at, 0:1].broadcast_to([P, B, NP]),
                                        iota_q[:].unsqueeze(1).broadcast_to([P, B, NP]), ALU.is_equal)
                        dve.wait_ge(gathered[b], landed0[s] + per_batch[s] * i + per_batch[s])
                        V.tensor_tensor(gmsg[:, b, :, 0:D], rawf[:, us], payd[:, at, 2:3].broadcast_to([P, B, D]),
                                        ALU.mult).then_inc(raw_free, 1)
                        dve.wait_ge(raw_free, 2 + raw0[s] + 2 * i + b + 1)
                        dve.sem_inc(gmsg_ready, 1)
                dve.wait_ge(sum_done, k + 1)
                CP(agg[:], PS[0:NP, 0:NJ * D].rearrange("p (j d) -> p j d", d=D))

            n_tr, n_mm, n_ax = [0], [0], [0]

            def transposed(width):
                signal(tr_ready)
                n_tr[0] += 1
                dve.wait_ge(tr_done, n_tr[0])
                CP(hT[0:width, 0:24 * NP].rearrange("c (a n) -> c a n", a=6),
                   PS[0:width, 0:6 * BANK].rearrange("c (a n) -> c a n", a=6)[:, :, 0:4 * NP])
                CP(hT[0:width, 24 * NP:25 * NP], PS[0:width, 6 * BANK:6 * BANK + NP])

            def product(to, cout, per_bank, bias):
                signal(mm_ready)
                n_mm[0] += 1
                dve.wait_ge(mm_done, n_mm[0])
                for a in range(0, NJ, per_bank):
                    n = min(per_bank, NJ - a)
                    c = BANK * (a // per_bank)
                    got = PS[0:NP, c:c + n * cout].rearrange("p (j d) -> p j d", d=cout)
                    if bias is None:
                        CP(to[:, a:a + n, :], got)
                    else:
                        TT(to[:, a:a + n, :], got, bias.unsqueeze(1).broadcast_to([NP, n, cout]), ALU.add)

            def bias_of(b_):
                return b_[:].unsqueeze(1).broadcast_to([NP, NJ, H])

            def asked():
                signal(ax_ready)
                n_ax[0] += 1
                dve.wait_ge(ax_done, n_ax[0])

            def elu(v):
                TS(tmpA, v, 0.0, ALU.min)
                asked()
                TS(v, v, 0.0, ALU.max, -1.0, ALU.add)
                TT(v, v, tmpB, ALU.add)

            def knots(ps):
                pos = arena[:, 0:3 * G].rearrange("p (t c) -> p t c", c=3)
                i0 = arena[:, 3 * G:6 * G].rearrange("p (t c) -> p t c", c=3)
                one = arena[:, 6 * G:9 * G].rearrange("p (t c) -> p t c", c=3)
                TS(pos, ps, float(KS - 1), ALU.mult)
                TS(i0, pos, 1.0, ALU.is_ge)
                for step in range(2, CELLS):
                    link(V.scalar_tensor_tensor(i0, pos, float(step), i0, ALU.is_ge, ALU.add))
                TT(pos, pos, i0, ALU.subtract)
                TS(one, pos, -1.0, ALU.mult, 1.0, ALU.add)
                return pos, i0, one

            def spline_basis(ps, n):
                pos, i0, one = knots(ps)
                q12 = arena[:, 9 * G:13 * G].rearrange("p (t q) -> p t q", q=4)
                rowf = arena[:, 13 * G:14 * G]
                side = (one, pos)
                for q in range(4):
                    TT(q12[:, :, q], side[q // 2][:, :, 0], side[q % 2][:, :, 1], ALU.mult)
                for g in range(2):
                    TT(basis[:, :, 4 * g:4 * g + 4], q12, side[g][:, :, 2:3].broadcast_to([P, G, 4]), ALU.mult)
                link(V.scalar_tensor_tensor(rowf, i0[:, :, 0], float(CELLS), i0[:, :, 1], ALU.mult, ALU.add))
                link(V.scalar_tensor_tensor(rowf, rowf, float(K3[n]), i0[:, :, 2], ALU.mult, ALU.add))
                link(V.scalar_tensor_tensor(rowf, pay[:, :, 2], float(CELLS * CELLS * K3[n]), rowf, ALU.mult, ALU.add))
                CP(row2[:, 0, :], rowf)
                if n == 0:
                    TS(rowf, rowf, 1.0, ALU.add)
                    CP(row2[:, 1, :], rowf)

            def hat_messages():
                pos, i0, one = knots(pay[:, :, 3:6])
                kk = iota_q[:, 0:KS].unsqueeze(1).broadcast_to([P, G, KS])
                tk = hT[:, 0:G * KS].rearrange("p (g k) -> p g k", k=KS)
                for c in range(3):
                    h = hats[:, c]
                    TT(tk, kk, i0[:, :, c:c + 1].broadcast_to([P, G, KS]), ALU.is_equal)
                    TT(h, tk, one[:, :, c:c + 1].broadcast_to([P, G, KS]), ALU.mult)
                    TS(i0[:, :, c:c + 1], i0[:, :, c:c + 1], 1.0, ALU.add)
                    TT(tk, kk, i0[:, :, c:c + 1].broadcast_to([P, G, KS]), ALU.is_equal)
                    TT(tk, tk, pos[:, :, c:c + 1].broadcast_to([P, G, KS]), ALU.mult)
                    TT(h, h, tk, ALU.add)
                link(V.memset(hat123[:, :, :, KS ** 3:KP1], 1.0))
                signal(agg_copied)
                base = loop0[0]
                with dve.Fori(0, GTURNS) as i:
                    for b in range(2):
                        at = bass.ds(U * i + b * B, B)
                        dve.wait_ge(hat_done, 2 * i + b + 1)
                        V.tensor_tensor(hatq[:, b], pay[:, at, 0:1].broadcast_to([P, B, NP]),
                                        iota_q[:].unsqueeze(1).broadcast_to([P, B, NP]), ALU.is_equal)
                        V.tensor_tensor(hat12[:, b].rearrange("p u (k l) -> p u k l", k=KS),
                                        hats[:, 0, at, :].unsqueeze(3).broadcast_to([P, B, KS, KS]),
                                        hats[:, 1, at, :].unsqueeze(2).broadcast_to([P, B, KS, KS]),
                                        ALU.mult).then_inc(dve_loop, 1)
                        dve.wait_ge(dve_loop, base + 2 * i + b + 1)
                        V.tensor_tensor(hat123[:, b, :, 0:KS ** 3].rearrange("p u (k l) -> p u k l", l=KS),
                                        hat12[:, b].unsqueeze(3).broadcast_to([P, B, KS * KS, KS]),
                                        hats[:, 2, at, :].unsqueeze(2).broadcast_to([P, B, KS * KS, KS]),
                                        ALU.mult).then_inc(hat_ready, 1)
                loop0[0] = base + 2 * GTURNS
                dve.wait_ge(hat_sum, 1)
                CP(hsum[:, 0:24, :].rearrange("p (a j) d -> p a j d", a=6),
                   PS[0:NP, 0:6 * BANK].rearrange("p (a j d) -> p a j d", a=6, j=4)[:, :, :, 0:KP1])
                CP(hsum[:, 24, :], PS[0:NP, 6 * BANK:6 * BANK + KP1])

            def grouped_step(n, m, at, b, landed):
                width = (H, D)[n]
                us = slice(b * B, b * B + B)
                dve.wait_ge(gmsg_done, m + 2 * GTURNS * n * (PASSES + 1) + 1)
                V.tensor_tensor(grq[:, b], pay[:, at, 0:1].broadcast_to([P, B, NP]),
                                iota_q[:].unsqueeze(1).broadcast_to([P, B, NP]), ALU.is_equal)
                dve.wait_ge(gathered[b], landed)
                rr = raw[:, us, 0:8 * width].rearrange("p u (c f) -> p u c f", f=width)
                V.tensor_tensor(rr, rr, basis[:, at, :].unsqueeze(3).broadcast_to([P, B, 8, width]),
                                ALU.mult).then_inc(dve_loop, 1)
                dve.wait_ge(dve_loop, m + gbase[n] + 1)
                V.tensor_reduce(gmsg[:, b, :, 0:width],
                                raw[:, us, 0:8 * width].rearrange("p u (c f) -> p u f c", f=width), AX.X,
                                ALU.add).then_inc(raw_free, 1)
                dve.wait_ge(raw_free, m + 2 + raw0[("grouped", n)] + 1)
                dve.sem_inc(gmsg_ready, 1)

            def grouped_batch(i, q):
                s = ("grouped", 0)
                grouped_step(0, i + q, bass.ds(B * i + B * q, B), q % 2,
                             per_batch[s] // 2 * i + landed0[s] + per_batch[s] * (q // 2 + 1))

            def grouped_last():
                s = ("grouped", 1)
                signal(agg_copied)
                with dve.Fori(0, GTURNS) as i:
                    for b in range(2):
                        grouped_step(1, 2 * i + b, bass.ds(U * i + b * B, B), b,
                                     landed0[s] + per_batch[s] * i + per_batch[s])
                dve.wait_ge(gsum_done, 2)

            def source_onehots(i, q):
                V.tensor_tensor(grq[:, q % 2], pay[:, bass.ds(B * i + B * q, B), 0:1].broadcast_to([P, B, NP]),
                                iota_q[:].unsqueeze(1).broadcast_to([P, B, NP]), ALU.is_equal).then_inc(hot_ready, 1)

            def offsets(i, q):
                s = ("offsets", 1)
                b = q % 2
                us = slice(b * B, b * B + B)
                dve.wait_ge(tsrc_ready, i + q + 1)
                dve.wait_ge(gathered[b], landed0[s] + per_batch[s] // 2 * i + per_batch[s] * (q // 2 + 1))
                c = (3 + 4 * b) * BANK
                V.tensor_tensor(pay[:, bass.ds(B * i + B * q, B), 6:9], rawt[:, us, 0:3],
                                PS[:, c:c + 4 * B].rearrange("p (u c) -> p u c", c=4)[:, :, 0:3],
                                ALU.subtract).then_inc(raw_free, 1)

            def build(n):
                width = (H, D)[n]
                if n == 1:
                    source_onehots(0, 0)
                with dve.Fori(0, NJ) as j:
                    gate(dve, "dve", z_mm, KS * (NJ * n + j) + 1)
                    V.tensor_copy(hcur[0:width, :], hT[0:width, bass.ds(NP * j, NP)]).then_inc(z_in, 1)
                    for c1 in range(CELLS):
                        dve.wait_ge(z_mm, KS * (NJ * n + j) + c1 + 2)
                        if c1 >= 1:
                            dve.wait_ge(z_act, CELLS * (NJ * n + j) + c1 + 1)
                        dve.wait_ge(z_stored[c1 % 2], 32 * (2 * (NJ * n + j) + c1 // 2) + 32)
                        for to, points in corners(n, c1, c1, 0):
                            cp = V.tensor_copy(to, points)
                        cp.then_inc(z_dve, 1)
                        if n == 1:
                            source_onehots(SIDE * j, c1 + 1)
                            offsets(SIDE * j, c1)
                if n == 1:
                    for q in range(SIDE * NJ, 2 * GTURNS):
                        if q + 1 < 2 * GTURNS:
                            source_onehots(0, q + 1)
                        offsets(0, q)
                for h in range(2):
                    dve.wait_ge(z_stored[h], 32 + 32 * 2 * NJ * (n + 1))

            dve.wait_ge(scal_ready, 1)
            CP(scal[:], PS[0:NP, 7 * BANK:7 * BANK + NJ * 3].rearrange("p (j v) -> p j v", v=3))
            TS(pad, dst_q[:], 0.0, ALU.is_lt)
            group_edges(1, dst_r[:], 2 * NJ + 2 * TURNS, pos_by_dst[:], block_by_dst[:])
            loop0[0] += 2 * NJ
            layernorm(1)
            dve.wait_ge(loaded_w, 16 * (LAYERS * 3 + 11))
            TS(st[:, 5, :], scal[:, :, 0], 1.0, ALU.max)
            TS(scal[:, :, 1], scal[:, :, 1], 1.0, ALU.add)
            TS(st[:, 6, :], scal[:, :, 1], 1e-30, ALU.max)
            asked()
            link(V.reciprocal(st[:, DI:DI + 2, :], st[:, 7:9, :]))
            for c, row in ((0, DI), (1, DW)):
                TS(st[:, 0, :], scal[:, :, c], 0.0, ALU.is_gt)
                TT(st[:, row, :], st[:, row, :], st[:, 0, :], ALU.mult)
            TT(st[:, DW2, :], st[:, DW, :], st[:, DW, :], ALU.mult)
            TS(st[:, BI, :], scal[:, :, 2], alphas[0:NP, 1:2], ALU.mult)
            TS(st[:, 0, :], nvec[:], alphas[0:NP, 3:4], ALU.mult)
            TT(st[:, BI, :], st[:, BI, :], st[:, 0, :], ALU.add)
            for g, (m, own) in enumerate(((0, 0), (4, 2), (6, 3))):
                TT(gate_b[:, :, g, :], cb[:, :, m, :], cb[:, :, m + 1, :], ALU.add)
                TT(gate_b[:, :, g, :], gate_b[:, :, g, :], gbg[:, :, own, :], ALU.add)

            dve.wait_ge(pay_loaded, 16)
            TS(dstg[:], pay[:, :, 2], -float(MID), ALU.add)
            adjacency()

            hat_messages()
            TS(st[:, RC, :], hsum[:, :, KS ** 3], 1.0, ALU.max)
            link(V.reciprocal(st[:, RC, :], st[:, RC, :]))
            transposed(KS ** 3)
            product(h64, H, 8, None)
            TT(h64[:], h64[:], bcn(st[:, RC, :], H), ALU.mult)
            TT(h64[:], h64[:], bias_of(b1), ALU.add)
            elu(h64[:])
            transposed(H)
            build(0)
            spline_basis(pay[:, :, 3:6], 0)
            signal(edges_ready)
            gbase = [loop0[0], None]
            signal(agg_copied)

            TT(cur[:], hs[:], bcn(st[:, DI, :]), ALU.mult)
            dense_round(0)
            TT(cur[:], agg[:], bcn(st[:, DI, :]), ALU.mult)
            TT(xs[:], xs[:], cur[:], ALU.add)

            layernorm(2)
            CP(cur[:], hs[:])
            for r in range(ITERS):
                dense_round(1 + r)
                TS(cur[:], agg[:], alphas[0:NP, 0:1], ALU.mult)
                TT(cur[:], cur[:], bcn(st[:, BI, :]), ALU.add)
                TS(cur[:], cur[:], 0.0, ALU.max)
            TT(xs[:], xs[:], cur[:], ALU.add)

            for q in range(ROUNDS * SLOTS, 2 * GTURNS):
                grouped_batch(0, q)
            loop0[0] = gbase[0] + 2 * GTURNS
            dve.wait_ge(gsum_done, 1)
            TT(h64[:], PS[0:NP, GSUM0 * BANK:GSUM0 * BANK + NJ * H].rearrange("p (j f) -> p j f", f=H),
               bcn(st[:, RC, :], H), ALU.mult)
            TT(h64[:], h64[:], bias_of(b2), ALU.add)
            elu(h64[:])
            transposed(H)
            product(h64, H, 8, b3[:])
            elu(h64[:])
            transposed(H)
            product(t4[:, :, 0:3], 3, 25, b4[:])
            link(V.memset(t4[:, :, 3:4], 0.0))
            signal(table_built)

            dve.wait_ge(payd_loaded, 16)
            layernorm(3)
            CP(cur[:], hs[:])
            for l in range(LAYERS):
                TT(cur[:], cur[:], bcn(st[:, DW, :]), ALU.mult)
                signal(table_built)
                edge_pass(l)
                TT(cur[:], cur[:], agg[:], ALU.add)
                TT(agg[:], cur[:], bcn(st[:, DW, :]), ALU.mult)
                transposed(D)
                product(gates, 3 * D, 5, gate_b[:, l].rearrange("p g d -> p (g d)"))
                asked()
                TT(cur[:], g3[:, :, 0, :], g3[:, :, 1, :], ALU.mult)
                TT(tmpB[:, :, 0:D], cur[:], gwc[:, l, 2:3, :].broadcast_to([NP, NJ, D]), ALU.mult)
                TT(g3[:, :, 2, :], g3[:, :, 2, :], tmpB[:, :, 0:D], ALU.add)
                CP(tmpB[:, :, 0:D], cur[:])
                asked()
                TT(cur[:], g3[:, :, 2, :], tmpA[:, :, 0:D], ALU.mult)
            TT(xs[:], xs[:], cur[:], ALU.add)
            layernorm(4)

            CP(row2[:, 0, :], pay[:, :, 2])
            signal(edges_ready)
            transposed(D)
            build(1)
            dve.wait_ge(raw_free, 2 + raw0[("offsets", 1)] + 2 * GTURNS)
            TT(pay[:, :, 3:6], pay[:, :, 3:6], pay[:, :, 6:9], ALU.add)
            TS(pay[:, :, 3:6], pay[:, :, 3:6], 0.0, ALU.max, 1.0, ALU.min)
            spline_basis(pay[:, :, 3:6], 1)
            signal(edges_ready)
            gbase[1] = loop0[0]
            grouped_last()
            TT(cur[:], PS[0:NP, 0:NJ * D].rearrange("p (j f) -> p j f", f=D), bcn(st[:, RC, :]), ALU.mult)
            TT(cur[:], cur[:], bc[:].unsqueeze(1).broadcast_to([NP, NJ, D]), ALU.add)
            TT(xs[:], xs[:], cur[:], ALU.add)
            signal(out_ready)


_INS = ["x", "src", "dst", "edge_attr_3", "edge_weight", "node_vec", "L1_gnn_alpha1", "L1_gnn_alpha2",
        "L1_gnn_alpha3", "L1_gnn_alpha4", "L2_gnn_conv_w", "L2_gnn_conv_b", "L2_gnn_wc", "L2_gnn_bg",
        "L3_gnn_stn1_w", "L3_gnn_stn1_b", "L3_gnn_stn2_w", "L3_gnn_stn2_b", "L3_gnn_stn3_w",
        "L3_gnn_stn3_b", "L3_gnn_stn4_w", "L3_gnn_stn4_b", "L3_gnn_conv_w", "L3_gnn_conv_b"]


def kernel(**inputs):
    import concourse.bacc as bacc
    from concourse.bass_utils import run_bass_kernel_spmd

    nc = bacc.Bacc("TRN2", target_bir_lowering=False, num_devices=1)
    arrays, args = {}, []
    for name in _INS:
        a = np.ascontiguousarray(inputs[name])
        arrays[f"in_{name}"] = a
        args.append(nc.dram_tensor(f"in_{name}", a.shape, mybir.dt.from_np(a.dtype), kind="ExternalInput").ap())
    out = nc.dram_tensor("out_x", inputs["x"].shape, F32, kind="ExternalOutput").ap()
    gnn_kernel(nc, *args, out)
    r = run_bass_kernel_spmd(nc, [arrays], core_ids=[0])
    return r.results[0]["out_x"]
```
